# Optimizing a Trainium2 kernel written in Bass

```python
import numpy as np
import jax
import jax.numpy as jnp

def _softmax(x, axis=-1):
    return jax.nn.softmax(x, axis=axis)

def _gelu(x):
    return jax.nn.gelu(x, approximate=True)

def _silu(x):
    return jax.nn.silu(x)

def _sigmoid(x):
    return jax.nn.sigmoid(x)

def _layernorm(x, axis=-1, eps=1e-05):
    m = jnp.mean(x, axis=axis, keepdims=True)
    v = jnp.var(x, axis=axis, keepdims=True)
    return (x - m) / jnp.sqrt(v + eps)

def _scatter_add(tgt, idx, src, axis=0):
    return tgt.at[idx].add(src)

def _segment_sum(src, seg, n):
    return jax.ops.segment_sum(src, seg, n)
kernel_name = 'mk_seq_postln_d1_jaxref_r4_1a4246'

def setup_inputs(seed: int=0):
    np.random.seed(seed)
    _w = jnp.asarray

    def _L0_attn_setup():
        import jax, jax.numpy as jnp
        import numpy as np
        CHUNK = 32

        def _l2norm(x):
            return x * jax.lax.rsqrt(jnp.sum(x * x, -1, keepdims=True) + 1e-06)

        def _short_conv(x, w):
            K = w.shape[-1]
            L = x.shape[1]
            xp = jnp.pad(x, ((0, 0), (K - 1, 0), (0, 0)))
            y = sum((xp[:, t:t + L, :] * w[:, t] for t in range(K)))
            return jax.nn.silu(y)

        def _fir_conv(x, w):
            B, L, H, D = x.shape
            K = w.shape[-1]
            xf = x.reshape(B, L, H * D).transpose(0, 2, 1)
            wf = w.reshape(H * D, 1, K)
            y = jax.lax.conv_general_dilated(xf, wf, (1,), [(K - 1, 0)], feature_group_count=H * D, dimension_numbers=('NCH', 'OIH', 'NCH'))
            return y.transpose(0, 2, 1).reshape(B, L, H, D)

        def _delta_rule(q, k, v, beta, chunk=CHUNK):
            B, H, L, Dk = q.shape
            Dv = v.shape[-1]
            pad = -L % chunk
            if pad:
                q, k, v = (jnp.pad(t, ((0, 0), (0, 0), (0, pad), (0, 0))) for t in (q, k, v))
                beta = jnp.pad(beta, ((0, 0), (0, 0), (0, pad)))
            Lp = L + pad
            n = Lp // chunk
            q = _l2norm(q)
            k = _l2norm(k)
            v = v * beta[..., None]
            kb = k * beta[..., None]
            resh = lambda t: t.reshape(B, H, n, chunk, -1)
            q, k, v, kb = map(resh, (q, k, v, kb))
            tri = jnp.triu(jnp.ones((chunk, chunk), bool))
            tri_s = jnp.triu(tri, 1)
            A = jnp.where(tri, 0.0, -jnp.einsum('bhncd,bhnmd->bhncm', kb, k))
            for i in range(1, chunk):
                A = A.at[..., i, :i].add(jnp.einsum('...j,...jk->...k', A[..., i, :], A[..., :, :i]))
            T = A + jnp.eye(chunk, dtype=A.dtype)
            u = T @ v
            w = T @ kb

            def step(S, inp):
                qi, ki, ui, wi = inp
                attn = jnp.where(tri_s, 0.0, qi @ jnp.swapaxes(ki, -1, -2))
                u_i = ui - wi @ S
                o = qi @ S + attn @ u_i
                S = S + jnp.swapaxes(ki, -1, -2) @ u_i
                return (S, o)
            S0 = jnp.zeros((B, H, Dk, Dv), q.dtype)
            blocks = lambda t: jnp.moveaxis(t, 2, 0)
            S, out = jax.lax.scan(step, S0, (blocks(q), blocks(k), blocks(u), blocks(w)))
            out = jnp.moveaxis(out, 0, 2).reshape(B, H, Lp, Dv)[:, :, :L]
            return (out, S)
        key = jax.random.key(seed)
        B, L, D, H = (2, 512, 256, 4)
        Dv = D // H
        ks = jax.random.split(key, 16)
        nrm = lambda k, s, sc: jax.random.normal(k, s, jnp.float32) * sc
        gate_in_dim = D + 2 * H * 4
        hid = 2 * D
        return {'hidden_states': nrm(ks[0], (B, L, D), 1.0), 'Wq': nrm(ks[1], (D, D), D ** (-0.5)), 'Wk': nrm(ks[2], (D, D), D ** (-0.5)), 'Wv': nrm(ks[3], (D, D), D ** (-0.5)), 'Wb': nrm(ks[4], (H, D), D ** (-0.5)), 'qconv_w': nrm(ks[5], (D, 4), 0.5), 'kconv_w': nrm(ks[6], (D, 4), 0.5), 'vconv_w': nrm(ks[7], (D, 4), 0.5), 'fir_short_w': jnp.zeros((H, Dv, 3)).at[..., -1].set(1.0) + nrm(ks[8], (H, Dv, 3), 0.02), 'fir_long_w': jnp.zeros((H, Dv, 63)).at[..., -1].set(1.0) + nrm(ks[9], (H, Dv, 63), 0.02), 'gate_w1': nrm(ks[10], (hid, gate_in_dim), gate_in_dim ** (-0.5)), 'gate_b1': jnp.zeros((hid,), jnp.float32), 'gate_w2': nrm(ks[11], (H * 4, hid), hid ** (-0.5)), 'log_temp': jnp.zeros((H,), jnp.float32), 'base_bias': jnp.zeros((H, 4)).at[:, 3].set(2.0), 'floor_raw': jnp.full((H, 4), float(np.log(0.5)), jnp.float32), 'onorm_w': jnp.ones((Dv,), jnp.float32), 'Wo': nrm(ks[12], (D, D), D ** (-0.5))}
    _L0_attn_in = _L0_attn_setup()

    def _L0_ffn_setup():
        import jax, jax.numpy as jnp
        import numpy as np
        EMBED = 256
        NUM_EXPERTS = 8
        TOP_K = 2
        key = jax.random.key(seed)
        ks = jax.random.split(key, 6)
        scale = EMBED ** (-0.5)
        return {'x': jax.random.normal(ks[0], (4, 1024, EMBED), jnp.float32), 'router_w': jax.random.normal(ks[1], (EMBED, NUM_EXPERTS), jnp.float32) * scale, 'router_b': jnp.zeros((NUM_EXPERTS,), jnp.float32), 'we_gate': jax.random.normal(ks[2], (NUM_EXPERTS, EMBED, EMBED), jnp.float32) * scale, 'we_up': jax.random.normal(ks[3], (NUM_EXPERTS, EMBED, EMBED), jnp.float32) * scale, 'we_down': jax.random.normal(ks[4], (NUM_EXPERTS, EMBED, EMBED), jnp.float32) * scale}
    _L0_ffn_in = _L0_ffn_setup()
    _d = {'L0_attn_hidden_states': _L0_attn_in['hidden_states'], 'L0_attn_Wq': _L0_attn_in['Wq'], 'L0_attn_Wk': _L0_attn_in['Wk'], 'L0_attn_Wv': _L0_attn_in['Wv'], 'L0_attn_Wb': _L0_attn_in['Wb'], 'L0_attn_qconv_w': _L0_attn_in['qconv_w'], 'L0_attn_kconv_w': _L0_attn_in['kconv_w'], 'L0_attn_vconv_w': _L0_attn_in['vconv_w'], 'L0_attn_fir_short_w': _L0_attn_in['fir_short_w'], 'L0_attn_fir_long_w': _L0_attn_in['fir_long_w'], 'L0_attn_gate_w1': _L0_attn_in['gate_w1'], 'L0_attn_gate_b1': _L0_attn_in['gate_b1'], 'L0_attn_gate_w2': _L0_attn_in['gate_w2'], 'L0_attn_log_temp': _L0_attn_in['log_temp'], 'L0_attn_base_bias': _L0_attn_in['base_bias'], 'L0_attn_floor_raw': _L0_attn_in['floor_raw'], 'L0_attn_onorm_w': _L0_attn_in['onorm_w'], 'L0_attn_Wo': _L0_attn_in['Wo'], 'L0_ffn_router_w': _L0_ffn_in['router_w'], 'L0_ffn_router_b': _L0_ffn_in['router_b'], 'L0_ffn_we_gate': _L0_ffn_in['we_gate'], 'L0_ffn_we_up': _L0_ffn_in['we_up'], 'L0_ffn_we_down': _L0_ffn_in['we_down']}
    _x0 = _d['L0_attn_hidden_states']
    _d['L0_attn_hidden_states'] = jax.random.normal(jax.random.fold_in(jax.random.key(seed), 1), (16, 512, 256), dtype=_x0.dtype)
    del _x0
    return _d

def reference(L0_attn_hidden_states, L0_attn_Wq, L0_attn_Wk, L0_attn_Wv, L0_attn_Wb, L0_attn_qconv_w, L0_attn_kconv_w, L0_attn_vconv_w, L0_attn_fir_short_w, L0_attn_fir_long_w, L0_attn_gate_w1, L0_attn_gate_b1, L0_attn_gate_w2, L0_attn_log_temp, L0_attn_base_bias, L0_attn_floor_raw, L0_attn_onorm_w, L0_attn_Wo, L0_ffn_router_w, L0_ffn_router_b, L0_ffn_we_gate, L0_ffn_we_up, L0_ffn_we_down):

    def _L0_attn_ref(hidden_states, Wq, Wk, Wv, Wb, qconv_w, kconv_w, vconv_w, fir_short_w, fir_long_w, gate_w1, gate_b1, gate_w2, log_temp, base_bias, floor_raw, onorm_w, Wo):
        import jax, jax.numpy as jnp
        import numpy as np
        CHUNK = 32

        def _l2norm(x):
            return x * jax.lax.rsqrt(jnp.sum(x * x, -1, keepdims=True) + 1e-06)

        def _short_conv(x, w):
            K = w.shape[-1]
            L = x.shape[1]
            xp = jnp.pad(x, ((0, 0), (K - 1, 0), (0, 0)))
            y = sum((xp[:, t:t + L, :] * w[:, t] for t in range(K)))
            return jax.nn.silu(y)

        def _fir_conv(x, w):
            B, L, H, D = x.shape
            K = w.shape[-1]
            xf = x.reshape(B, L, H * D).transpose(0, 2, 1)
            wf = w.reshape(H * D, 1, K)
            y = jax.lax.conv_general_dilated(xf, wf, (1,), [(K - 1, 0)], feature_group_count=H * D, dimension_numbers=('NCH', 'OIH', 'NCH'))
            return y.transpose(0, 2, 1).reshape(B, L, H, D)

        def _delta_rule(q, k, v, beta, chunk=CHUNK):
            B, H, L, Dk = q.shape
            Dv = v.shape[-1]
            pad = -L % chunk
            if pad:
                q, k, v = (jnp.pad(t, ((0, 0), (0, 0), (0, pad), (0, 0))) for t in (q, k, v))
                beta = jnp.pad(beta, ((0, 0), (0, 0), (0, pad)))
            Lp = L + pad
            n = Lp // chunk
            q = _l2norm(q)
            k = _l2norm(k)
            v = v * beta[..., None]
            kb = k * beta[..., None]
            resh = lambda t: t.reshape(B, H, n, chunk, -1)
            q, k, v, kb = map(resh, (q, k, v, kb))
            tri = jnp.triu(jnp.ones((chunk, chunk), bool))
            tri_s = jnp.triu(tri, 1)
            A = jnp.where(tri, 0.0, -jnp.einsum('bhncd,bhnmd->bhncm', kb, k))
            for i in range(1, chunk):
                A = A.at[..., i, :i].add(jnp.einsum('...j,...jk->...k', A[..., i, :], A[..., :, :i]))
            T = A + jnp.eye(chunk, dtype=A.dtype)
            u = T @ v
            w = T @ kb

            def step(S, inp):
                qi, ki, ui, wi = inp
                attn = jnp.where(tri_s, 0.0, qi @ jnp.swapaxes(ki, -1, -2))
                u_i = ui - wi @ S
                o = qi @ S + attn @ u_i
                S = S + jnp.swapaxes(ki, -1, -2) @ u_i
                return (S, o)
            S0 = jnp.zeros((B, H, Dk, Dv), q.dtype)
            blocks = lambda t: jnp.moveaxis(t, 2, 0)
            S, out = jax.lax.scan(step, S0, (blocks(q), blocks(k), blocks(u), blocks(w)))
            out = jnp.moveaxis(out, 0, 2).reshape(B, H, Lp, Dv)[:, :, :L]
            return (out, S)
        B, L, D = hidden_states.shape
        H = log_temp.shape[0]
        P = 4
        q = _short_conv(hidden_states @ Wq.T, qconv_w).reshape(B, L, H, -1)
        k = _short_conv(hidden_states @ Wk.T, kconv_w).reshape(B, L, H, -1)
        v = _short_conv(hidden_states @ Wv.T, vconv_w).reshape(B, L, H, -1)
        beta = jax.nn.sigmoid(hidden_states @ Wb.T)
        tr = lambda t: jnp.swapaxes(t, 1, 2)
        delta, _S = _delta_rule(tr(q), tr(k), tr(v), jnp.swapaxes(beta, 1, 2))
        delta = jnp.swapaxes(delta, 1, 2)
        short = _fir_conv(v, fir_short_w)
        longp = _fir_conv(v, fir_long_w)
        paths = (short, longp, delta, v)

        def stats(p):
            m = p.mean(-1)
            va = p.var(-1)
            return jnp.stack([m, va], -1).reshape(B, L, H * 2)
        gate_in = jnp.concatenate([hidden_states] + [stats(p) for p in paths], -1)
        hmid = jax.nn.gelu(gate_in @ gate_w1.T + gate_b1, approximate=False)
        logits = hmid @ gate_w2.T + base_bias.reshape(-1)
        temp = jax.nn.softplus(log_temp) + 0.0001
        logits = logits.reshape(B, L, H, P) / temp[None, None, :, None]
        probs = jax.nn.softmax(logits, -1)
        floor_val = 0.05 * jax.nn.sigmoid(floor_raw)
        probs = jnp.maximum(probs, floor_val)
        probs = probs / probs.sum(-1, keepdims=True)
        out = sum((probs[..., i, None] * p for i, p in enumerate(paths)))
        out = out * jax.lax.rsqrt(jnp.mean(out * out, -1, keepdims=True) + 1e-05) * onorm_w
        return out.reshape(B, L, -1) @ Wo.T

    def _L0_ffn_ref(x, router_w, router_b, we_gate, we_up, we_down):
        import jax, jax.numpy as jnp
        import numpy as np
        EMBED = 256
        NUM_EXPERTS = 8
        TOP_K = 2
        x_shape = x.shape
        x_flat = x.reshape(-1, x_shape[-1])
        num_tokens = x_flat.shape[0]
        router_logits = x_flat @ router_w + router_b
        topk_weights, topk_indices = jax.lax.top_k(router_logits, k=TOP_K)
        topk_weights = jax.nn.softmax(topk_weights, axis=-1)
        token_idx_mesh = jnp.repeat(jnp.arange(num_tokens), TOP_K)
        expert_idx_mesh = topk_indices.reshape(-1)
        sort_permutation = jnp.argsort(expert_idx_mesh)
        sorted_expert_idx = expert_idx_mesh[sort_permutation]
        sorted_token_idx = token_idx_mesh[sort_permutation]
        group_sizes = jnp.bincount(sorted_expert_idx, length=NUM_EXPERTS)
        sorted_tokens = x_flat[sorted_token_idx]
        ff_gate = jax.lax.ragged_dot(sorted_tokens, we_gate, group_sizes)
        ff_up = jax.lax.ragged_dot(sorted_tokens, we_up, group_sizes)
        activated = jax.nn.silu(ff_gate) * ff_up
        ff_out = jax.lax.ragged_dot(activated, we_down, group_sizes)
        sorted_weights = topk_weights.reshape(-1)[sort_permutation]
        ff_out = ff_out * sorted_weights[:, None]
        output_flat = jnp.zeros_like(x_flat).at[sorted_token_idx].add(ff_out)
        return output_flat.reshape(x_shape)
    x = L0_attn_hidden_states
    x = _layernorm(x + _L0_attn_ref(x, L0_attn_Wq, L0_attn_Wk, L0_attn_Wv, L0_attn_Wb, L0_attn_qconv_w, L0_attn_kconv_w, L0_attn_vconv_w, L0_attn_fir_short_w, L0_attn_fir_long_w, L0_attn_gate_w1, L0_attn_gate_b1, L0_attn_gate_w2, L0_attn_log_temp, L0_attn_base_bias, L0_attn_floor_raw, L0_attn_onorm_w, L0_attn_Wo), axis=-1)
    x = _layernorm(x + _L0_ffn_ref(x, L0_ffn_router_w, L0_ffn_router_b, L0_ffn_we_gate, L0_ffn_we_up, L0_ffn_we_down), axis=-1)
    return x

_drawn_inputs = setup_inputs


def setup_inputs(seed=0):
    import zlib

    import numpy as np

    out = dict(_drawn_inputs(seed))
    spreads = {'L0_attn_gate_b1': (0.0, 0.333),
     'L0_attn_log_temp': (0.0, 0.452),
     'L0_attn_floor_raw': (-0.6931471824645996, 0.6),
     'L0_attn_onorm_w': (1.0, 0.2),
     'L0_ffn_router_b': (0.0, 0.1)}
    factors = {}
    for name, (base, spread) in spreads.items():
        noise = np.random.default_rng([zlib.crc32(name.encode()), seed]).standard_normal(out[name].shape)
        drawn = base * np.exp(spread * noise) if base else spread * noise
        out[name] = jnp.asarray(drawn.astype(out[name].dtype))
    for name, factor in factors.items():
        out[name] = (out[name] * factor).astype(out[name].dtype)
    return out
```

```python
from contextlib import ExitStack

import concourse.bass as bass
from concourse import mybir

F32 = mybir.dt.float32
BF16 = mybir.dt.bfloat16
U32 = mybir.dt.uint32
I32 = mybir.dt.int32
ALU = mybir.AluOpType
ACT = mybir.ActivationFunctionType
AX = mybir.AxisListType

P = 128
BATCH, SEQ, D = 16, 512, 256
HEADS, DH = 4, 64
TOKENS = BATCH * SEQ
TILES = TOKENS // P
TPB = SEQ // P
CH = D // P
PAIRS = BATCH // 2
PT = 2 * TPB
PTOK = 2 * SEQ
FIR = 63
SHORT = 3
TAPS = 4
FPAD = 320
OCT = 8


def need(eng, sem, value):
    if isinstance(value, int) and value <= 0:
        return
    eng.wait_ge(sem, value)


def hold(eng, sem, value):
    need(eng, sem, value)
    if not isinstance(value, int):
        eng.nop(nofuse=True)


def back(it, g, k, per):
    q = g - k
    n = 0
    while q < 0:
        q += per
        n += 1
    return (it - n if n else it), q


def conv_and_fir(nc, t):
    per = 2 * CH
    groups = PAIRS * per
    with ExitStack() as ctx:
        def sb(name, shape, dt=F32):
            return ctx.enter_context(nc.sbuf_tensor(name, shape, dt))

        def ps(name, shape):
            return ctx.enter_context(nc.psum_tensor(name, shape, F32))

        def sem(name):
            return ctx.enter_context(nc.semaphore(name))

        v_all = sb("v_all", [P, TILES, D])
        long_sb = sb("long_sb", [P, TILES, D])
        toep = sb("toep", [P, 2, OCT, 192])
        x_t = sb("xA", [P, 2, CH, SEQ])
        wv = sb("wvA", [P, CH, D])
        cw = sb("cwA", [P, CH, TAPS])
        fw = sb("fwA", [P, CH, SHORT])
        ident = sb("identA", [P, P])
        flip = sb("flipA", [P, P])
        conv = sb("convA", [P, 2, SEQ])
        v_t = sb("vtA", [P, 2, SEQ])
        sh_t = sb("shtA", [P, 2, SEQ])
        mid = sb("midA", [P, SEQ - 1])
        v_tok = sb("vtokA", [P, 2, TPB, D])
        sh_tok = sb("shtokA", [P, 2, TPB, D])
        ps_x = [ps(f"psxA{i}", [P, SEQ]) for i in range(2)]
        ps_v = ps("psvA", [P, TPB, P])
        ps_r = ps("psrA", [P, TPB, P])
        ps_s = ps("pssA", [P, TPB, P])
        ps_f = [ps(f"psfA{i}", [P, OCT, TILES]) for i in range(2)]

        weights_in = sem("A_weights_in")
        x_in = [sem(f"A_x_in{i}") for i in range(2)]
        toep_in = [sem(f"A_toep_in{i}") for i in range(2)]
        ident_z = sem("A_ident_zero")
        ident_ok = sem("A_ident_ok")
        projected = sem("A_projected")
        tap3 = sem("A_tap3")
        taps = sem("A_taps")
        v_ready = sem("A_v_ready")
        sh_start = sem("A_sh_start")
        sh_prod = sem("A_sh_prod")
        sh_mid = sem("A_sh_mid")
        sh_ready = sem("A_sh_ready")
        v_turned = sem("A_v_turned")
        sh_turned = sem("A_sh_turned")
        v_kept = sem("A_v_kept")
        r_turned = sem("A_r_turned")
        r_kept = sem("A_r_kept")
        sh_kept = sem("A_sh_kept")
        v_out = [sem(f"A_v_out{i}") for i in range(2)]
        sh_out = [sem(f"A_sh_out{i}") for i in range(2)]
        fir_done = sem("A_fir_done")
        long_kept = [sem(f"A_long_kept{i}") for i in range(2)]
        long_out = sem("A_long_out")

        xd = t["xT"].rearrange("(c p) n -> p c n", p=P)
        vd = t["v_d"].rearrange("(t p) c -> p t c", p=P)
        sd = t["short_d"].rearrange("(t p) c -> p t c", p=P)
        ld = t["long_d"].rearrange("(t p) c -> p t c", p=P)
        fl = t["fir_long"]
        octets = D // OCT

        with nc.Block() as block:
            @block.sync
            def _(sp):
                sp.dma_start(wv[:], t["WvT"].rearrange("(c p) n -> p c n", p=P)).then_inc(weights_in, 16)
                sp.dma_start(cw[:], t["vconv"].rearrange("(c p) k -> p c k", p=P)).then_inc(weights_in, 16)
                sp.dma_start(fw[:], t["fir_short"].rearrange("(c p) k -> p c k", p=P)).then_inc(weights_in, 16)

                def pair(p):
                    for b in range(2):
                        need(sp, projected, per * (p - 1) + CH * (b + 1))
                        sp.dma_start(x_t[:, b], xd[:, :, bass.ds(p * PTOK + b * SEQ, SEQ)]).then_inc(x_in[b], 16)
                pair(0)
                with sp.Fori(1, PAIRS) as p:
                    pair(p)

            @block.gpsimd
            def _(pool):
                pool.memset(ident[:], 0.0).then_inc(ident_z, 1)
                pool.memset(flip[:], 0.0).then_inc(ident_z, 1)
                pool.wait_ge(ident_z, 2)
                pool.affine_select(out=ident[:], in_=ident[:], compare_op=ALU.not_equal, fill=1.0, base=0,
                                   pattern=[[-1, P]], channel_multiplier=1).then_inc(ident_ok, 1)
                pool.affine_select(out=flip[:], in_=flip[:], compare_op=ALU.not_equal, fill=1.0, base=1 - P,
                                   pattern=[[1, P]], channel_multiplier=1).then_inc(ident_ok, 1)
                def load_toep(o, u):
                    pool.dma_start(toep[:, u], bass.AP(fl.tensor, o * (OCT * FPAD),
                                                       [[1, P], [FPAD, OCT], [1, 192]])).then_inc(toep_in[u], 16)
                for u in range(2):
                    load_toep(u, u)
                pool.wait_ge(weights_in, 48)

                def pair(p):
                    for g in range(per):
                        n = per * p + g
                        pool.wait_ge(sh_start, n + 1)
                        need(pool, sh_mid, n)
                        pool.tensor_tensor(mid[:], v_t[:, g % 2, :SEQ - 1],
                                           fw[:, g % CH, 1:2].to_broadcast([P, SEQ - 1]), ALU.mult).then_inc(sh_prod, 1)
                        pool.wait_ge(sh_prod, n + 1)
                        pool.tensor_tensor(sh_t[:, g % 2, 1:], sh_t[:, g % 2, 1:], mid[:], ALU.add).then_inc(sh_mid, 1)
                        if g % CH == CH - 1:
                            b = g // CH
                            pool.wait_ge(v_kept, n + 1)
                            pool.wait_ge(sh_kept, n + 1)
                            rows = bass.ds(p * PT + b * TPB, TPB)
                            pool.dma_start(vd[:, rows, :], v_tok[:, b]).then_inc(v_out[b], 16)
                            pool.dma_start(sd[:, rows, :], sh_tok[:, b]).then_inc(sh_out[b], 16)
                pair(0)
                with pool.Fori(1, PAIRS) as p:
                    pair(p)
                for o in range(2, octets):
                    pool.wait_ge(fir_done, o - 1)
                    load_toep(o, o % 2)
                pool.wait_ge(long_kept[0], octets // 2)
                pool.wait_ge(long_kept[1], octets // 2)
                for q in range(4):
                    rows = slice(q * TILES // 4, (q + 1) * TILES // 4)
                    pool.dma_start(ld[:, rows, :], long_sb[:, rows, :]).then_inc(long_out, 16)
                pool.wait_ge(long_out, 64)
                for b in range(2):
                    pool.wait_ge(v_out[b], 16 * PAIRS)
                    pool.wait_ge(sh_out[b], 16 * PAIRS)

            def slots(eng, body, lag):
                for g in range(2 * per):
                    body(g // per, g % per, lambda k, g=g: g >= k)
                with eng.Fori(2, PAIRS) as p:
                    for g in range(per):
                        body(p, g, lambda k: True)
                for g in range(lag):
                    body(PAIRS, g, lambda k, g=g: k > g)

            @block.tensor
            def _(pe):
                pe.wait_ge(weights_in, 48)
                pe.wait_ge(ident_ok, 2)

                def slot(p, g, has):
                    if has(0):
                        n = per * p + g
                        if g % CH == 0:
                            pe.wait_ge(x_in[g // CH], 16 * (p + 1))
                        need(pe, taps, 3 * (n - 1))
                        for c in range(CH):
                            mm = nc.tensor.matmul(ps_x[g % 2][:], wv[:, c, (g % CH) * P:(g % CH + 1) * P],
                                                  x_t[:, g // CH, c, :], start=c == 0, stop=c == CH - 1)
                        mm.then_inc(projected, 1)
                    if has(2):
                        q, h = back(p, g, 2, per)
                        n = per * q + h
                        pe.wait_ge(v_ready, n + 1)
                        need(pe, v_kept, n)
                        for j in range(TPB):
                            mm = nc.tensor.transpose(ps_v[:, j, :], v_t[:, h % 2, j * P:(j + 1) * P], ident[:])
                        mm.then_inc(v_turned, 1)
                        pe.wait_ge(sh_ready, n + 1)
                        need(pe, sh_kept, n)
                        for j in range(TPB):
                            mm = nc.tensor.transpose(ps_s[:, j, :], sh_t[:, h % 2, j * P:(j + 1) * P], ident[:])
                        mm.then_inc(sh_turned, 1)
                    if has(4):
                        q, h = back(p, g, 4, per)
                        b, m = h // CH, h % CH
                        pe.wait_ge(v_kept, per * q + h + 1)
                        need(pe, r_kept, per * q + h)
                        nc.tensor.matmul(ps_r[:], flip[:], v_tok[:, b, :, m * P:(m + 1) * P], start=True,
                                         stop=True).then_inc(r_turned, 1)
                slots(pe, slot, 4)

                pe.wait_ge(r_kept, groups)
                byseq = v_all[:].rearrange("p (b t) c -> p b t c", t=TPB)

                def octets2(k):
                    for u in range(2):
                        pe.wait_ge(toep_in[u], 16 * (k + 1))
                        need(pe, long_kept[u], k)
                        for c in range(OCT):
                            ch = (2 * k + u) * OCT + c
                            nc.tensor.matmul(ps_f[u][:, c, :], toep[:, u, c, 0:P],
                                             v_all[:, :, bass.ds(ch, 1)], start=True, stop=True)
                            out = ps_f[u][0:64, c, :].rearrange("p (b t) -> p b t", t=TPB)[:, :, 1:TPB]
                            mm = nc.tensor.matmul(out, toep[:, u, c, P:192],
                                                  byseq[:, :, 0:TPB - 1, bass.ds(ch, 1)], start=False, stop=True,
                                                  skip_group_check=True)
                        mm.then_inc(fir_done, 1)
                octets2(0)
                with pe.Fori(1, octets // 2) as k:
                    octets2(k)

            def keep_long(eng, copy, k, u):
                eng.wait_ge(fir_done, 2 * k + u + 1)
                copy(long_sb[:, :, bass.ds((2 * k + u) * OCT, OCT)],
                     ps_f[u][:].rearrange("p c t -> p t c")).then_inc(long_kept[u], 1)

            @block.scalar
            def _(act):
                act.wait_ge(weights_in, 48)

                def slot(p, g, has):
                    if has(0):
                        n = per * p + g
                        act.wait_ge(projected, n + 1)
                        need(act, v_ready, n - 1)
                        nc.scalar.activation(conv[:, g % 2], ps_x[g % 2][:], ACT.Copy,
                                             scale=cw[:, g % CH, 3:4]).then_inc(tap3, 1)
                    if has(1):
                        q, h = back(p, g, 1, per)
                        n = per * q + h
                        act.wait_ge(taps, 3 * (n + 1))
                        need(act, v_turned, n - 1)
                        need(act, sh_turned, n - 1)
                        nc.scalar.activation(v_t[:, h % 2], conv[:, h % 2], ACT.Silu).then_inc(v_ready, 1)
                        act.wait_ge(v_ready, n + 1)
                        nc.scalar.activation(sh_t[:, h % 2], v_t[:, h % 2], ACT.Copy,
                                             scale=fw[:, h % CH, 2:3]).then_inc(sh_start, 1)
                    if has(3):
                        q, h = back(p, g, 3, per)
                        n = per * q + h
                        b, m = h // CH, h % CH
                        act.wait_ge(v_turned, n + 1)
                        need(act, r_turned, n - per + 1)
                        if m == 0:
                            need(act, v_out[b], 16 * q)
                        nc.scalar.activation(v_tok[:, b, :, m * P:(m + 1) * P], ps_v[:], ACT.Copy).then_inc(v_kept, 1)
                        act.wait_ge(sh_turned, n + 1)
                        if m == 0:
                            need(act, sh_out[b], 16 * q)
                        nc.scalar.activation(sh_tok[:, b, :, m * P:(m + 1) * P], ps_s[:],
                                             ACT.Copy).then_inc(sh_kept, 1)
                slots(act, slot, 3)

                def copy(out, in_):
                    return nc.scalar.activation(out, in_, ACT.Copy)
                keep_long(act, copy, 0, 1)
                with act.Fori(1, octets // 2) as k:
                    keep_long(act, copy, k, 1)

            @block.vector
            def _(dve):
                dve.wait_ge(weights_in, 48)

                def slot(p, g, has):
                    if has(0):
                        n = per * p + g
                        dve.wait_ge(tap3, n + 1)
                        for k in range(1, TAPS):
                            need(dve, taps, 3 * n + k - 1)
                            nc.vector.scalar_tensor_tensor(
                                conv[:, g % 2, k:], ps_x[g % 2][:, :SEQ - k], cw[:, g % CH, 3 - k:4 - k],
                                conv[:, g % 2, k:], ALU.mult, ALU.add).then_inc(taps, 1)
                    if has(1):
                        q, h = back(p, g, 1, per)
                        n = per * q + h
                        dve.wait_ge(sh_mid, n + 1)
                        nc.vector.scalar_tensor_tensor(
                            sh_t[:, h % 2, 2:], v_t[:, h % 2, :SEQ - 2], fw[:, h % CH, 0:1],
                            sh_t[:, h % 2, 2:], ALU.mult, ALU.add).then_inc(sh_ready, 1)
                    if has(4):
                        q, h = back(p, g, 4, per)
                        dve.wait_ge(r_turned, per * q + h + 1)
                        nc.vector.tensor_copy(v_all[:, bass.ds(q * PT + h // CH * TPB, TPB),
                                                    h % CH * P:(h % CH + 1) * P], ps_r[:]).then_inc(r_kept, 1)
                slots(dve, slot, 4)
                keep_long(dve, nc.vector.tensor_copy, 0, 0)
                with dve.Fori(1, octets // 2) as k:
                    keep_long(dve, nc.vector.tensor_copy, k, 0)


NEXP, TOPK = 8, 2
CAP = TOKENS + P
GATE_HID = 512
STATS = 32
PATHS = 4
HID_CH = GATE_HID // P
BLK = 32
NBLK = P // BLK
UNITS = PT * HEADS


def delta_and_gate(nc, t, keep):
    with ExitStack() as ctx:
        def sb(name, shape, dt=F32):
            return ctx.enter_context(nc.sbuf_tensor("B_" + name, shape, dt))

        def ps(name, shape=(P, 512)):
            return ctx.enter_context(nc.psum_tensor("B_ps_" + name, list(shape), F32))

        def sem(name):
            return ctx.enter_context(nc.semaphore("B_" + name))

        wq = sb("wq", [P, CH, D]); wk = sb("wk", [P, CH, D]); wb = sb("wb", [P, CH, HEADS])
        cw = sb("cw", [P, 2, CH, TAPS])
        w1x = sb("w1x", [P, CH, GATE_HID]); w1s = sb("w1s", [STATS, GATE_HID])
        b1 = sb("b1", [P, HID_CH]); w2 = sb("w2", [P, HID_CH, HEADS * PATHS])
        wo = sb("wo", [P, CH, D]); onw = sb("onw", [P, 1])
        rw = sb("rw", [P, CH, NEXP]); rb = sb("rb", [P, NEXP])
        bias16 = sb("bias16", [P, 16]); floor16 = sb("floor16", [P, 16]); itemp = sb("itemp", [P, HEADS])
        ident = sb("ident", [P, P]); upper = sb("upper", [P, P])
        before = sb("before", [P, P], BF16); ones = sb("ones", [P, P], BF16)
        headsel = sb("headsel", [P, 2]); iota8 = sb("iota8", [P, NEXP]); base8 = sb("base8", [P, NEXP])
        eps6 = sb("eps6", [P, 1]); eps5 = sb("eps5", [P, 1])
        xa = sb("xa", [P, CH, PTOK])
        conv = sb("conv", [P, 2, SEQ]); sq = sb("sq", [P, 2, SEQ])
        kraw = sb("kraw", [P, CH, PTOK]); k_t = sb("k_t", [P, CH, PTOK]); q_t = sb("q_t", [P, CH, PTOK])
        k_tok = sb("k_tok", [P, PT, D])
        nrm = sb("nrm", [P, 2, PT * HEADS]); rn = sb("rn", [P, 2, PT * HEADS])
        th = sb("th", [P, PT * HEADS]); beta = sb("beta", [P, PT, HEADS]); nbeta = sb("nbeta", [P, PT, HEADS])
        a_sb = sb("a_sb", [P, PT, HEADS, P])
        at_t = sb("at_t", [P, PT, HEADS, P])
        z = sb("z", [P, BLK, BLK]); zt = sb("zt", [P, BLK, BLK])
        xf = sb("xf", [P, UNITS, 2 * BLK]); mt = sb("mt", [P, UNITS, P])
        s_bd = sb("s_bd", [P, 4, P])
        r_sb = sb("r_sb", [P, 2, HEADS, DH]); u_sb = sb("u_sb", [P, 2, HEADS, DH])
        v_tok = sb("v_tok", [P, PT, D]); delta = sb("delta", [P, PT, D])
        xg = sb("xg", [P, CH, SEQ])
        sh = sb("sh", [P, 2, TPB, D]); lo = sb("lo", [P, 2, TPB, D]); x1 = sb("x1", [P, 2, TPB, D])
        hid = sb("hid", [P, HID_CH, SEQ])
        bn = sb("bn", [P, TPB, PATHS, HEADS, 6]); dm = sb("dm", [P, TPB, STATS // 2]); gst = sb("gst", [P, TPB, STATS])
        st_t = sb("st_t", [STATS, SEQ])
        lg = sb("lg", [P, 16, PATHS]); s16 = sb("s16", [P, 16]); r16 = sb("r16", [P, 16])
        tmp = sb("tmp", [P, TPB, D])
        o_t = sb("o_t", [P, CH, SEQ])
        lbn = sb("lbn", [P, TPB, 6]); mv = sb("mv", [P, TPB, 2]); rstd = sb("rstd", [P, TPB])
        rl = sb("rl", [P, TPB, NEXP]); mx8 = sb("mx8", [P, TPB, 8]); mi8 = sb("mi8", [P, TPB, 8], U32)
        ef = sb("ef", [P, TPB * TOPK]); oh = sb("oh", [P, TPB * TOPK, NEXP]); m_bf = sb("m_bf", [P, TPB, NEXP], BF16); m_sum = sb("m_sum", [P, NEXP])
        rk = sb("rk", [P, TPB, NEXP]); slot_u = sb("slot_u", [P, 2, TPB * TOPK], U32)
        z1 = tmp[:].rearrange("p t (a b) -> p (t a) b", b=BLK)
        z2 = hid[:].rearrange("p c (a b) -> p (c a) b", b=2 * BLK)

        X = [ps("x0"), ps("x1")]
        B2, B3, B4, B5, SM, TR = (ps(n) for n in ("b2", "b3", "b4", "b5", "small", "turn"))

        w_in = sem("weights_in"); pool_c = sem("pool_const"); dve_c = sem("dve_const"); act_c = sem("act_const")
        xa_in, xg_in = sem("xa_in"), sem("xg_in")
        v_in = sem("v_in")
        sl_in = [sem(f"short_long_in{i}") for i in range(2)]; x_in = [sem(f"x_in{i}") for i in range(2)]
        projected, tap3, taps, raw = sem("projected"), sem("tap3"), sem("taps"), sem("silu_done")
        squared, selected = sem("squared"), sem("selected")
        beta_mm, beta_th, beta_ok = sem("beta_mm"), sem("beta_th"), sem("beta_ok")
        rooted, rn_ok = sem("norm_rooted"), sem("norm_ok")
        k_turned, k_kept, k_back, kt_kept = sem("k_turned"), sem("k_kept"), sem("k_back"), sem("kt_kept")
        a_mm, a_kept, at_mm, at_kept = sem("a_mm"), sem("a_kept"), sem("at_mm"), sem("at_kept")
        a_out, z_in, solve, x_out, x_back = sem("a_out"), sem("z_in"), sem("solve"), sem("x_out"), sem("x_back")
        m_pe, m_dve, m_act = sem("merge_pe"), sem("merge_dve"), sem("merge_act")
        s_zero, r_p, r_q, r_r1, r_r, r_u, r_ub = (sem(n) for n in (
            "s_zero", "rec_p", "rec_q", "rec_r1", "rec_r", "rec_u", "rec_ub"))
        r_sx, r_s, r_o, r_out = sem("rec_sx"), sem("rec_s"), sem("rec_o"), sem("rec_out")
        st_dve, st_turned, st_kept = sem("stats_dve"), sem("stats_turned"), sem("stats_kept")
        gate_mm, gelu_ok, logit_mm = sem("gate_mm"), sem("gelu_ok"), sem("logit_mm")
        sm_dve, sm_exp = sem("softmax_dve"), sem("softmax_exp")
        mixp, mix = sem("mix_pool"), sem("mix_dve")
        sq_ok, rms_rt = sem("rms_squared"), sem("rms_rooted")
        o_turned, o_kept, wo_mm = sem("o_turned"), sem("o_kept"), sem("wo_mm")
        ln, ln_rt = sem("ln_dve"), sem("ln_rooted")
        x1_turned, x1_kept, rt_mm = sem("x1_turned"), sem("x1_kept"), sem("router_mm")
        rt, ranked = sem("route_dve"), sem("ranked")
        scattered = [sem(f"scattered{i}") for i in range(2)]; x1_out = [sem(f"x1_out{i}") for i in range(2)]

        xd = t["xT"].rearrange("(c p) n -> p c n", p=P)
        tok = lambda n: t[n].rearrange("(t p) c -> p t c", p=P)
        POOL_C = 12
        LN, RT = 15, 14
        eidx, slotf, top2, m_acc = keep["eidx"], keep["slotf"], keep["top2"], keep["m_acc"]

        def hp(h):
            return slice((h % 2) * DH, (h % 2 + 1) * DH)

        with nc.Block() as block:
            @block.sync
            def _(sp):
                bc = lambda name, n: t[name].rearrange("(o n) -> o n", o=1).to_broadcast([P, n])
                rows = lambda name: t[name].rearrange("(c p) n -> p c n", p=P)
                for dst, src in (
                    (wq[:], rows("WqT")), (wk[:], rows("WkT")), (wb[:], rows("WbT")),
                    (cw[:, 0], rows("kconv")), (cw[:, 1], rows("qconv")),
                    (w1x[:], t["w1T"][0:D, :].rearrange("(c p) n -> p c n", p=P)), (w1s[:], t["w1T"][D:D + STATS, :]),
                    (b1[:], t["b1"]), (w2[:], rows("w2T")), (wo[:], rows("WoT")),
                    (onw[0:DH, :], t["onorm"].rearrange("(p o) -> p o", o=1)),
                    (onw[DH:P, :], t["onorm"].rearrange("(p o) -> p o", o=1)),
                    (rw[:], rows("rw")), (rb[:], bc("rb", NEXP)), (bias16[:], bc("bias", 16)),
                    (floor16[:], bc("floor", 16)), (itemp[:], bc("log_temp", HEADS)),
                ):
                    sp.dma_start(dst, src).then_inc(w_in, 16)

                def load_xa(p):
                    hold(sp, beta_mm, p)
                    hold(sp, projected, 8 * p)
                    sp.dma_start(xa[:], xd[:, :, bass.ds(p * PTOK, PTOK)]).then_inc(xa_in, 16)

                def load_half(i, b):
                    if not isinstance(i, int) or i > 0:
                        hold(sp, mix, 7 * (2 * i + b - 1))
                        hold(sp, o_turned, 2 * (2 * i + b - 1))
                    hold(sp, scattered[b], 16 * 8 * i)
                    hold(sp, x1_out[b], 16 * i)
                    r = bass.ds(i * PT + b * TPB, TPB)
                    sp.dma_start(sh[:, b], tok("short_d")[:, r, :]).then_inc(sl_in[b], 16)
                    sp.dma_start(lo[:, b], tok("long_d")[:, r, :]).then_inc(sl_in[b], 16)
                    sp.dma_start(x1[:, b], tok("x")[:, r, :]).then_inc(x_in[b], 16)

                def load_xg(i, b):
                    hold(sp, gate_mm, 4 * (2 * i + b))
                    sp.dma_start(xg[:], xd[:, :, bass.ds(i * PTOK + b * SEQ, SEQ)]).then_inc(xg_in, 16)

                def load_v(i):
                    hold(sp, mixp, 3 * 2 * i)
                    hold(sp, st_dve, 7 * 2 * i)
                    sp.dma_start(v_tok[:], tok("v_d")[:, bass.ds(i * PT, PT), :]).then_inc(v_in, 16)

                def solve_dmas(p):
                    hold(sp, a_kept, 8 * (p + 1))
                    for k in range(NBLK):
                        s = slice(k * BLK, (k + 1) * BLK)
                        sp.dma_start(t["scr_a"][k], a_sb[s, :, :, s].rearrange("i t h k -> i (t h) k")).then_inc(a_out, 16)
                    hold(sp, a_out, 64 * (p + 1))
                    for k in range(NBLK):
                        sp.dma_start(z[k * BLK:(k + 1) * BLK], t["scr_a"][k].rearrange("i u k -> u i k")).then_inc(z_in, 16)

                def solved_dmas(p):
                    hold(sp, solve, 64 * (p + 1))
                    sp.dma_start(t["scr_x"][:], z[:]).then_inc(x_out, 16)
                    sp.dma_start(t["scr_xt"][:], zt[:]).then_inc(x_out, 16)
                    hold(sp, x_out, 32 * (p + 1))
                    for k in range(NBLK):
                        s = slice(k * BLK, (k + 1) * BLK)
                        c = (k % 2) * BLK
                        sp.dma_start(xf[s, :, c:c + BLK], t["scr_x"][s].rearrange("u i k -> i u k")).then_inc(x_back, 16)
                        sp.dma_start(mt[s, :, s], t["scr_xt"][s].rearrange("u k i -> k u i")).then_inc(x_back, 16)

                def store_x1(i):
                    for b in range(2):
                        hold(sp, ln, LN * (2 * i + b + 1))
                        sp.dma_start(tok("x1_d")[:, bass.ds(i * PT + b * TPB, TPB), :], x1[:, b]).then_inc(x1_out[b], 16)

                load_xa(0)
                load_v(0)
                solve_dmas(0)
                solved_dmas(0)

                def step(i, has_next):
                    if has_next:
                        load_xa(i + 1)
                    if not isinstance(i, int) or i > 0:
                        load_v(i)
                    load_half(i, 0)
                    load_half(i, 1)
                    load_xg(i, 0)
                    if has_next:
                        solve_dmas(i + 1)
                    load_xg(i, 1)
                    if has_next:
                        solved_dmas(i + 1)
                    store_x1(i)
                step(0, True)
                with sp.Fori(1, PAIRS - 1) as i:
                    step(i, True)
                step(PAIRS - 1, False)
                for b in range(2):
                    hold(sp, x1_out[b], 16 * PAIRS)

            @block.gpsimd
            def _(pool):
                pool.memset(ident[:], 0.0).then_inc(pool_c, 1)
                pool.memset(upper[:], 1.0).then_inc(pool_c, 1)
                pool.memset(before[:], 1.0).then_inc(pool_c, 1)
                pool.memset(ones[:], 1.0).then_inc(pool_c, 1)
                pool.memset(headsel[:], 1.0).then_inc(pool_c, 1)
                pool.iota(mi8[:, 0, :], [[1, NEXP]], base=0, channel_multiplier=0).then_inc(pool_c, 1)
                pool.wait_ge(pool_c, 6)
                pool.affine_select(out=ident[:], in_=ident[:], compare_op=ALU.not_equal, fill=1.0, base=0,
                                   pattern=[[-1, P]], channel_multiplier=1).then_inc(pool_c, 1)
                pool.affine_select(out=upper[:], in_=upper[:], compare_op=ALU.is_ge, fill=0.0, base=0,
                                   pattern=[[1, P]], channel_multiplier=-1).then_inc(pool_c, 1)
                pool.affine_select(out=before[:], in_=before[:], compare_op=ALU.is_gt, fill=0.0, base=0,
                                   pattern=[[1, P]], channel_multiplier=-1).then_inc(pool_c, 1)
                pool.affine_select(out=headsel[:, 0:1], in_=headsel[:, 0:1], compare_op=ALU.is_gt, fill=0.0, base=DH,
                                   pattern=[[0, 1]], channel_multiplier=-1).then_inc(pool_c, 1)
                pool.affine_select(out=headsel[:, 1:2], in_=headsel[:, 1:2], compare_op=ALU.is_ge, fill=0.0, base=-DH,
                                   pattern=[[0, 1]], channel_multiplier=1).then_inc(pool_c, 1)
                pool.memset(m_acc[:], 0.0).then_inc(pool_c, 1)

                def zero_state(p):
                    need(pool, r_q, 4 * p)
                    pool.nop(nofuse=True)
                    pool.memset(s_bd[:], 0.0).then_inc(s_zero, 1)

                def solver(p):
                    pool.wait_ge(z_in, 64 * (p + 1))
                    c = 64 * p
                    pool.nop(nofuse=True)
                    pool.affine_select(out=z[:], in_=z[:], compare_op=ALU.is_gt, fill=0.0, base=0,
                                       pattern=[[1, BLK], [-1, BLK]], channel_multiplier=0).then_inc(solve, 1)
                    pool.wait_ge(solve, c + 1)
                    pool.nop(nofuse=True)
                    pool.affine_select(out=z[:], in_=z[:], compare_op=ALU.not_equal, fill=1.0, base=0,
                                       pattern=[[1, BLK], [-1, BLK]], channel_multiplier=0).then_inc(solve, 1)
                    k = 2
                    need(pool, x_out, 32 * p)
                    for j in range(1, BLK - 1):
                        r = BLK - 1 - j
                        pool.wait_ge(solve, c + k)
                        pool.tensor_tensor(zt[:, 0:r, 0:j], z[:, j + 1:, j:j + 1].to_broadcast([P, r, j]),
                                           z[:, j:j + 1, 0:j].to_broadcast([P, r, j]), ALU.mult).then_inc(solve, 1)
                        pool.wait_ge(solve, c + k + 1)
                        pool.tensor_tensor(z[:, j + 1:, 0:j], z[:, j + 1:, 0:j], zt[:, 0:r, 0:j], ALU.add).then_inc(solve, 1)
                        k += 2
                    pool.wait_ge(solve, c + k)
                    pool.nop(nofuse=True)
                    pool.tensor_copy(zt[:], z[:].rearrange("p i k -> p k i")).then_inc(solve, 2)

                def mix_and_scatter(i, b):
                    half = 2 * i + b
                    p3 = lambda k: lg[:, :, k:k + 1].to_broadcast([P, 16, DH])
                    v3 = lambda x: x.rearrange("p t (h d) -> p (t h) d", d=DH)
                    pool.wait_ge(sm_dve, 11 * (half + 1))
                    pool.wait_ge(st_dve, 7 * (half + 1))
                    need(pool, mix, 7 * half)
                    pool.tensor_tensor(v3(tmp[:]), v3(v_tok[:, b * TPB:(b + 1) * TPB]), p3(3), ALU.mult).then_inc(mixp, 1)
                    pool.tensor_tensor(v3(sh[:, b]), v3(sh[:, b]), p3(0), ALU.mult).then_inc(mixp, 1)
                    pool.wait_ge(mixp, 3 * half + 2)
                    pool.tensor_tensor(sh[:, b], sh[:, b], tmp[:], ALU.add).then_inc(mixp, 1)

                def scatter(i, b):
                    half = 2 * i + b
                    pool.wait_ge(rt, RT * (half + 1))
                    pool.nop(nofuse=True)
                    for j in range(TPB):
                        for k in range(TOPK):
                            c = j * TOPK + k
                            pool.indirect_dma_start(t["xs_d"][:, :], bass.IndirectOffsetOnAxis(
                                ap=slot_u[:, b, c:c + 1], axis=0), x1[:, b, j, :], None).then_inc(scattered[b], 16)

                pool.memset(mt[:], 0.0).then_inc(pool_c, 1)
                pool.memset(xf[:], 0.0).then_inc(pool_c, 1)
                zero_state(0)
                pool.wait_ge(pool_c, POOL_C + 2)
                solver(0)

                def step(i, has_next):
                    if has_next:
                        zero_state(i + 1)
                        solver(i + 1)
                    for b in range(2):
                        mix_and_scatter(i, b)
                    for b in range(2):
                        scatter(i, b)
                step(0, True)
                with pool.Fori(1, PAIRS - 1) as i:
                    step(i, True)
                step(PAIRS - 1, False)
                for b in range(2):
                    pool.wait_ge(scattered[b], 16 * 8 * PAIRS)

            @block.tensor
            def _(pe):
                mm = nc.tensor.matmul
                pe.wait_ge(w_in, 16 * 17)
                pe.wait_ge(pool_c, POOL_C + 2)
                pe.wait_ge(dve_c, 8)

                def project(p, g):
                    gg = g % 4
                    b, m = gg // CH, gg % CH
                    w = wk if g < 4 else wq
                    if g == 0:
                        pe.wait_ge(xa_in, 16 * (p + 1))
                    if g < 2:
                        need(pe, gelu_ok, 8 * (p - 1))
                    else:
                        pe.wait_ge(taps, 24 * p + 3 * (g - 1))
                    for c in range(CH):
                        i = mm(X[g % 2][:], w[:, c, m * P:(m + 1) * P], xa[:, c, b * SEQ:(b + 1) * SEQ],
                               start=c == 0, stop=c == CH - 1)
                    i.then_inc(projected, 1)

                def select(p, g):
                    kq, gg = g // 4, g % 4
                    b, m = gg // CH, gg % CH
                    pe.wait_ge(squared, 8 * p + g + 1)
                    for j in range(TPB):
                        c = kq * 32 + (b * TPB + j) * HEADS + m * 2
                        i = mm(SM[:, c:c + 2], sq[:, g % 2, j * P:(j + 1) * P], headsel[:], start=True, stop=True)
                    i.then_inc(selected, 1)

                def betas(p):
                    for j in range(PT):
                        for c in range(CH):
                            i = mm(SM[:, 64 + 4 * j:68 + 4 * j], xa[:, c, j * P:(j + 1) * P], wb[:, c, :],
                                   start=c == 0, stop=c == CH - 1)
                    i.then_inc(beta_mm, 1)

                def stage1b(p):
                    select(p, 3)
                    betas(p)
                    project(p, 4)
                    project(p, 5)
                    for j in range(4):
                        b, m = j // CH, j % CH
                        if j >= 2:
                            pe.wait_ge(k_kept, 4 * p + j - 1)
                        for q in range(TPB):
                            s = slice((b * TPB + q) * P, (b * TPB + q + 1) * P)
                            i = nc.tensor.transpose((TR, B2)[j % 2][:, q * P:(q + 1) * P], kraw[:, m, s], ident[:])
                        i.then_inc(k_turned, 1)
                    for j in range(4):
                        b, m = j // CH, j % CH
                        pe.wait_ge(k_kept, 4 * p + j + 1)
                        if j >= 2:
                            pe.wait_ge(kt_kept, 4 * p + j - 1)
                        for q in range(TPB):
                            i = nc.tensor.transpose((B3, B5)[j % 2][:, q * P:(q + 1) * P],
                                                    k_tok[:, b * TPB + q, m * P:(m + 1) * P], ident[:])
                        i.then_inc(k_back, 1)
                    pe.wait_ge(rooted, 2 * p + 1)
                    pe.wait_ge(beta_th, p + 1)
                    select(p, 4)
                    project(p, 6)
                    select(p, 5)
                    project(p, 7)
                    quad = (B2, B3, B4, B5)
                    pe.wait_ge(kt_kept, 4 * (p + 1))
                    for jj in range(PT // 2):
                        if jj == 1:
                            need(pe, r_out, 4 * p)
                        if jj >= 2:
                            pe.wait_ge(a_kept, 8 * p + 2 * (jj - 1))
                        for c in range(4):
                            s = slice((2 * jj + c // 2) * P, (2 * jj + c // 2 + 1) * P)
                            for par in range(2):
                                kk = k_t[hp(par), c % 2, s]
                                i = mm(quad[2 * (jj % 2) + par][:, c * P:(c + 1) * P], kk, kk, start=True, stop=True)
                                if c == 3:
                                    i.then_inc(a_mm, 1)
                    select(p, 6)
                    select(p, 7)
                    for jj in range(PT // 2):
                        if jj < 2:
                            pe.wait_ge(a_kept, 8 * p + 6 + 2 * jj)
                        else:
                            pe.wait_ge(at_kept, 8 * p + 2 * (jj - 1))
                        for c in range(4):
                            s = slice((2 * jj + c // 2) * P, (2 * jj + c // 2 + 1) * P)
                            for par in range(2):
                                i = mm(quad[2 * (jj % 2) + par][:, c * P:(c + 1) * P], k_t[hp(par), c % 2, s],
                                       q_t[hp(par), c % 2, s], start=True, stop=True)
                                if c == 3:
                                    i.then_inc(at_mm, 1)

                def merges(i):
                    pe.wait_ge(x_back, 128 * (i + 1))
                    pe.wait_ge(a_kept, 8 * (i + 1))
                    pe.wait_ge(at_kept, 8 * (i + 1))
                    need(pe, ln, LN * 2 * i)
                    need(pe, x1_kept, 2 * 2 * i)
                    pe.nop(nofuse=True)
                    for bank, u0 in ((B2, 0), (B3, 16)):
                        for u in range(u0, u0 + 16):
                            for q in range(2):
                                lo_, hi = q * 64, q * 64 + 32
                                w = mm(bank[lo_:lo_ + 32, (u - u0) * 32:(u - u0 + 1) * 32],
                                       a_sb[hi:hi + 32, u // 4, u % 4, lo_:lo_ + 32], mt[hi:hi + 32, u, hi:hi + 32],
                                       start=True, stop=True)
                        w.then_inc(m_pe, 1)
                    pe.wait_ge(m_dve, 9 * i + 2)
                    pe.wait_ge(m_act, 9 * i + 2)
                    pe.nop(nofuse=True)
                    for bank, u0 in ((B4, 0), (B5, 16)):
                        for u in range(u0, u0 + 16):
                            for q in range(2):
                                s = slice(q * 64, q * 64 + 32)
                                w = mm(bank[s, (u - u0) * 32:(u - u0 + 1) * 32], xf[s, u, 0:32], z1[s, u, :],
                                       start=True, stop=True)
                        w.then_inc(m_pe, 1)
                    for bank, u0 in ((B2, 0), (B3, 16)):
                        for u in range(u0, u0 + 16):
                            w = mm(bank[32:64, (u - u0) * 32:(u - u0 + 1) * 32], z1[0:32, u, :], xf[0:32, u, 0:32],
                                   start=True, stop=True)
                        w.then_inc(m_pe, 1)
                    pe.wait_ge(m_dve, 9 * i + 5)
                    pe.wait_ge(m_act, 9 * i + 5)
                    pe.nop(nofuse=True)
                    for n_, bank in enumerate((B4, B5, B2, B3)):
                        for u in range(8 * n_, 8 * n_ + 8):
                            w = mm(bank[0:64, (u % 8) * 64:(u % 8 + 1) * 64], a_sb[64:128, u // 4, u % 4, 0:64],
                                   mt[64:128, u, 64:128], start=True, stop=True)
                        w.then_inc(m_pe, 1)
                    pe.wait_ge(m_dve, 9 * i + 7)
                    pe.wait_ge(m_act, 9 * i + 7)
                    pe.nop(nofuse=True)
                    for n_, bank in enumerate((B4, B5, B2, B3)):
                        for u in range(8 * n_, 8 * n_ + 8):
                            w = mm(bank[0:64, (u % 8) * 64:(u % 8 + 1) * 64], xf[0:64, u, :], z2[0:64, u, :],
                                   start=True, stop=True)
                        w.then_inc(m_pe, 1)
                    pe.wait_ge(m_dve, 9 * (i + 1))
                    pe.wait_ge(m_act, 9 * (i + 1))

                def recur(i, has_next):
                    pe.wait_ge(s_zero, i + 1)
                    for s in range(TPB):
                        if s:
                            pe.wait_ge(r_s, 6 * i + 2 * s)
                        for c in range(4):
                            b, m = c // 2, c % 2
                            tl = slice((b * TPB + s) * P, (b * TPB + s + 1) * P)
                            w = mm(B2[:, c * P:(c + 1) * P], k_t[:, m, tl], s_bd[:, c, :], start=True, stop=True)
                        w.then_inc(r_p, 1)
                        if s:
                            pe.wait_ge(r_out, 4 * i + s)
                        for c in range(4):
                            b, m = c // 2, c % 2
                            tl = slice((b * TPB + s) * P, (b * TPB + s + 1) * P)
                            w = mm(B4[:, c * P:(c + 1) * P], q_t[:, m, tl], s_bd[:, c, :], start=c == 0, stop=False,
                                   skip_group_check=True)
                        w.then_inc(r_q, 1)
                        if has_next:
                            project(i + 1, s)
                            if s:
                                select(i + 1, s - 1)
                        pe.wait_ge(r_r, 4 * i + s + 1)
                        for c in range(8):
                            b, h = c // 4, c % 4
                            w = mm(B3[:, c * DH:(c + 1) * DH], mt[:, (b * TPB + s) * HEADS + h, :], r_sb[:, b, h, :],
                                   start=True, stop=True)
                        w.then_inc(r_u, 1)
                        pe.wait_ge(r_ub, 4 * i + s + 1)
                        if s < TPB - 1:
                            for c in range(4):
                                b, m = c // 2, c % 2
                                w = mm(B5[:, c * P:(c + 1) * P], k_tok[:, b * TPB + s, m * P:(m + 1) * P],
                                       u_sb[:, b, 2 * m:2 * m + 2, :], start=True, stop=True)
                            w.then_inc(r_sx, 1)
                        for c in range(8):
                            b, h = c // 4, c % 4
                            w = mm(B4[:, c * DH:(c + 1) * DH], at_t[:, b * TPB + s, h, :], u_sb[:, b, h, :],
                                   start=False, stop=c == 7, skip_group_check=True)
                        w.then_inc(r_o, 1)

                def gate(i, b, has_next):
                    half = 2 * i + b
                    pe.wait_ge(st_dve, 7 * (half + 1))
                    for j in range(TPB):
                        w = nc.tensor.transpose(TR[0:STATS, j * P:(j + 1) * P], gst[:, j, :], ident[:])
                    w.then_inc(st_turned, 1)
                    pe.wait_ge(xg_in, 16 * (half + 1))
                    for c in range(HID_CH):
                        if b == 0 and c == 0:
                            pe.wait_ge(taps, 24 * (i + 2) if has_next else 24 * (i + 1))
                        if not (b == 0 and c < 2):
                            pe.wait_ge(gelu_ok, 4 * half + c - 1)
                        for k in range(CH):
                            mm(X[c % 2][:], w1x[:, k, c * P:(c + 1) * P], xg[:, k, :], start=k == 0, stop=False)
                        if c == 0:
                            pe.wait_ge(st_kept, half + 1)
                        mm(X[c % 2][:], w1s[:, c * P:(c + 1) * P], st_t[:], start=False, stop=True).then_inc(gate_mm, 1)
                    pe.wait_ge(gelu_ok, 4 * (half + 1))
                    for j in range(TPB):
                        o = 128 + (b * TPB + j) * 16
                        for c in range(HID_CH):
                            w = mm((B5, SM)[b][:, o:o + 16], hid[:, c, j * P:(j + 1) * P], w2[:, c, :], start=c == 0, stop=c == 3)
                    w.then_inc(logit_mm, 1)

                def output(i, b):
                    half = 2 * i + b
                    pe.wait_ge(mix, 7 * (half + 1))
                    for m in range(CH):
                        for j in range(TPB):
                            w = nc.tensor.transpose((TR, B2)[m][:, j * P:(j + 1) * P], lo[:, b, j, m * P:(m + 1) * P], ident[:])
                        w.then_inc(o_turned, 1)
                    pe.wait_ge(o_kept, 2 * (half + 1))
                    for j in range(TPB):
                        o = (j % 2) * D
                        for m in range(CH):
                            w = mm((B3, B4)[j // 2][:, o:o + D], o_t[:, m, j * P:(j + 1) * P], wo[:, m, :],
                                   start=m == 0, stop=m == 1)
                        if j % 2:
                            w.then_inc(wo_mm, 1)

                def route(i, b):
                    half = 2 * i + b
                    pe.wait_ge(ln, LN * (half + 1))
                    for m in range(CH):
                        for j in range(TPB):
                            w = nc.tensor.transpose((TR, B2)[m][:, j * P:(j + 1) * P], x1[:, b, j, m * P:(m + 1) * P], ident[:])
                        w.then_inc(x1_turned, 1)
                    pe.wait_ge(x1_kept, 2 * (half + 1))
                    for j in range(TPB):
                        o = 256 + (b * TPB + j) * NEXP
                        for m in range(CH):
                            w = mm(B5[:, o:o + NEXP], o_t[:, m, j * P:(j + 1) * P], rw[:, m, :], start=m == 0, stop=m == 1)
                    w.then_inc(rt_mm, 1)
                    pe.wait_ge(rt, RT * half + 7)
                    o = 320 + b * 32
                    mm(B5[:, o:o + 32], before[:], m_bf[:].rearrange("p t e -> p (t e)"), start=True, stop=False,
                       skip_group_check=True)
                    for j in range(TPB - 1):
                        k = TPB - 1 - j
                        mm(B5[:, o + 8 * (j + 1):o + 32].rearrange("p (t e) -> p t e", e=NEXP), ones[:],
                           m_bf[:, j:j + 1, :].to_broadcast([P, k, NEXP]), start=False, stop=False, skip_group_check=True)
                    mm(B5[:, o:o + 32].rearrange("p (t e) -> p t e", e=NEXP), ones[:],
                       m_acc[:].unsqueeze(1).to_broadcast([P, TPB, NEXP]), start=False, stop=True,
                       skip_group_check=True).then_inc(ranked, 1)

                for g in range(4):
                    project(0, g)
                    if g:
                        select(0, g - 1)
                stage1b(0)

                def step(i, has_next):
                    merges(i)
                    recur(i, has_next)
                    if has_next:
                        stage1b(i + 1)
                    for b in range(2):
                        gate(i, b, has_next)
                    for b in range(2):
                        output(i, b)
                        route(i, b)
                step(0, True)
                with pe.Fori(1, PAIRS - 1) as i:
                    step(i, True)
                step(PAIRS - 1, False)

            @block.scalar
            def _(act):
                A = nc.scalar.activation
                act.wait_ge(w_in, 16 * 17)
                A(itemp[:], itemp[:], ACT.Exp).then_inc(act_c, 1)
                act.wait_ge(act_c, 1)
                A(itemp[:], itemp[:], ACT.Ln, bias=1.0).then_inc(act_c, 1)
                A(floor16[:], floor16[:], ACT.Sigmoid).then_inc(act_c, 1)
                act.wait_ge(dve_c, 2)

                def group_a(p, g):
                    gg = g % 4
                    act.wait_ge(projected, 8 * p + g + 1)
                    need(act, raw, 8 * p + g - 1)
                    need(act, squared, 8 * p + g - 1)
                    A(conv[:, g % 2], X[g % 2][:], ACT.Copy, scale=cw[:, g // 4, gg % CH, 3:4]).then_inc(tap3, 1)

                def group_b(p, g):
                    gg = g % 4
                    b, m = gg // CH, gg % CH
                    dst = (kraw if g < 4 else q_t)[:, m, b * SEQ:(b + 1) * SEQ]
                    act.wait_ge(taps, 24 * p + 3 * (g + 1))
                    if g == 0:
                        need(act, k_turned, 4 * p)
                    if g == 4:
                        need(act, r_q, 4 * p)
                        need(act, at_mm, 8 * p)
                    A(dst, conv[:, g % 2], ACT.Silu).then_inc(raw, 1)
                    act.wait_ge(raw, 8 * p + g + 1)
                    need(act, selected, 8 * p + g - 1)
                    A(sq[:, g % 2], dst, ACT.Square).then_inc(squared, 1)

                def stage1b(p):
                    group_b(p, 3)
                    act.wait_ge(beta_mm, p + 1)
                    need(act, beta_ok, 2 * p)
                    A(th[:], SM[:, 64:96], ACT.Tanh, scale=0.5).then_inc(beta_th, 1)
                    group_a(p, 4)
                    group_a(p, 5)
                    act.wait_ge(selected, 8 * p + 4)
                    need(act, rn_ok, 2 * p)
                    A(nrm[:, 0], SM[:, 0:32], ACT.Sqrt, bias=eps6[:, 0:1]).then_inc(rooted, 1)
                    group_b(p, 4)
                    group_b(p, 5)
                    for j in range(4):
                        act.wait_ge(k_back, 4 * p + j + 1)
                        A(k_t[:, j % CH, (j // CH) * SEQ:(j // CH + 1) * SEQ], (B3, B5)[j % 2][:], ACT.Copy).then_inc(kt_kept, 1)
                    group_a(p, 6)
                    group_a(p, 7)
                    group_b(p, 6)
                    group_b(p, 7)
                    act.wait_ge(selected, 8 * p + 8)
                    A(nrm[:, 1], SM[:, 32:64], ACT.Sqrt, bias=eps6[:, 0:1]).then_inc(rooted, 1)

                def merges(i):
                    c = lambda x: x.rearrange("p (u k) -> p u k", k=BLK)
                    c2 = lambda x: x.rearrange("p (u k) -> p u k", k=2 * BLK)
                    act.wait_ge(m_pe, 14 * i + 2)
                    for q in range(2):
                        s = slice(q * 64, q * 64 + 32)
                        A(z1[s, 16:32, :], c(B3[s, :]), ACT.Copy).then_inc(m_act, 1)
                    act.wait_ge(m_pe, 14 * i + 4)
                    for q in range(2):
                        s = slice(q * 64, q * 64 + 32)
                        A(mt[s, 16:32, q * 64 + 32:q * 64 + 64], c(B5[s, :]), ACT.Copy).then_inc(m_act, 1)
                    act.wait_ge(m_pe, 14 * i + 6)
                    A(xf[32:64, 16:32, 0:32], c(B3[32:64, :]), ACT.Copy).then_inc(m_act, 1)
                    act.wait_ge(m_pe, 14 * i + 8)
                    A(z2[0:64, 8:16, :], c2(B5[0:64, :]), ACT.Copy).then_inc(m_act, 1)
                    act.wait_ge(m_pe, 14 * i + 10)
                    A(z2[0:64, 24:32, :], c2(B3[0:64, :]), ACT.Copy).then_inc(m_act, 1)
                    act.wait_ge(m_pe, 14 * i + 12)
                    A(mt[0:64, 8:16, 64:128], c2(B5[0:64, :]), ACT.Copy).then_inc(m_act, 1)
                    act.wait_ge(m_pe, 14 * i + 14)
                    A(mt[0:64, 24:32, 64:128], c2(B3[0:64, :]), ACT.Copy).then_inc(m_act, 1)

                def recur(i, has_next):
                    for s in range(TPB):
                        if has_next:
                            group_a(i + 1, s)
                        act.wait_ge(r_u, 4 * i + s + 1)
                        A(u_sb[:].rearrange("p b h d -> p (b h d)"), B3[:], ACT.Copy).then_inc(r_ub, 1)
                        if has_next and s < 3:
                            group_b(i + 1, s)

                def gate(i, b):
                    half = 2 * i + b
                    act.wait_ge(st_turned, half + 1)
                    need(act, gate_mm, 4 * half)
                    A(st_t[:], TR[0:STATS, :], ACT.Copy).then_inc(st_kept, 1)
                    need(act, logit_mm, half)
                    for c in range(HID_CH):
                        act.wait_ge(gate_mm, 4 * half + c + 1)
                        A(hid[:, c, :], X[c % 2][:], ACT.Gelu, bias=b1[:, c:c + 1]).then_inc(gelu_ok, 1)

                def mixed(i, b):
                    half = 2 * i + b
                    act.wait_ge(sm_dve, 11 * half + 4)
                    A(lg[:], lg[:], ACT.Exp).then_inc(sm_exp, 1)
                    act.wait_ge(mix, 7 * half + 4)
                    A(tmp[:], lo[:, b], ACT.Square).then_inc(sq_ok, 1)
                    act.wait_ge(mix, 7 * half + 5)
                    A(s16[:], s16[:], ACT.Sqrt, bias=eps5[:, 0:1], scale=1.0 / DH).then_inc(rms_rt, 1)

                def finish(i, b):
                    half = 2 * i + b
                    for m in range(CH):
                        act.wait_ge(o_turned, 2 * half + m + 1)
                        if m == 0:
                            need(act, rt_mm, half)
                        A(o_t[:, m, :], (TR, B2)[m][:], ACT.Copy).then_inc(o_kept, 1)
                    act.wait_ge(ln, LN * half + 10)
                    A(rstd[:], mv[:, :, 1], ACT.Sqrt, bias=eps5[:, 0:1]).then_inc(ln_rt, 1)
                    for m in range(CH):
                        act.wait_ge(x1_turned, 2 * half + m + 1)
                        if m == 0:
                            act.wait_ge(wo_mm, 2 * (half + 1))
                        A(o_t[:, m, :], (TR, B2)[m][:], ACT.Copy).then_inc(x1_kept, 1)

                for g in range(4):
                    group_a(0, g)
                    if g < 3:
                        group_b(0, g)
                stage1b(0)

                def step(i, has_next):
                    merges(i)
                    recur(i, has_next)
                    if has_next:
                        stage1b(i + 1)
                    for b in range(2):
                        gate(i, b)
                    for b in range(2):
                        mixed(i, b)
                        finish(i, b)
                step(0, True)
                with act.Fori(1, PAIRS - 1) as i:
                    step(i, True)
                step(PAIRS - 1, False)

            @block.vector
            def _(dve):
                V = nc.vector
                dve.wait_ge(w_in, 16 * 17)
                V.memset(eps6[:], 1e-6).then_inc(dve_c, 1)
                V.memset(eps5[:], 1e-5).then_inc(dve_c, 1)
                V.tensor_scalar(wo[:], wo[:], onw[:, 0:1], None, ALU.mult).then_inc(dve_c, 1)
                dve.wait_ge(pool_c, 6)
                V.tensor_copy(iota8[:], mi8[:, 0, :]).then_inc(dve_c, 1)
                dve.wait_ge(dve_c, 4)
                V.tensor_scalar(base8[:], iota8[:], float(CAP), None, ALU.mult).then_inc(dve_c, 1)
                dve.wait_ge(act_c, 3)
                V.tensor_scalar(floor16[:], floor16[:], 0.05, None, ALU.mult).then_inc(dve_c, 1)
                V.tensor_scalar(itemp[:], itemp[:], 1e-4, None, ALU.add).then_inc(dve_c, 1)
                dve.wait_ge(dve_c, 7)
                V.reciprocal(itemp[:], itemp[:]).then_inc(dve_c, 1)
                dve.wait_ge(pool_c, POOL_C + 2)

                def taps_of(p, g):
                    gg = g % 4
                    dve.wait_ge(tap3, 8 * p + g + 1)
                    for k in range(1, TAPS):
                        need(dve, taps, 24 * p + 3 * g + k - 1)
                        V.scalar_tensor_tensor(conv[:, g % 2, k:], X[g % 2][:, :SEQ - k],
                                               cw[:, g // 4, gg % CH, 3 - k:4 - k], conv[:, g % 2, k:],
                                               ALU.mult, ALU.add).then_inc(taps, 1)

                def norm(p, kq):
                    dve.wait_ge(rooted, 2 * p + kq + 1)
                    V.reciprocal(rn[:, kq], nrm[:, kq]).then_inc(rn_ok, 1)

                def stage1b(p):
                    taps_of(p, 4)
                    dve.wait_ge(beta_th, p + 1)
                    V.tensor_scalar(beta[:].rearrange("p t h -> p (t h)"), th[:], 0.5, 0.5, ALU.mult, ALU.add).then_inc(beta_ok, 1)
                    V.tensor_scalar(nbeta[:].rearrange("p t h -> p (t h)"), th[:], -0.5, -0.5, ALU.mult, ALU.add).then_inc(beta_ok, 1)
                    norm(p, 0)
                    taps_of(p, 5)
                    dve.wait_ge(rn_ok, 2 * p + 1)
                    for j in range(4):
                        b, m = j // CH, j % CH
                        dve.wait_ge(k_turned, 4 * p + j + 1)
                        r = rn[:, 0].rearrange("p (t h) -> p t h", h=HEADS)[:, b * TPB:(b + 1) * TPB, 2 * m:2 * m + 2]
                        V.tensor_tensor(
                            k_tok[:, b * TPB:(b + 1) * TPB, m * P:(m + 1) * P].rearrange("p t (h d) -> p t h d", d=DH),
                            (TR, B2)[j % 2][:].rearrange("p (t h d) -> p t h d", h=2, d=DH),
                            r.unsqueeze(3).to_broadcast([P, TPB, 2, DH]), ALU.mult).then_inc(k_kept, 1)
                    taps_of(p, 6)
                    taps_of(p, 7)
                    dve.wait_ge(beta_ok, 2 * (p + 1))
                    for n_ in range(PT):
                        jj, par = n_ // 2, n_ % 2
                        ts = slice(2 * jj, 2 * jj + 2)
                        dve.wait_ge(a_mm, 8 * p + n_ + 1)
                        if n_ == 0:
                            need(dve, m_pe, 14 * p)
                        V.tensor_tensor(a_sb[:, ts, par::2, :],
                                        (B2, B3, B4, B5)[n_ % 4][:].rearrange("p (t m s) -> p t m s", t=2, m=2),
                                        nbeta[:, ts, par::2].unsqueeze(3).to_broadcast([P, 2, 2, P]),
                                        ALU.mult).then_inc(a_kept, 1)
                    for n_ in range(PT):
                        jj, par = n_ // 2, n_ % 2
                        dve.wait_ge(at_mm, 8 * p + n_ + 1)
                        V.tensor_tensor(at_t[:, 2 * jj:2 * jj + 2, par::2, :],
                                        (B2, B3, B4, B5)[n_ % 4][:].rearrange("p (t m s) -> p t m s", t=2, m=2),
                                        upper[:].unsqueeze(1).unsqueeze(1).to_broadcast([P, 2, 2, P]),
                                        ALU.mult).then_inc(at_kept, 1)
                    norm(p, 1)

                def merges(i):
                    c = lambda x: x.rearrange("p (u k) -> p u k", k=BLK)
                    c2 = lambda x: x.rearrange("p (u k) -> p u k", k=2 * BLK)
                    cp = V.tensor_copy
                    dve.wait_ge(m_pe, 14 * i + 1)
                    for q in range(2):
                        s = slice(q * 64, q * 64 + 32)
                        cp(z1[s, 0:16, :], c(B2[s, :])).then_inc(m_dve, 1)
                    dve.wait_ge(m_pe, 14 * i + 3)
                    for q in range(2):
                        s = slice(q * 64, q * 64 + 32)
                        cp(mt[s, 0:16, q * 64 + 32:q * 64 + 64], c(B4[s, :])).then_inc(m_dve, 1)
                    dve.wait_ge(m_pe, 14 * i + 5)
                    cp(xf[32:64, 0:16, 0:32], c(B2[32:64, :])).then_inc(m_dve, 1)
                    dve.wait_ge(m_pe, 14 * i + 7)
                    cp(z2[0:64, 0:8, :], c2(B4[0:64, :])).then_inc(m_dve, 1)
                    dve.wait_ge(m_pe, 14 * i + 9)
                    cp(z2[0:64, 16:24, :], c2(B2[0:64, :])).then_inc(m_dve, 1)
                    dve.wait_ge(m_pe, 14 * i + 11)
                    cp(mt[0:64, 0:8, 64:128], c2(B4[0:64, :])).then_inc(m_dve, 1)
                    dve.wait_ge(m_pe, 14 * i + 13)
                    cp(mt[0:64, 16:24, 64:128], c2(B2[0:64, :])).then_inc(m_dve, 1)

                def recur(i, has_next):
                    vv = v_tok[:].rearrange("p (b t) c -> p b t c", t=TPB)
                    bb = beta[:].rearrange("p (b t) h -> p b t h", t=TPB)
                    qn = rn[:, 1].rearrange("p (b t h) -> p b t h", t=TPB, h=HEADS)
                    dl = delta[:].rearrange("p (b t) c -> p b t c", t=TPB)
                    dve.wait_ge(v_in, 16 * (i + 1))
                    dve.wait_ge(rn_ok, 2 * (i + 1))
                    for s in range(TPB):
                        dve.wait_ge(r_p, 4 * i + s + 1)
                        V.tensor_tensor(r_sb[:].rearrange("p b h d -> p b (h d)"), vv[:, :, s, :],
                                        B2[:].rearrange("p (b c) -> p b c", b=2), ALU.subtract).then_inc(r_r1, 1)
                        dve.wait_ge(r_r1, 4 * i + s + 1)
                        V.tensor_tensor(r_sb[:], r_sb[:], bb[:, :, s, :].unsqueeze(3).to_broadcast([P, 2, HEADS, DH]),
                                        ALU.mult).then_inc(r_r, 1)
                        if has_next:
                            taps_of(i + 1, s)
                        if s < TPB - 1:
                            dve.wait_ge(r_sx, 3 * i + s + 1)
                            dve.wait_ge(r_q, 4 * i + s + 1)
                            for q in range(2):
                                hs = slice(q * DH, (q + 1) * DH)
                                V.tensor_tensor(s_bd[hs, :, hs], s_bd[hs, :, hs],
                                                B5[hs, :].rearrange("p (c d) -> p c d", d=P)[:, :, hs],
                                                ALU.add).then_inc(r_s, 1)
                        dve.wait_ge(r_o, 4 * i + s + 1)
                        V.tensor_tensor(dl[:, :, s, :].rearrange("p b (h d) -> p b h d", d=DH),
                                        B4[:].rearrange("p (b h d) -> p b h d", h=HEADS, d=DH),
                                        qn[:, :, s, :].unsqueeze(3).to_broadcast([P, 2, HEADS, DH]),
                                        ALU.mult).then_inc(r_out, 1)

                def stats(i, b):
                    half = 2 * i + b
                    dve.wait_ge(sl_in[b], 32 * (i + 1))
                    dve.wait_ge(r_out, 4 * (i + 1))
                    ts = lambda x: x[:, b * TPB:(b + 1) * TPB]
                    for k, src in enumerate((sh[:, b], lo[:, b], ts(delta), ts(v_tok))):
                        for j in range(TPB):
                            for h in range(HEADS):
                                w = V.bn_stats(bn[:, j, k, h, :], src[:, j, h * DH:(h + 1) * DH])
                    w.then_inc(st_dve, 1)
                    f = bn[:].rearrange("p t k h s -> p t (k h) s")
                    g = gst[:].rearrange("p t (a s) -> p t a s", s=2)
                    c = 7 * half
                    dve.wait_ge(st_dve, c + 1)
                    need(dve, st_turned, half)
                    V.tensor_tensor(g[:, :, :, 0], f[:, :, :, 1], f[:, :, :, 4], ALU.add).then_inc(st_dve, 1)
                    V.tensor_tensor(dm[:], f[:, :, :, 1], f[:, :, :, 4], ALU.subtract).then_inc(st_dve, 1)
                    V.tensor_tensor(g[:, :, :, 1], f[:, :, :, 2], f[:, :, :, 5], ALU.add).then_inc(st_dve, 1)
                    dve.wait_ge(st_dve, c + 4)
                    V.scalar_tensor_tensor(dm[:], dm[:], 0.25, dm[:], ALU.mult, ALU.mult).then_inc(st_dve, 1)
                    V.tensor_scalar(g[:, :, :, 0], g[:, :, :, 0], 0.5, None, ALU.mult).then_inc(st_dve, 1)
                    dve.wait_ge(st_dve, c + 6)
                    V.scalar_tensor_tensor(g[:, :, :, 1], g[:, :, :, 1], 1.0 / DH, dm[:], ALU.mult,
                                           ALU.add).then_inc(st_dve, 1)

                def softmax(i, b):
                    half = 2 * i + b
                    c = 11 * half
                    t4 = lambda x: x[:].rearrange("p (t h) k -> p t h k", h=HEADS)
                    t16 = lambda x: x[:].rearrange("p (t h) k -> p t (h k)", h=HEADS)
                    g3 = [P, 16, PATHS]
                    dve.wait_ge(logit_mm, half + 1)
                    need(dve, mixp, 3 * half)
                    V.tensor_tensor(t16(lg), (B5, SM)[b][:, 128 + 64 * b:192 + 64 * b].rearrange("p (t k) -> p t k", t=TPB),
                                    bias16[:].unsqueeze(1).to_broadcast([P, TPB, 16]), ALU.add).then_inc(sm_dve, 1)
                    dve.wait_ge(sm_dve, c + 1)
                    V.tensor_tensor(t4(lg), t4(lg), itemp[:].unsqueeze(1).unsqueeze(3).to_broadcast([P, TPB, HEADS, PATHS]),
                                    ALU.mult).then_inc(sm_dve, 1)
                    dve.wait_ge(sm_dve, c + 2)
                    V.tensor_reduce(s16[:], lg[:], AX.X, ALU.max).then_inc(sm_dve, 1)
                    dve.wait_ge(sm_dve, c + 3)
                    V.tensor_tensor(lg[:], lg[:], s16[:].unsqueeze(2).to_broadcast(g3), ALU.subtract).then_inc(sm_dve, 1)
                    dve.wait_ge(sm_exp, half + 1)
                    V.tensor_reduce(s16[:], lg[:], AX.X, ALU.add).then_inc(sm_dve, 1)
                    dve.wait_ge(sm_dve, c + 5)
                    V.reciprocal(r16[:], s16[:]).then_inc(sm_dve, 1)
                    dve.wait_ge(sm_dve, c + 6)
                    V.tensor_tensor(lg[:], lg[:], r16[:].unsqueeze(2).to_broadcast(g3), ALU.mult).then_inc(sm_dve, 1)
                    dve.wait_ge(sm_dve, c + 7)
                    V.tensor_tensor(t16(lg), t16(lg), floor16[:].unsqueeze(1).to_broadcast([P, TPB, 16]),
                                    ALU.max).then_inc(sm_dve, 1)
                    dve.wait_ge(sm_dve, c + 8)
                    V.tensor_reduce(s16[:], lg[:], AX.X, ALU.add).then_inc(sm_dve, 1)
                    dve.wait_ge(sm_dve, c + 9)
                    V.reciprocal(r16[:], s16[:]).then_inc(sm_dve, 1)
                    dve.wait_ge(sm_dve, c + 10)
                    V.tensor_tensor(lg[:], lg[:], r16[:].unsqueeze(2).to_broadcast(g3), ALU.mult).then_inc(sm_dve, 1)

                def mixed(i, b):
                    half = 2 * i + b
                    c = 7 * half
                    v3 = lambda x: x.rearrange("p t (h d) -> p (t h) d", d=DH)
                    p3 = lambda k: lg[:, :, k:k + 1].to_broadcast([P, 16, DH])
                    dlt = delta[:, b * TPB:(b + 1) * TPB]
                    dve.wait_ge(sm_dve, 11 * (half + 1))
                    V.tensor_tensor(v3(lo[:, b]), v3(lo[:, b]), p3(1), ALU.mult).then_inc(mix, 1)
                    V.tensor_tensor(v3(dlt), v3(dlt), p3(2), ALU.mult).then_inc(mix, 1)
                    dve.wait_ge(mix, c + 2)
                    V.tensor_tensor(lo[:, b], lo[:, b], dlt, ALU.add).then_inc(mix, 1)
                    dve.wait_ge(mix, c + 3)
                    dve.wait_ge(mixp, 3 * (half + 1))
                    V.tensor_tensor(lo[:, b], lo[:, b], sh[:, b], ALU.add).then_inc(mix, 1)
                    dve.wait_ge(sq_ok, half + 1)
                    V.tensor_reduce(s16[:], v3(tmp[:]), AX.X, ALU.add).then_inc(mix, 1)
                    dve.wait_ge(rms_rt, half + 1)
                    V.reciprocal(r16[:], s16[:]).then_inc(mix, 1)
                    dve.wait_ge(mix, c + 6)
                    V.tensor_tensor(v3(lo[:, b]), v3(lo[:, b]), r16[:].unsqueeze(2).to_broadcast([P, 16, DH]),
                                    ALU.mult).then_inc(mix, 1)

                def norm1(i, b):
                    half = 2 * i + b
                    c = LN * half
                    dve.wait_ge(x_in[b], 16 * (i + 1))
                    for j in range(2):
                        dve.wait_ge(wo_mm, 2 * half + j + 1)
                        V.tensor_tensor(x1[:, b, 2 * j:2 * j + 2], x1[:, b, 2 * j:2 * j + 2],
                                        (B3, B4)[j][:].rearrange("p (t c) -> p t c", c=D), ALU.add).then_inc(ln, 1)
                    dve.wait_ge(ln, c + 2)
                    for j in range(TPB):
                        V.bn_stats(lbn[:, j], x1[:, b, j]).then_inc(ln, 1)
                    for j in range(TPB):
                        dve.wait_ge(ln, c + 3 + j)
                        dve.nop(nofuse=True)
                        V.bn_aggr(mv[:, j], lbn[:, j]).then_inc(ln, 1)
                    dve.wait_ge(ln_rt, half + 1)
                    V.reciprocal(rstd[:], rstd[:]).then_inc(ln, 1)
                    dve.wait_ge(ln, c + 11)
                    for j in range(TPB):
                        V.tensor_scalar(x1[:, b, j], x1[:, b, j], mv[:, j, 0:1], rstd[:, j:j + 1], ALU.subtract,
                                        ALU.mult).then_inc(ln, 1)

                def route(i, b):
                    half = 2 * i + b
                    c = RT * half
                    at = bass.ds(i * (PT * TOPK) + b * TPB * TOPK, TPB * TOPK)
                    dve.wait_ge(rt_mm, half + 1)
                    V.tensor_tensor(rl[:], B5[:, 256 + 32 * b:288 + 32 * b].rearrange("p (t e) -> p t e", e=NEXP),
                                    rb[:].unsqueeze(1).to_broadcast([P, TPB, NEXP]), ALU.add).then_inc(rt, 1)
                    dve.wait_ge(rt, c + 1)
                    dve.nop(nofuse=True)
                    for j in range(TPB):
                        w = V.max(mx8[:, j], rl[:, j])
                    w.then_inc(rt, 1)
                    dve.wait_ge(rt, c + 2)
                    dve.nop(nofuse=True)
                    for j in range(TPB):
                        w = V.max_index(mi8[:, j], mx8[:, j], rl[:, j])
                    w.then_inc(rt, 1)
                    dve.wait_ge(rt, c + 3)
                    dve.nop(nofuse=True)
                    V.tensor_copy(ef[:].rearrange("p (t k) -> p t k", k=TOPK), mi8[:, :, 0:TOPK]).then_inc(rt, 1)
                    V.tensor_copy(top2[:, at].rearrange("p (t k) -> p t k", k=TOPK), mx8[:, :, 0:TOPK]).then_inc(rt, 1)
                    dve.wait_ge(rt, c + 4)
                    V.tensor_tensor(oh[:], ef[:].unsqueeze(2).to_broadcast([P, TPB * TOPK, NEXP]),
                                    iota8[:].unsqueeze(1).to_broadcast([P, TPB * TOPK, NEXP]), ALU.is_equal).then_inc(rt, 1)
                    dve.wait_ge(rt, c + 6)
                    o4 = oh[:].rearrange("p (t k) e -> p t k e", k=TOPK)
                    V.tensor_tensor(m_bf[:], o4[:, :, 0, :], o4[:, :, 1, :], ALU.add).then_inc(rt, 1)
                    dve.wait_ge(ranked, half + 1)
                    V.tensor_tensor(rk[:], B5[:, 320 + 32 * b:352 + 32 * b].rearrange("p (t e) -> p t e", e=NEXP),
                                    base8[:].unsqueeze(1).to_broadcast([P, TPB, NEXP]), ALU.add).then_inc(rt, 1)
                    dve.wait_ge(rt, c + 8)
                    V.tensor_tensor(o4, o4, rk[:].unsqueeze(2).to_broadcast([P, TPB, TOPK, NEXP]), ALU.mult).then_inc(rt, 1)
                    dve.wait_ge(rt, c + 9)
                    V.tensor_reduce(slotf[:, at], oh[:], AX.X, ALU.add).then_inc(rt, 1)
                    dve.wait_ge(rt, c + 10)
                    dve.nop(nofuse=True)
                    V.tensor_copy(slot_u[:, b], slotf[:, at]).then_inc(rt, 1)
                    V.tensor_reduce(m_sum[:], m_bf[:].rearrange("p t e -> p e t"), AX.X, ALU.add).then_inc(rt, 1)
                    dve.wait_ge(rt, c + 12)
                    V.tensor_tensor(m_acc[:], m_acc[:], m_sum[:], ALU.add).then_inc(rt, 1)
                    V.tensor_copy(eidx[:, at], ef[:]).then_inc(rt, 1)

                for g in range(4):
                    taps_of(0, g)
                stage1b(0)

                def step(i, has_next):
                    merges(i)
                    recur(i, has_next)
                    if has_next:
                        stage1b(i + 1)
                    for b in range(2):
                        stats(i, b)
                    for b in range(2):
                        softmax(i, b)
                        mixed(i, b)
                        norm1(i, b)
                        route(i, b)
                step(0, True)
                with dve.Fori(1, PAIRS - 1) as i:
                    step(i, True)
                step(PAIRS - 1, False)


EXTRA = NEXP
NMOE = TOKENS * TOPK // P + EXTRA
SPARE = NEXP * CAP
GU = 2 * D


def experts_and_combine(nc, t, keep):
    with ExitStack() as ctx:
        def sb(name, shape, dt=F32):
            return ctx.enter_context(nc.sbuf_tensor("C_" + name, shape, dt))

        def ps(name):
            return ctx.enter_context(nc.psum_tensor("C_ps_" + name, [P, 512], F32))

        def sem(name):
            return ctx.enter_context(nc.semaphore("C_" + name))

        eidx, slotf, top2, m_acc = keep["eidx"], keep["slotf"], keep["top2"], keep["m_acc"]
        wgu = sb("wgu", [P, NEXP, CH, GU]); wd = sb("wd", [P, NEXP, CH, D])
        ident = sb("ident", [P, P]); ones = sb("ones", [P, P], BF16); zero = sb("zero", [P, D])
        i8 = sb("i8", [P, NEXP], I32); it = sb("it", [P, NMOE], I32); i64 = sb("i64", [P, TILES], I32)
        ip = sb("ip", [P, 1], I32)
        f8 = sb("f8", [P, NEXP]); ft = sb("ft", [P, NMOE]); f64 = sb("f64", [P, TILES]); fp = sb("fp", [P, 1])
        cnt = sb("cnt", [P, NEXP]); gt = sb("gt", [P, NEXP, TILES]); tiles = sb("tiles", [P, NEXP])
        below = sb("below", [P, NEXP, NEXP]); tbase = sb("tbase", [P, NEXP]); tend = sb("tend", [P, NEXP])
        ge = sb("ge", [P, NMOE, NEXP]); ex = sb("ex", [P, NMOE]); tb = sb("tb", [P, NMOE])
        xrow = sb("xrow", [P, NMOE]); xrow_i = sb("xrow_i", [P, NMOE], I32); ex_i = sb("ex_i", [P, NMOE], I32)
        pad = sb("pad", [P, NEXP]); pad_u = sb("pad_u", [P, NEXP], U32)
        oh = sb("oh", [P, TILES * TOPK, NEXP]); off = sb("off", [P, NEXP])
        yr = sb("yr", [P, TILES * TOPK]); yr_u = sb("yr_u", [P, TILES * TOPK], U32)
        ev = sb("ev", [P, TILES]); wts = sb("wts", [P, TILES, TOPK]); den = sb("den", [P, TILES])
        xb = sb("xb", [P, 2, D]); xt = sb("xt", [P, 2, CH, P]); sg = sb("sg", [P, 2, D]); av = sb("av", [P, 2, D])
        avt = sb("avt", [P, 2, CH, P]); yb = sb("yb", [P, 2, D])
        G4 = 4
        gy = sb("gy", [P, 2, G4 * TOPK, D]); gx = sb("gx", [P, 2, G4, D])
        now = sb("now", [P, 2, G4 * TOPK], U32)
        lbn = sb("lbn", [P, 2, G4, 6]); mv = sb("mv", [P, 2, G4, 2]); rstd = sb("rstd", [P, 2, G4])
        eps = sb("eps", [P, 1])
        ps_x = [ps(f"x{i}") for i in range(2)]; ps_g = [ps(f"g{i}") for i in range(2)]
        ps_a = [ps(f"a{i}") for i in range(2)]; ps_y = [ps(f"y{i}") for i in range(2)]

        w_in, pool_c, idx, counted = sem("weights_in"), sem("pool_const"), sem("tables"), sem("counted")
        tiles_ok, pads_ok, gap_ok, rows_ok = sem("tiles_ok"), sem("pads_ok"), sem("gap_ok"), sem("rows_ok")
        exps, zeroed = sem("gate_exp"), sem("pads_zeroed")
        x_in = [sem(f"x_in{i}") for i in range(2)]; y_out = [sem(f"y_out{i}") for i in range(2)]
        x_turned, x_kept, gu_mm, silu_ok, act_ok = (sem(n) for n in ("x_turned", "x_kept", "gu_mm", "silu_ok", "act_ok"))
        a_turned, a_kept, y_mm, y_kept = (sem(n) for n in ("a_turned", "a_kept", "y_mm", "y_kept"))
        gy_in = [sem(f"gy_in{i}") for i in range(2)]; gx_in = [sem(f"gx_in{i}") for i in range(2)]
        now_ok = sem("now_ok")
        fin, rooted = sem("final_dve"), sem("final_rooted")
        out_ok = [sem(f"out{i}") for i in range(2)]
        groups = TILES // G4
        FIN = 5 * G4 + 1
        xs = t["xs_d"]
        tok = lambda n: t[n].rearrange("(t p) c -> p t c", p=P)

        with nc.Block() as block:
            @block.sync
            def _(sp):
                for name, lo_ in (("we_gate", 0), ("we_up", D)):
                    for e in range(NEXP):
                        sp.dma_start(wgu[:, e, :, lo_:lo_ + D], t[name][e].rearrange("(c p) n -> p c n", p=P)).then_inc(w_in, 16)
                for e in range(NEXP):
                    sp.dma_start(wd[:, e], t["we_down"][e].rearrange("(c p) n -> p c n", p=P)).then_inc(w_in, 16)
                sp.wait_ge(tiles_ok, 2)
                sp.wait_ge(zeroed, 16 * (NEXP + EXTRA))

                def load(j, u):
                    hold(sp, x_turned, j - 1)
                    row = sp.value_load(xrow_i[0:1, bass.ds(j, 1)], min_val=0, max_val=SPARE + (EXTRA - 1) * P)
                    sp.dma_start(xb[:, u], xs[bass.ds(row, P), :]).then_inc(x_in[u], 16)
                load(0, 0)
                load(1, 1)
                with sp.Fori(1, NMOE // 2) as i:
                    for u in range(2):
                        load(2 * i + u, u)

                def group(g, u):
                    if not isinstance(g, int) or g > 1:
                        hold(sp, out_ok[u], 8 * (g - u))
                    sp.dma_start(gx[:, u], tok("x1_d")[:, bass.ds(g * G4, G4), :]).then_inc(gx_in[u], 16)

                def store(g, u):
                    hold(sp, fin, FIN * (g + 1))
                    sp.dma_start(tok("out")[:, bass.ds(g * G4, G4), :], gx[:, u]).then_inc(out_ok[u], 16)
                group(0, 0)
                group(1, 1)
                with sp.Fori(0, groups // 2 - 1) as i:
                    for u in range(2):
                        store(2 * i + u, u)
                        group(2 * i + u + 2, u)
                for u in range(2):
                    store(groups - 2 + u, u)
                for u in range(2):
                    sp.wait_ge(out_ok[u], 16 * groups // 2)

            @block.gpsimd
            def _(pool):
                pool.memset(ident[:], 0.0).then_inc(pool_c, 1)
                pool.memset(ones[:], 1.0).then_inc(pool_c, 1)
                pool.memset(zero[:], 0.0).then_inc(pool_c, 1)
                pool.iota(i8[:], [[1, NEXP]], base=0, channel_multiplier=0).then_inc(pool_c, 1)
                pool.iota(it[:], [[1, NMOE]], base=0, channel_multiplier=0).then_inc(pool_c, 1)
                pool.iota(i64[:], [[P, TILES]], base=0, channel_multiplier=0).then_inc(pool_c, 1)
                pool.iota(ip[:], [[0, 1]], base=0, channel_multiplier=1).then_inc(pool_c, 1)
                pool.wait_ge(pool_c, 7)
                pool.affine_select(out=ident[:], in_=ident[:], compare_op=ALU.not_equal, fill=1.0, base=0,
                                   pattern=[[-1, P]], channel_multiplier=1).then_inc(pool_c, 1)
                for k in range(EXTRA):
                    pool.dma_start(xs[SPARE + k * P:SPARE + (k + 1) * P, :], zero[:]).then_inc(zeroed, 16)
                pool.wait_ge(pads_ok, 1)
                for e in range(NEXP):
                    pool.indirect_dma_start(xs[:, :], bass.IndirectOffsetOnAxis(ap=pad_u[:, e:e + 1], axis=0),
                                            zero[:], None).then_inc(zeroed, 16)

                def store(j, u):
                    hold(pool, y_kept, j + 1)
                    pool.dma_start(t["y_d"][bass.ds(j * P, P), :], yb[:, u]).then_inc(y_out[u], 16)
                with pool.Fori(0, NMOE // 2) as i:
                    for u in range(2):
                        store(2 * i + u, u)
                for u in range(2):
                    pool.wait_ge(y_out[u], 16 * NMOE // 2)
                pool.wait_ge(rows_ok, 1)

                def gather(g, u):
                    if not isinstance(g, int) or g > 1:
                        hold(pool, fin, FIN * (g - 1))
                    pool.tensor_copy(now[:, u], yr_u[:, bass.ds(g * (G4 * TOPK), G4 * TOPK)]).then_inc(now_ok, 1)
                    hold(pool, now_ok, g + 1)
                    for c in range(G4 * TOPK):
                        pool.indirect_dma_start(gy[:, u, c, :], None, t["y_d"][:, :], bass.IndirectOffsetOnAxis(
                            ap=now[:, u, c:c + 1], axis=0)).then_inc(gy_in[u], 16)
                gather(0, 0)
                gather(1, 1)
                with pool.Fori(1, groups // 2) as i:
                    for u in range(2):
                        gather(2 * i + u, u)

            @block.tensor
            def _(pe):
                mm = nc.tensor.matmul
                pe.wait_ge(pool_c, 8)
                mm(ps_y[0][:, 0:NEXP], ones[:], m_acc[:], start=True, stop=True).then_inc(counted, 1)
                pe.wait_ge(w_in, 16 * 3 * NEXP)
                pe.wait_ge(tiles_ok, 2)

                def turn_x(j, u):
                    pe.wait_ge(x_in[u], 8 * (j - u) + 16)
                    need(pe, x_kept, j - 1)
                    for c in range(CH):
                        w = nc.tensor.transpose(ps_x[u][:, c * P:(c + 1) * P], xb[:, u, c * P:(c + 1) * P], ident[:])
                    w.then_inc(x_turned, 1)

                def expert(j):
                    return pe.value_load(ex_i[0:1, bass.ds(j, 1)], min_val=0, max_val=NEXP - 1)

                def gate_up(j, u):
                    e = expert(j)
                    pe.wait_ge(x_kept, j + 1)
                    need(pe, act_ok, j - 1)
                    for c in range(CH):
                        w = mm(ps_g[u][:], xt[:, u, c, :], wgu[:, bass.ds(e, 1), c, :], start=c == 0, stop=c == CH - 1)
                    w.then_inc(gu_mm, 1)

                def turn_act(j, u):
                    pe.wait_ge(act_ok, j + 1)
                    need(pe, a_kept, j - 1)
                    for c in range(CH):
                        w = nc.tensor.transpose(ps_a[u][:, c * P:(c + 1) * P], av[:, u, c * P:(c + 1) * P], ident[:])
                    w.then_inc(a_turned, 1)

                def down(j, u):
                    e = expert(j)
                    pe.wait_ge(a_kept, j + 1)
                    need(pe, y_kept, j - 1)
                    for c in range(CH):
                        w = mm(ps_y[u][:, 0:D], avt[:, u, c, :], wd[:, bass.ds(e, 1), c, :], start=c == 0, stop=c == CH - 1)
                    w.then_inc(y_mm, 1)
                turn_x(0, 0)
                turn_x(1, 1)
                gate_up(0, 0)

                def step(j, u):
                    turn_x(j + 1, 1 - u)
                    turn_act(j - 1, 1 - u)
                    gate_up(j, u)
                    down(j - 1, 1 - u)
                step(1, 1)
                step(2, 0)
                with pe.Fori(1, NMOE // 2 - 1) as i:
                    step(2 * i + 1, 1)
                    step(2 * i + 2, 0)
                j = NMOE - 1
                turn_act(j - 1, 0)
                gate_up(j, 1)
                down(j - 1, 0)
                turn_act(j, 1)
                down(j, 1)

            @block.scalar
            def _(act):
                A = nc.scalar.activation
                act.wait_ge(gap_ok, 1)
                A(ev[:], ev[:], ACT.Exp).then_inc(exps, 1)

                def keep_x(j, u):
                    act.wait_ge(x_turned, j + 1)
                    need(act, gu_mm, j - 1)
                    A(xt[:, u].rearrange("p c n -> p (c n)"), ps_x[u][:, 0:D], ACT.Copy).then_inc(x_kept, 1)

                def silu(j, u):
                    act.wait_ge(gu_mm, j + 1)
                    need(act, act_ok, j - 1)
                    A(sg[:, u], ps_g[u][:, 0:D], ACT.Silu).then_inc(silu_ok, 1)

                def keep_y(j, u):
                    act.wait_ge(y_mm, j + 1)
                    if not isinstance(j, int) or j > 1:
                        act.wait_ge(y_out[u], 8 * (j - u))
                    A(yb[:, u], ps_y[u][:, 0:D], ACT.Copy).then_inc(y_kept, 1)

                def step(j, u):
                    keep_x(j + 1, 1 - u)
                    silu(j, u)
                    keep_y(j - 1, 1 - u)
                keep_x(0, 0)
                keep_x(1, 1)
                silu(0, 0)
                step(1, 1)
                step(2, 0)
                with act.Fori(1, NMOE // 2 - 1) as i:
                    step(2 * i + 1, 1)
                    step(2 * i + 2, 0)
                j = NMOE - 1
                silu(j, 1)
                keep_y(j - 1, 0)
                keep_y(j, 1)

                def root(g, u):
                    act.wait_ge(fin, FIN * g + 4 * G4)
                    A(rstd[:, u], mv[:, u, :, 1], ACT.Sqrt, bias=eps[:, 0:1]).then_inc(rooted, 1)
                root(0, 0)
                root(1, 1)
                with act.Fori(1, groups // 2) as i:
                    for u in range(2):
                        root(2 * i + u, u)

            @block.vector
            def _(dve):
                V = nc.vector
                count = [0]

                def then(ins):
                    ins.then_inc(idx, 1)
                    count[0] += 1
                    dve.wait_ge(idx, count[0])
                dve.wait_ge(pool_c, 7)
                bc = lambda x, d, shape: x.unsqueeze(d).to_broadcast(shape)
                V.memset(eps[:], 1e-5).then_inc(idx, 1)
                V.tensor_copy(f8[:], i8[:]).then_inc(idx, 1)
                V.tensor_copy(ft[:], it[:]).then_inc(idx, 1)
                V.tensor_copy(f64[:], i64[:]).then_inc(idx, 1)
                V.tensor_copy(fp[:], ip[:]).then_inc(idx, 1)
                count[0] = 5
                dve.wait_ge(counted, 1)
                then(V.tensor_copy(cnt[:], ps_y[0][:, 0:NEXP]))
                then(V.scalar_tensor_tensor(pad[:], f8[:], float(CAP), cnt[:], ALU.mult, ALU.add))
                V.tensor_scalar(pad_u[:], pad[:], fp[:, 0:1], None, ALU.add).then_inc(pads_ok, 1)
                s = [P, NEXP, TILES]
                then(V.tensor_tensor(gt[:], bc(cnt[:], 2, s), bc(f64[:], 1, s), ALU.is_gt))
                then(V.tensor_reduce(tiles[:], gt[:], AX.X, ALU.add))
                s = [P, NEXP, NEXP]
                then(V.tensor_tensor(below[:], bc(f8[:], 2, s), bc(f8[:], 1, s), ALU.is_gt))
                then(V.tensor_tensor(below[:], below[:], bc(tiles[:], 1, s), ALU.mult))
                then(V.tensor_reduce(tbase[:], below[:], AX.X, ALU.add))
                then(V.tensor_tensor(tend[:], tbase[:], tiles[:], ALU.add))
                s = [P, NMOE, NEXP]
                then(V.tensor_tensor(ge[:], bc(ft[:], 2, s), bc(tend[:], 1, s), ALU.is_ge))
                then(V.tensor_reduce(ex[:], ge[:], AX.X, ALU.add))
                V.tensor_scalar(ex_i[:], ex[:], float(NEXP - 1), None, ALU.min).then_inc(tiles_ok, 1)
                then(V.tensor_tensor(ge[:], ge[:], bc(tiles[:], 1, s), ALU.mult))
                then(V.tensor_reduce(tb[:], ge[:], AX.X, ALU.add))
                then(V.tensor_tensor(tb[:], ft[:], tb[:], ALU.subtract))
                then(V.tensor_scalar(xrow[:], ex[:], float(CAP), None, ALU.mult))
                V.scalar_tensor_tensor(xrow_i[:], tb[:], float(P), xrow[:], ALU.mult, ALU.add).then_inc(tiles_ok, 1)
                t2 = top2[:].rearrange("p (t k) -> p t k", k=TOPK)
                V.tensor_tensor(ev[:], t2[:, :, 1], t2[:, :, 0], ALU.subtract).then_inc(gap_ok, 1)
                then(V.tensor_scalar(off[:], f8[:], -float(CAP), None, ALU.mult))
                then(V.scalar_tensor_tensor(off[:], tbase[:], float(P), off[:], ALU.mult, ALU.add))
                s = [P, TILES * TOPK, NEXP]
                then(V.tensor_tensor(oh[:], bc(eidx[:], 2, s), bc(f8[:], 1, s), ALU.is_equal))
                then(V.tensor_tensor(oh[:], oh[:], bc(off[:], 1, s), ALU.mult))
                then(V.tensor_reduce(yr[:], oh[:], AX.X, ALU.add))
                V.tensor_tensor(yr_u[:], yr[:], slotf[:], ALU.add).then_inc(rows_ok, 1)
                dve.wait_ge(exps, 1)
                then(V.tensor_scalar(den[:], ev[:], 1.0, None, ALU.add))
                then(V.reciprocal(den[:], den[:]))
                then(V.tensor_copy(wts[:, :, 0], den[:]))
                then(V.tensor_tensor(wts[:, :, 1], ev[:], den[:], ALU.mult))

                def gated(j, u):
                    dve.wait_ge(silu_ok, j + 1)
                    need(dve, a_turned, j - 1)
                    V.tensor_tensor(av[:, u], sg[:, u], ps_g[u][:, D:GU], ALU.mult).then_inc(act_ok, 1)

                def keep_a(j, u):
                    dve.wait_ge(a_turned, j + 1)
                    need(dve, y_mm, j - 1)
                    V.tensor_copy(avt[:, u].rearrange("p c n -> p (c n)"), ps_a[u][:, 0:D]).then_inc(a_kept, 1)
                gated(0, 0)

                def step(j, u):
                    keep_a(j - 1, 1 - u)
                    gated(j, u)
                step(1, 1)
                step(2, 0)
                with dve.Fori(1, NMOE // 2 - 1) as i:
                    step(2 * i + 1, 1)
                    step(2 * i + 2, 0)
                step(NMOE - 1, 1)
                keep_a(NMOE - 1, 1)

                def combine(g, u):
                    c = FIN * g
                    wt = wts[:].rearrange("p t k -> p (t k)")
                    dve.wait_ge(gy_in[u], 64 * (g - u) + 128)
                    dve.wait_ge(gx_in[u], 8 * (g - u) + 16)
                    for k in range(TOPK):
                        if k:
                            dve.wait_ge(fin, c + G4)
                        for j in range(G4):
                            V.scalar_tensor_tensor(gx[:, u, j], gy[:, u, j * TOPK + k],
                                                   wt[:, bass.ds(g * (G4 * TOPK) + j * TOPK + k, 1)], gx[:, u, j],
                                                   ALU.mult, ALU.add).then_inc(fin, 1)
                    for j in range(G4):
                        dve.wait_ge(fin, c + G4 + j + 1)
                        V.bn_stats(lbn[:, u, j], gx[:, u, j]).then_inc(fin, 1)
                    for j in range(G4):
                        hold(dve, fin, c + 2 * G4 + j + 1)
                        V.bn_aggr(mv[:, u, j], lbn[:, u, j]).then_inc(fin, 1)

                def combined(g, u):
                    c = FIN * g
                    dve.wait_ge(rooted, g + 1)
                    V.reciprocal(rstd[:, u], rstd[:, u]).then_inc(fin, 1)
                    dve.wait_ge(fin, c + 4 * G4 + 1)
                    for j in range(G4):
                        V.tensor_scalar(gx[:, u, j], gx[:, u, j], mv[:, u, j, 0:1], rstd[:, u, j:j + 1],
                                        ALU.subtract, ALU.mult).then_inc(fin, 1)

                def both(g, u):
                    combine(g, u)
                    combined(g, u)
                both(0, 0)
                both(1, 1)
                with dve.Fori(1, groups // 2) as i:
                    for u in range(2):
                        both(2 * i + u, u)


def post_norm_layer(nc, t):
    t = dict(t)
    for name, shape in (
        ("v_d", (TOKENS, D)), ("short_d", (TOKENS, D)), ("long_d", (TOKENS, D)), ("x1_d", (TOKENS, D)),
        ("scr_a", (NBLK, BLK, UNITS, BLK)), ("scr_x", (P, BLK, BLK)), ("scr_xt", (P, BLK, BLK)),
        ("xs_d", (SPARE + EXTRA * P, D)), ("y_d", (NMOE * P, D)),
    ):
        t[name] = nc.dram_tensor(name, shape, F32, kind="Internal").ap()
    with ExitStack() as ctx:
        def sb(name, shape, dt=F32):
            return ctx.enter_context(nc.sbuf_tensor(name, shape, dt))
        keep = {"eidx": sb("eidx", [P, TILES * TOPK]), "slotf": sb("slotf", [P, TILES * TOPK]),
                "top2": sb("top2", [P, TILES * TOPK]), "m_acc": sb("m_acc", [P, NEXP], BF16)}
        conv_and_fir(nc, t)
        delta_and_gate(nc, t, keep)
        experts_and_combine(nc, t, keep)


def kernel(**inputs):
    import numpy as np
    import concourse.bacc as bacc
    from concourse.bass_utils import run_bass_kernel_spmd

    def arr(name):
        return np.asarray(inputs[name])

    def turned(name):
        return np.ascontiguousarray(arr(name).T)
    x = np.ascontiguousarray(arr("L0_attn_hidden_states").reshape(TOKENS, D))
    fir_long = np.zeros((D, FPAD), x.dtype)
    fir_long[:, P - 1:P - 1 + FIR] = arr("L0_attn_fir_long_w").reshape(D, FIR)[:, ::-1]
    arrays = {
        "x": x, "xT": np.ascontiguousarray(x.T),
        "WqT": turned("L0_attn_Wq"), "WkT": turned("L0_attn_Wk"), "WvT": turned("L0_attn_Wv"),
        "WbT": turned("L0_attn_Wb"), "WoT": turned("L0_attn_Wo"),
        "qconv": arr("L0_attn_qconv_w"), "kconv": arr("L0_attn_kconv_w"), "vconv": arr("L0_attn_vconv_w"),
        "fir_short": np.ascontiguousarray(arr("L0_attn_fir_short_w").reshape(D, SHORT)), "fir_long": fir_long,
        "w1T": turned("L0_attn_gate_w1"), "w2T": turned("L0_attn_gate_w2"),
        "b1": np.ascontiguousarray(arr("L0_attn_gate_b1").reshape(HID_CH, P).T),
        "bias": np.ascontiguousarray(arr("L0_attn_base_bias").reshape(-1)),
        "floor": np.ascontiguousarray(arr("L0_attn_floor_raw").reshape(-1)),
        "log_temp": arr("L0_attn_log_temp"), "onorm": arr("L0_attn_onorm_w"),
        "rw": arr("L0_ffn_router_w"), "rb": arr("L0_ffn_router_b"),
        "we_gate": arr("L0_ffn_we_gate"), "we_up": arr("L0_ffn_we_up"), "we_down": arr("L0_ffn_we_down"),
    }
    nc = bacc.Bacc("TRN2", target_bir_lowering=False, num_devices=1)
    t = {name: nc.dram_tensor(name, a.shape, mybir.dt.from_np(a.dtype), kind="ExternalInput").ap()
         for name, a in arrays.items()}
    t["out"] = nc.dram_tensor("out", (TOKENS, D), F32, kind="ExternalOutput").ap()
    post_norm_layer(nc, t)
    r = run_bass_kernel_spmd(nc, [arrays], core_ids=[0])
    return r.results[0]["out"].reshape(BATCH, SEQ, D)
```

```python
from contextlib import ExitStack

import concourse.bass as bass
from concourse import mybir

F32 = mybir.dt.float32
BF16 = mybir.dt.bfloat16
U32 = mybir.dt.uint32
I32 = mybir.dt.int32
ALU = mybir.AluOpType
ACT = mybir.ActivationFunctionType
AX = mybir.AxisListType

P = 128
BATCH, SEQ, D = 16, 512, 256
HEADS, DH = 4, 64
TOKENS = BATCH * SEQ
TILES = TOKENS // P
TPB = SEQ // P
CH = D // P
PAIRS = BATCH // 2
PT = 2 * TPB
PTOK = 2 * SEQ
FIR = 63
SHORT = 3
TAPS = 4
FPAD = 320
OCT = 8


def need(eng, sem, value):
    if isinstance(value, int) and value <= 0:
        return
    eng.wait_ge(sem, value)


def hold(eng, sem, value):
    need(eng, sem, value)
    if not isinstance(value, int):
        eng.nop(nofuse=True)


def back(it, g, k, per):
    q = g - k
    n = 0
    while q < 0:
        q += per
        n += 1
    return (it - n if n else it), q


def conv_and_fir(nc, t):
    UN = 4
    STEPS = BATCH // UN
    TB = 4
    OPC = P // OCT
    LAG_TURN, LAG_KEEP, LAG_FLIP, LAG_LONG, LAG_STORE = 3, 4, 5, 6, 5
    with ExitStack() as ctx:
        def sb(name, shape, dt=F32):
            return ctx.enter_context(nc.sbuf_tensor("A_" + name, shape, dt))

        def ps(name, shape):
            return ctx.enter_context(nc.psum_tensor("A_ps_" + name, shape, F32))

        def sem(name):
            return ctx.enter_context(nc.semaphore("A_" + name))

        v_back = sb("v_back", [P, TILES, D])
        long_sb = sb("long", [P, TILES, D])
        toep = sb("toep", [P, TB, OCT, 192])
        x_t = sb("x", [P, 2, CH, SEQ])
        wv = sb("wv", [P, CH, D])
        cw = sb("cw", [P, CH, TAPS])
        fw = sb("fw", [P, CH, SHORT])
        ident = sb("ident", [P, P])
        flip = sb("flip", [P, P])
        conv = sb("conv", [P, UN, SEQ])
        v_t = sb("v_t", [P, UN, SEQ])
        sh_t = sb("sh_t", [P, UN, SEQ])
        mid = sb("mid", [P, SEQ - 1])
        v_tok = sb("v_tok", [P, 2, TPB, P])
        sh_tok = sb("sh_tok", [P, 2, TPB, P])
        ps_x = [ps(f"x{i}", [P, SEQ]) for i in range(2)]
        ps_v = ps("v", [P, TPB, P])
        ps_r = ps("back", [P, TPB, P])
        ps_s = ps("short", [P, TPB, P])
        ps_f = [ps(f"f{i}", [P, OCT, TILES]) for i in range(2)]

        weights_in = sem("weights_in")
        x_in = [sem(f"x_in{i}") for i in range(2)]
        toep_in = [sem(f"toep_in{i}") for i in range(TB)]
        zeroed, ident_ok = sem("zeroed"), sem("ident_ok")
        projected = sem("projected")
        tap3 = sem("tap3")
        taps = sem("taps")
        v_ready = sem("v_ready")
        sh_start = sem("sh_start")
        sh_prod = sem("sh_prod")
        sh_mid = sem("sh_mid")
        sh_ready = sem("sh_ready")
        v_turned, sh_turned = sem("v_turned"), sem("sh_turned")
        v_kept, sh_kept = sem("v_kept"), sem("sh_kept")
        flipped = sem("flipped")
        back_kept = sem("back_kept")
        stored = [sem(f"stored{i}") for i in range(2)]
        fir_done = sem("fir_done")
        long_kept = [sem(f"long_kept{i}") for i in range(2)]
        long_out = sem("long_out")

        tok = lambda n: t[n].rearrange("(t p) c -> p t c", p=P)
        windows = bass.AP(t["fir_long"].tensor, 0, [[1, P], [FPAD, D], [1, 192]])

        def slots(eng, m, body, lag):
            for g in range(2 * UN):
                body(STEPS * m + g // UN, g % UN, lambda k, g=g: g >= k)
            with eng.Fori(STEPS * m + 2, STEPS * (m + 1)) as p:
                for g in range(UN):
                    body(p, g, lambda k: True)
            for g in range(lag):
                body(STEPS * (m + 1) + g // UN, g % UN, lambda k, g=g: k > g)

        with nc.Block() as block:
            @block.sync
            def _(sp):
                sp.dma_start(wv[:], t["WvT"].rearrange("(c p) n -> p c n", p=P)).then_inc(weights_in, 16)
                sp.dma_start(cw[:], t["vconv"].rearrange("(c p) k -> p c k", p=P)).then_inc(weights_in, 16)
                sp.dma_start(fw[:], t["fir_short"].rearrange("(c p) k -> p c k", p=P)).then_inc(weights_in, 16)
                xd = t["xT"].rearrange("(c p) n -> p c n", p=P)

                def chunk(m):
                    def slot(p, g, has):
                        if has(0):
                            need(sp, projected, UN * p + g - 1)
                            seq = (p - STEPS * m) * UN + g
                            sp.dma_start(x_t[:, g % 2], xd[:, :, bass.ds(seq * SEQ, SEQ)]).then_inc(x_in[g % 2], 16)
                        if has(LAG_STORE):
                            q, h = back(p, g, LAG_STORE, UN)
                            n = UN * q + h
                            rows = bass.ds(((q - STEPS * m) * UN + h) * TPB, TPB)
                            cols = slice(m * P, (m + 1) * P)
                            sp.wait_ge(v_kept, n + 1)
                            sp.dma_start(tok("v_d")[:, rows, cols], v_tok[:, h % 2]).then_inc(stored[h % 2], 16)
                            sp.wait_ge(sh_kept, n + 1)
                            sp.dma_start(tok("short_d")[:, rows, cols], sh_tok[:, h % 2]).then_inc(stored[h % 2], 16)
                    slots(sp, m, slot, LAG_STORE)
                for m in range(CH):
                    chunk(m)

                def store_long(c0, c1, pieces):
                    for k in long_kept:
                        sp.wait_ge(k, c1 // OCT // 2)
                    for q in range(pieces):
                        rows = slice(q * TILES // pieces, (q + 1) * TILES // pieces)
                        sp.dma_start(tok("long_d")[:, rows, c0:c1], long_sb[:, rows, c0:c1]).then_inc(long_out, 16)
                store_long(0, P, 4)
                store_long(P, P + P // 2, 2)
                store_long(P + P // 2, D, 2)
                sp.wait_ge(long_out, 16 * 8)
                for k in stored:
                    sp.wait_ge(k, 32 * BATCH)

            @block.gpsimd
            def _(pool):
                def load_toep(o, u):
                    pool.dma_start(toep[:, u], windows[:, bass.ds(o * OCT, OCT), :]).then_inc(toep_in[u], 16)
                pool.memset(ident[:], 0.0).then_inc(zeroed, 1)
                pool.memset(flip[:], 0.0).then_inc(zeroed, 1)
                pool.wait_ge(zeroed, 2)
                pool.affine_select(out=ident[:], in_=ident[:], compare_op=ALU.not_equal, fill=1.0, base=0,
                                   pattern=[[-1, P]], channel_multiplier=1).then_inc(ident_ok, 1)
                pool.affine_select(out=flip[:], in_=flip[:], compare_op=ALU.not_equal, fill=1.0, base=1 - P,
                                   pattern=[[1, P]], channel_multiplier=1).then_inc(ident_ok, 1)
                for u in range(TB):
                    load_toep(u, u)
                pool.wait_ge(weights_in, 48)

                def chunk(m):
                    def slot(p, g, has):
                        if has(0):
                            n = UN * p + g
                            pool.wait_ge(sh_start, n + 1)
                            need(pool, sh_mid, n)
                            pool.tensor_tensor(mid[:], v_t[:, g, :SEQ - 1],
                                               fw[:, m, 1:2].to_broadcast([P, SEQ - 1]), ALU.mult).then_inc(sh_prod, 1)
                            pool.wait_ge(sh_prod, n + 1)
                            pool.tensor_tensor(sh_t[:, g, 1:], sh_t[:, g, 1:], mid[:], ALU.add).then_inc(sh_mid, 1)
                        if m and has(1):
                            q, h = back(p, g, 1, UN)
                            o = (q - STEPS) * UN + h
                            hold(pool, fir_done, o + 1)
                            load_toep(o + TB, h)
                    slots(pool, m, slot, 1 if m else 0)
                for m in range(CH):
                    chunk(m)
                with pool.Fori(OPC // TB, D // OCT // TB - 1) as k:
                    for u in range(TB):
                        hold(pool, fir_done, TB * k + u + 1)
                        load_toep(TB * (k + 1) + u, u)

            @block.tensor
            def _(pe):
                pe.wait_ge(weights_in, 48)
                pe.wait_ge(ident_ok, 2)
                byseq = v_back[:].rearrange("p (b t) c -> p b t c", t=TPB)

                def octet(k, u):
                    o = TB * k + u
                    pe.wait_ge(toep_in[u], 16 * (k + 1))
                    need(pe, long_kept[u % 2], TB // 2 * k + u // 2)
                    for c in range(OCT):
                        ch = o * OCT + c
                        nc.tensor.matmul(ps_f[u % 2][:, c, :], toep[:, u, c, 0:P],
                                         v_back[:, :, bass.ds(ch, 1)], start=True, stop=True)
                        out = ps_f[u % 2][0:64, c, :].rearrange("p (b t) -> p b t", t=TPB)[:, :, 1:TPB]
                        mm = nc.tensor.matmul(out, toep[:, u, c, P:192],
                                              byseq[:, :, 0:TPB - 1, bass.ds(ch, 1)], start=False, stop=True,
                                              skip_group_check=True)
                    mm.then_inc(fir_done, 1)

                def chunk(m):
                    def slot(p, g, has):
                        if has(0):
                            n = UN * p + g
                            pe.wait_ge(x_in[g % 2], 16 * (UN // 2 * p + g // 2 + 1))
                            need(pe, taps, 3 * (n - 1))
                            for c in range(CH):
                                mm = nc.tensor.matmul(ps_x[g % 2][:], wv[:, c, m * P:(m + 1) * P],
                                                      x_t[:, g % 2, c, :], start=c == 0, stop=c == CH - 1)
                            mm.then_inc(projected, 1)
                        if has(LAG_TURN):
                            q, h = back(p, g, LAG_TURN, UN)
                            n = UN * q + h
                            pe.wait_ge(v_ready, n + 1)
                            need(pe, v_kept, n)
                            for j in range(TPB):
                                mm = nc.tensor.transpose(ps_v[:, j, :], v_t[:, h, j * P:(j + 1) * P], ident[:])
                            mm.then_inc(v_turned, 1)
                            pe.wait_ge(sh_ready, n + 1)
                            need(pe, sh_kept, n)
                            for j in range(TPB):
                                mm = nc.tensor.transpose(ps_s[:, j, :], sh_t[:, h, j * P:(j + 1) * P], ident[:])
                            mm.then_inc(sh_turned, 1)
                        if has(LAG_FLIP):
                            q, h = back(p, g, LAG_FLIP, UN)
                            n = UN * q + h
                            pe.wait_ge(v_kept, n + 1)
                            need(pe, back_kept, n)
                            nc.tensor.matmul(ps_r[:], flip[:], v_tok[:, h % 2], start=True,
                                             stop=True).then_inc(flipped, 1)
                        if m and has(0):
                            octet(p - STEPS, g)
                    slots(pe, m, slot, LAG_FLIP)
                    pe.wait_ge(back_kept, BATCH * (m + 1))
                for m in range(CH):
                    chunk(m)
                with pe.Fori(OPC // TB, D // OCT // TB) as k:
                    for u in range(TB):
                        octet(k, u)

            def keep_long(eng, copy, k, u):
                o = TB * k + u
                eng.wait_ge(fir_done, o + 1)
                copy(long_sb[:, :, bass.ds(o * OCT, OCT)],
                     ps_f[u % 2][:].rearrange("p c t -> p t c")).then_inc(long_kept[u % 2], 1)

            @block.scalar
            def _(act):
                A = nc.scalar.activation
                act.wait_ge(weights_in, 48)

                def copy(out, in_):
                    return A(out, in_, ACT.Copy)

                def chunk(m):
                    def slot(p, g, has):
                        if has(LAG_KEEP):
                            q, h = back(p, g, LAG_KEEP, UN)
                            n = UN * q + h
                            act.wait_ge(v_turned, n + 1)
                            need(act, flipped, n - 1)
                            need(act, stored[h % 2], 32 * (UN // 2 * q + h // 2))
                            A(v_tok[:, h % 2], ps_v[:], ACT.Copy).then_inc(v_kept, 1)
                            act.wait_ge(sh_turned, n + 1)
                            A(sh_tok[:, h % 2], ps_s[:], ACT.Copy).then_inc(sh_kept, 1)
                        if has(0):
                            n = UN * p + g
                            act.wait_ge(projected, n + 1)
                            need(act, v_ready, n - UN + 1)
                            A(conv[:, g], ps_x[g % 2][:], ACT.Copy, scale=cw[:, m, 3:4]).then_inc(tap3, 1)
                        if has(1):
                            q, h = back(p, g, 1, UN)
                            n = UN * q + h
                            act.wait_ge(taps, 3 * (n + 1))
                            need(act, v_turned, n - UN + 1)
                            need(act, sh_turned, n - UN + 1)
                            A(v_t[:, h], conv[:, h], ACT.Silu).then_inc(v_ready, 1)
                            act.wait_ge(v_ready, n + 1)
                            A(sh_t[:, h], v_t[:, h], ACT.Copy, scale=fw[:, m, 2:3]).then_inc(sh_start, 1)
                        if m and has(1):
                            q, h = back(p, g, 1, UN)
                            if h % 2:
                                keep_long(act, copy, q - STEPS, h)
                    slots(act, m, slot, LAG_KEEP)
                for m in range(CH):
                    chunk(m)
                with act.Fori(OPC // TB, D // OCT // TB) as k:
                    for u in range(1, TB, 2):
                        keep_long(act, copy, k, u)

            @block.vector
            def _(dve):
                dve.wait_ge(weights_in, 48)

                def chunk(m):
                    def slot(p, g, has):
                        if has(LAG_LONG):
                            q, h = back(p, g, LAG_LONG, UN)
                            dve.wait_ge(flipped, UN * q + h + 1)
                            rows = bass.ds(((q - STEPS * m) * UN + h) * TPB, TPB)
                            nc.vector.tensor_copy(v_back[:, rows, m * P:(m + 1) * P], ps_r[:]).then_inc(back_kept, 1)
                        if has(2):
                            q, h = back(p, g, 2, UN)
                            dve.wait_ge(sh_mid, UN * q + h + 1)
                            nc.vector.scalar_tensor_tensor(
                                sh_t[:, h, 2:], v_t[:, h, :SEQ - 2], fw[:, m, 0:1], sh_t[:, h, 2:],
                                ALU.mult, ALU.add).then_inc(sh_ready, 1)
                        if has(0):
                            n = UN * p + g
                            dve.wait_ge(tap3, n + 1)
                            for k in range(1, TAPS):
                                need(dve, taps, 3 * n + k - 1)
                                nc.vector.scalar_tensor_tensor(
                                    conv[:, g, k:], ps_x[g % 2][:, :SEQ - k], cw[:, m, 3 - k:4 - k],
                                    conv[:, g, k:], ALU.mult, ALU.add).then_inc(taps, 1)
                        if m and has(1):
                            q, h = back(p, g, 1, UN)
                            if h % 2 == 0:
                                keep_long(dve, nc.vector.tensor_copy, q - STEPS, h)
                    slots(dve, m, slot, LAG_LONG)
                for m in range(CH):
                    chunk(m)
                with dve.Fori(OPC // TB, D // OCT // TB) as k:
                    for u in range(0, TB, 2):
                        keep_long(dve, nc.vector.tensor_copy, k, u)


NEXP, TOPK = 8, 2
CAP = TOKENS + P
GATE_HID = 512
STATS = 32
PATHS = 4
HID_CH = GATE_HID // P
BLK = 32
NBLK = P // BLK
UNITS = PT * HEADS


def delta_and_gate(nc, t, keep):
    with ExitStack() as ctx:
        def sb(name, shape, dt=F32):
            return ctx.enter_context(nc.sbuf_tensor("B_" + name, shape, dt))

        def ps(name, shape=(P, 512)):
            return ctx.enter_context(nc.psum_tensor("B_ps_" + name, list(shape), F32))

        def sem(name):
            return ctx.enter_context(nc.semaphore("B_" + name))

        wq = sb("wq", [P, CH, D]); wk = sb("wk", [P, CH, D]); wb = sb("wb", [P, CH, HEADS])
        cw = sb("cw", [P, 2, CH, TAPS])
        w1x = sb("w1x", [P, CH, GATE_HID]); w1s = sb("w1s", [STATS, GATE_HID])
        b1 = sb("b1", [P, HID_CH]); w2 = sb("w2", [P, HID_CH, HEADS * PATHS])
        wo = sb("wo", [P, CH, D]); onw = sb("onw", [P, 1])
        rw = sb("rw", [P, CH, NEXP]); rb = sb("rb", [P, NEXP])
        bias16 = sb("bias16", [P, 16]); floor16 = sb("floor16", [P, 16]); itemp = sb("itemp", [P, HEADS])
        ident = sb("ident", [P, P]); upper = sb("upper", [P, P])
        before = sb("before", [P, P], BF16); ones = sb("ones", [P, P], BF16)
        headsel = sb("headsel", [P, 2]); iota8 = sb("iota8", [P, NEXP]); base8 = sb("base8", [P, NEXP])
        eps6 = sb("eps6", [P, 1]); eps5 = sb("eps5", [P, 1])
        xa = sb("xa", [P, CH, PTOK])
        conv = sb("conv", [P, 2, SEQ]); sq = sb("sq", [P, 2, SEQ])
        kraw = sb("kraw", [P, CH, PTOK]); k_t = sb("k_t", [P, CH, PTOK]); q_t = sb("q_t", [P, CH, PTOK])
        k_tok = sb("k_tok", [P, PT, D])
        nrm = sb("nrm", [P, 2, PT * HEADS]); rn = sb("rn", [P, 2, PT * HEADS])
        th = sb("th", [P, PT * HEADS]); beta = sb("beta", [P, PT, HEADS]); nbeta = sb("nbeta", [P, PT, HEADS])
        a_sb = sb("a_sb", [P, PT, HEADS, P])
        at_t = sb("at_t", [P, PT, HEADS, P])
        z = sb("z", [P, BLK, BLK]); zt = sb("zt", [P, BLK, BLK])
        xf = sb("xf", [P, UNITS, 2 * BLK]); mt = sb("mt", [P, UNITS, P])
        s_bd = sb("s_bd", [P, 4, P])
        r_sb = sb("r_sb", [P, 2, HEADS, DH]); u_sb = sb("u_sb", [P, 2, HEADS, DH])
        v_tok = sb("v_tok", [P, PT, D]); delta = sb("delta", [P, PT, D])
        xg = sb("xg", [P, CH, SEQ])
        sh = sb("sh", [P, 2, TPB, D]); lo = sb("lo", [P, 2, TPB, D]); x1 = sb("x1", [P, 2, TPB, D])
        hid = sb("hid", [P, HID_CH, SEQ])
        bnst = sb("bn", [P, PT, PATHS, HEADS, 6]); dm = sb("dm", [P, PT, STATS // 2]); gst = sb("gst", [P, PT, STATS])
        st_t = sb("st_t", [STATS, SEQ])
        lg = sb("lg", [P, UNITS, PATHS]); s32 = sb("s32", [P, UNITS]); r32 = sb("r32", [P, UNITS])
        o_t = sb("o_t", [P, 2, CH, SEQ])
        lbn = sb("lbn", [P, PT, 6]); mv = sb("mv", [P, PT, 2]); rstd = sb("rstd", [P, PT])
        rl = sb("rl", [P, PT, NEXP]); mx8 = sb("mx8", [P, PT, 8]); mi8 = sb("mi8", [P, PT, 8], U32)
        ef = sb("ef", [P, PT * TOPK]); oh = sb("oh", [P, PT * TOPK, NEXP])
        m_bf = sb("m_bf", [P, PT, NEXP], BF16); m_sum = sb("m_sum", [P, NEXP])
        rk = sb("rk", [P, PT, NEXP]); slot_u = sb("slot_u", [P, PT * TOPK], U32)
        z1 = conv[:].rearrange("p c (a b) -> p (c a) b", b=BLK)
        tmp = kraw[:, 0, :].rearrange("p (t c) -> p t c", c=D)
        squares = sq[:].rearrange("p c (a b) -> p (c a) b", b=D)
        z2 = hid[:].rearrange("p c (a b) -> p (c a) b", b=2 * BLK)

        X = [ps("x0"), ps("x1")]
        B2, B3, B4, B5, SM, TR = (ps(n) for n in ("b2", "b3", "b4", "b5", "small", "turn"))

        w_in = sem("weights_in"); pool_c = sem("pool_const"); dve_c = sem("dve_const"); act_c = sem("act_const")
        xa_in, xg_in = sem("xa_in"), sem("xg_in")
        v_in = sem("v_in")
        sl_in = [sem(f"short_long_in{i}") for i in range(2)]; x_in = [sem(f"x_in{i}") for i in range(2)]
        projected, tap3, taps, raw = sem("projected"), sem("tap3"), sem("taps"), sem("silu_done")
        squared, selected = sem("squared"), sem("selected")
        beta_mm, beta_th, beta_ok = sem("beta_mm"), sem("beta_th"), sem("beta_ok")
        rooted, rn_ok = sem("norm_rooted"), sem("norm_ok")
        k_turned, k_kept, k_back, kt_kept = sem("k_turned"), sem("k_kept"), sem("k_back"), sem("kt_kept")
        a_mm, a_kept, at_mm, at_kept = sem("a_mm"), sem("a_kept"), sem("at_mm"), sem("at_kept")
        a_out, z_in, masked, solve, zt_ok = sem("a_out"), sem("z_in"), sem("z_masked"), sem("solve"), sem("zt_ok")
        x_out, x_back = sem("x_out"), sem("x_back")
        m_pe, m_dve, m_act = sem("merge_pe"), sem("merge_dve"), sem("merge_act")
        s_zero, r_p, r_q, r_r1, r_r, r_u, r_ub = (sem(n) for n in (
            "s_zero", "rec_p", "rec_q", "rec_r1", "rec_r", "rec_u", "rec_ub"))
        r_sx, r_s, r_o, r_out = sem("rec_sx"), sem("rec_s"), sem("rec_o"), sem("rec_out")
        st_dve, st_turned, st_kept = sem("stats_dve"), sem("stats_turned"), sem("stats_kept")
        gate_mm, gelu_ok, logit_mm = sem("gate_mm"), sem("gelu_ok"), sem("logit_mm")
        sm_dve, sm_exp = sem("softmax_dve"), sem("softmax_exp")
        mixp, mix = sem("mix_pool"), [sem(f"mix_dve{i}") for i in range(2)]
        sq_ok, rms_rt = sem("rms_squared"), sem("rms_rooted")
        o_turned, o_kept, wo_mm = sem("o_turned"), sem("o_kept"), sem("wo_mm")
        ln, ln_rt = sem("ln_dve"), sem("ln_rooted")
        x1_turned, x1_kept, rt_mm = sem("x1_turned"), sem("x1_kept"), sem("router_mm")
        rt, ranked = sem("route_dve"), sem("ranked")
        scattered = [sem(f"scattered{i}") for i in range(2)]; x1_out = [sem(f"x1_out{i}") for i in range(2)]

        xd = t["xT"].rearrange("(c p) n -> p c n", p=P)
        tok = lambda n: t[n].rearrange("(t p) c -> p t c", p=P)
        POOL_C = 12
        SOLVE = 2 * (BLK - 2)
        LN, RT = 8, 14
        tails = (TR, B3)
        eidx, slotf, top2, m_acc = keep["eidx"], keep["slotf"], keep["top2"], keep["m_acc"]

        def hp(h):
            return slice((h % 2) * DH, (h % 2 + 1) * DH)

        with nc.Block() as block:
            @block.sync
            def _(sp):
                bc = lambda name, n: t[name].rearrange("(o n) -> o n", o=1).to_broadcast([P, n])
                rows = lambda name: t[name].rearrange("(c p) n -> p c n", p=P)
                for dst, src in (
                    (wq[:], rows("WqT")), (wk[:], rows("WkT")), (wb[:], rows("WbT")),
                    (cw[:, 0], rows("kconv")), (cw[:, 1], rows("qconv")),
                    (w1x[:], t["w1T"][0:D, :].rearrange("(c p) n -> p c n", p=P)), (w1s[:], t["w1T"][D:D + STATS, :]),
                    (b1[:], t["b1"]), (w2[:], rows("w2T")), (wo[:], rows("WoT")),
                    (onw[0:DH, :], t["onorm"].rearrange("(p o) -> p o", o=1)),
                    (onw[DH:P, :], t["onorm"].rearrange("(p o) -> p o", o=1)),
                    (rw[:], rows("rw")), (rb[:], bc("rb", NEXP)), (bias16[:], bc("bias", 16)),
                    (floor16[:], bc("floor", 16)), (itemp[:], bc("log_temp", HEADS)),
                ):
                    sp.dma_start(dst, src).then_inc(w_in, 16)

                def load_xa(p):
                    hold(sp, beta_mm, p)
                    hold(sp, projected, 8 * p)
                    sp.dma_start(xa[:], xd[:, :, bass.ds(p * PTOK, PTOK)]).then_inc(xa_in, 16)

                def load_paths(i):
                    hold(sp, o_turned, 4 * i)
                    for b in range(2):
                        r = bass.ds(i * PT + b * TPB, TPB)
                        sp.dma_start(sh[:, b], tok("short_d")[:, r, :]).then_inc(sl_in[b], 16)
                        sp.dma_start(lo[:, b], tok("long_d")[:, r, :]).then_inc(sl_in[b], 16)

                def load_x1(i):
                    for b in range(2):
                        hold(sp, scattered[b], 16 * 8 * i)
                        hold(sp, x1_out[b], 16 * i)
                        r = bass.ds(i * PT + b * TPB, TPB)
                        sp.dma_start(x1[:, b], tok("x")[:, r, :]).then_inc(x_in[b], 16)

                def load_xg(i, b):
                    hold(sp, gate_mm, 4 * (2 * i + b))
                    sp.dma_start(xg[:], xd[:, :, bass.ds(i * PTOK + b * SEQ, SEQ)]).then_inc(xg_in, 16)

                def load_v(i):
                    hold(sp, mixp, 6 * i)
                    hold(sp, st_dve, 7 * i)
                    sp.dma_start(v_tok[:], tok("v_d")[:, bass.ds(i * PT, PT), :]).then_inc(v_in, 16)

                def solve_dmas(p):
                    hold(sp, a_kept, 8 * (p + 1))
                    for k in range(NBLK):
                        s = slice(k * BLK, (k + 1) * BLK)
                        sp.dma_start(t["scr_a"][k], a_sb[s, :, :, s].rearrange("i t h k -> i (t h) k")).then_inc(a_out, 16)
                    hold(sp, a_out, 64 * (p + 1))
                    for k in range(NBLK):
                        sp.dma_start(z[k * BLK:(k + 1) * BLK], t["scr_a"][k].rearrange("i u k -> u i k")).then_inc(z_in, 16)

                def solved_dmas(p):
                    hold(sp, zt_ok, p + 1)
                    sp.dma_start(t["scr_x"][:], z[:]).then_inc(x_out, 16)
                    sp.dma_start(t["scr_xt"][:], zt[:]).then_inc(x_out, 16)
                    hold(sp, x_out, 32 * (p + 1))
                    for k in range(NBLK):
                        s = slice(k * BLK, (k + 1) * BLK)
                        c = (k % 2) * BLK
                        sp.dma_start(xf[s, :, c:c + BLK], t["scr_x"][s].rearrange("u i k -> i u k")).then_inc(x_back, 16)
                        sp.dma_start(mt[s, :, s], t["scr_xt"][s].rearrange("u k i -> k u i")).then_inc(x_back, 16)

                def store_x1(i):
                    hold(sp, ln, LN * (i + 1))
                    for b in range(2):
                        sp.dma_start(tok("x1_d")[:, bass.ds(i * PT + b * TPB, TPB), :], x1[:, b]).then_inc(x1_out[b], 16)

                load_xa(0)
                load_v(0)
                load_paths(0)
                solve_dmas(0)
                solved_dmas(0)
                load_xa(1)

                def step(i, has_prev, has_next, has_after):
                    load_xg(i, 0)
                    if has_prev:
                        store_x1(i - 1)
                    if has_next:
                        solve_dmas(i + 1)
                    load_xg(i, 1)
                    if has_next:
                        solved_dmas(i + 1)
                    if has_after:
                        load_xa(i + 2)
                    if has_next:
                        load_v(i + 1)
                    load_x1(i)
                    if has_next:
                        load_paths(i + 1)
                step(0, False, True, True)
                with sp.Fori(1, PAIRS - 2) as i:
                    step(i, True, True, True)
                step(PAIRS - 2, True, True, False)
                step(PAIRS - 1, True, False, False)
                store_x1(PAIRS - 1)
                for b in range(2):
                    hold(sp, x1_out[b], 16 * PAIRS)

            @block.gpsimd
            def _(pool):
                pool.memset(ident[:], 0.0).then_inc(pool_c, 1)
                pool.memset(upper[:], 1.0).then_inc(pool_c, 1)
                pool.memset(before[:], 1.0).then_inc(pool_c, 1)
                pool.memset(ones[:], 1.0).then_inc(pool_c, 1)
                pool.memset(headsel[:], 1.0).then_inc(pool_c, 1)
                pool.iota(mi8[:, 0, :], [[1, NEXP]], base=0, channel_multiplier=0).then_inc(pool_c, 1)
                pool.wait_ge(pool_c, 6)
                pool.affine_select(out=ident[:], in_=ident[:], compare_op=ALU.not_equal, fill=1.0, base=0,
                                   pattern=[[-1, P]], channel_multiplier=1).then_inc(pool_c, 1)
                pool.affine_select(out=upper[:], in_=upper[:], compare_op=ALU.is_ge, fill=0.0, base=0,
                                   pattern=[[1, P]], channel_multiplier=-1).then_inc(pool_c, 1)
                pool.affine_select(out=before[:], in_=before[:], compare_op=ALU.is_gt, fill=0.0, base=0,
                                   pattern=[[1, P]], channel_multiplier=-1).then_inc(pool_c, 1)
                pool.affine_select(out=headsel[:, 0:1], in_=headsel[:, 0:1], compare_op=ALU.is_gt, fill=0.0, base=DH,
                                   pattern=[[0, 1]], channel_multiplier=-1).then_inc(pool_c, 1)
                pool.affine_select(out=headsel[:, 1:2], in_=headsel[:, 1:2], compare_op=ALU.is_ge, fill=0.0, base=-DH,
                                   pattern=[[0, 1]], channel_multiplier=1).then_inc(pool_c, 1)
                pool.memset(m_acc[:], 0.0).then_inc(pool_c, 1)

                def zero_state(p):
                    need(pool, r_q, 4 * p)
                    pool.nop(nofuse=True)
                    pool.memset(s_bd[:], 0.0).then_inc(s_zero, 1)

                def mask_blocks(p):
                    pool.wait_ge(z_in, 64 * (p + 1))
                    pool.nop(nofuse=True)
                    pool.affine_select(out=z[:], in_=z[:], compare_op=ALU.is_gt, fill=0.0, base=0,
                                       pattern=[[1, BLK], [-1, BLK]], channel_multiplier=0).then_inc(masked, 1)
                    pool.wait_ge(masked, 2 * p + 1)
                    pool.nop(nofuse=True)
                    pool.affine_select(out=z[:], in_=z[:], compare_op=ALU.not_equal, fill=1.0, base=0,
                                       pattern=[[1, BLK], [-1, BLK]], channel_multiplier=0).then_inc(masked, 1)

                def mix_pool(i, b):
                    half = 2 * i + b
                    p3 = lambda k: lg[:, 16 * b:16 * b + 16, k:k + 1].to_broadcast([P, 16, DH])
                    v3 = lambda x: x.rearrange("p t (h d) -> p (t h) d", d=DH)
                    pool.wait_ge(sm_dve, 11 * (i + 1))
                    pool.wait_ge(st_dve, 7 * (i + 1))
                    need(pool, mixp, 3 * half)
                    pool.tensor_tensor(v3(tmp[:]), v3(v_tok[:, b * TPB:(b + 1) * TPB]), p3(3), ALU.mult).then_inc(mixp, 1)
                    pool.tensor_tensor(v3(sh[:, b]), v3(sh[:, b]), p3(0), ALU.mult).then_inc(mixp, 1)
                    pool.wait_ge(mixp, 3 * half + 2)
                    pool.tensor_tensor(sh[:, b], sh[:, b], tmp[:], ALU.add).then_inc(mixp, 1)

                def scatter(i):
                    pool.wait_ge(rt, RT * (i + 1))
                    pool.nop(nofuse=True)
                    for b in range(2):
                        for j in range(TPB):
                            for k in range(TOPK):
                                c = (b * TPB + j) * TOPK + k
                                pool.indirect_dma_start(t["xs_d"][:, :], bass.IndirectOffsetOnAxis(
                                    ap=slot_u[:, c:c + 1], axis=0), x1[:, b, j, :], None).then_inc(scattered[b], 16)

                pool.memset(mt[:], 0.0).then_inc(pool_c, 1)
                pool.memset(xf[:], 0.0).then_inc(pool_c, 1)
                zero_state(0)
                pool.wait_ge(pool_c, POOL_C + 2)
                mask_blocks(0)

                def step(i, has_prev, has_next):
                    if has_prev:
                        scatter(i - 1)
                    if has_next:
                        zero_state(i + 1)
                        mask_blocks(i + 1)
                    for b in range(2):
                        mix_pool(i, b)
                step(0, False, True)
                with pool.Fori(1, PAIRS - 1) as i:
                    step(i, True, True)
                step(PAIRS - 1, True, False)
                scatter(PAIRS - 1)
                for b in range(2):
                    pool.wait_ge(scattered[b], 16 * 8 * PAIRS)

            @block.tensor
            def _(pe):
                mm = nc.tensor.matmul
                pe.wait_ge(w_in, 16 * 17)
                pe.wait_ge(pool_c, POOL_C + 2)
                pe.wait_ge(dve_c, 8)

                def project(p, g):
                    gg = g % 4
                    b, m = gg // CH, gg % CH
                    w = wk if g < 4 else wq
                    if g == 0:
                        pe.wait_ge(xa_in, 16 * (p + 1))
                    if g < 2:
                        need(pe, gelu_ok, 8 * (p - 1))
                    else:
                        pe.wait_ge(taps, 24 * p + 3 * (g - 1))
                    for c in range(CH):
                        i = mm(X[g % 2][:], w[:, c, m * P:(m + 1) * P], xa[:, c, b * SEQ:(b + 1) * SEQ],
                               start=c == 0, stop=c == CH - 1)
                    i.then_inc(projected, 1)

                def select(p, g):
                    kq, gg = g // 4, g % 4
                    b, m = gg // CH, gg % CH
                    pe.wait_ge(squared, 8 * p + g + 1)
                    for j in range(TPB):
                        c = kq * 32 + (b * TPB + j) * HEADS + m * 2
                        i = mm(SM[:, c:c + 2], sq[:, g % 2, j * P:(j + 1) * P], headsel[:], start=True, stop=True)
                    i.then_inc(selected, 1)

                def betas(p):
                    for j in range(PT):
                        for c in range(CH):
                            i = mm(SM[:, 64 + 4 * j:68 + 4 * j], xa[:, c, j * P:(j + 1) * P], wb[:, c, :],
                                   start=c == 0, stop=c == CH - 1)
                    i.then_inc(beta_mm, 1)

                def stage1b(p, last=None):
                    select(p, 3)
                    betas(p)
                    project(p, 4)
                    project(p, 5)
                    if last is not None:
                        rank(last)
                    for j in range(4):
                        b, m = j // CH, j % CH
                        if j >= 2:
                            pe.wait_ge(k_kept, 4 * p + j - 1)
                        for q in range(TPB):
                            s = slice((b * TPB + q) * P, (b * TPB + q + 1) * P)
                            i = nc.tensor.transpose((TR, B2)[j % 2][:, q * P:(q + 1) * P], kraw[:, m, s], ident[:])
                        i.then_inc(k_turned, 1)
                    for j in range(4):
                        b, m = j // CH, j % CH
                        pe.wait_ge(k_kept, 4 * p + j + 1)
                        if j == 0 and last is not None:
                            pe.wait_ge(rt, RT * last + 8)
                        if j >= 2:
                            pe.wait_ge(kt_kept, 4 * p + j - 1)
                        for q in range(TPB):
                            i = nc.tensor.transpose((B3, B5)[j % 2][:, q * P:(q + 1) * P],
                                                    k_tok[:, b * TPB + q, m * P:(m + 1) * P], ident[:])
                        i.then_inc(k_back, 1)
                    pe.wait_ge(rooted, 2 * p + 1)
                    pe.wait_ge(beta_th, p + 1)
                    select(p, 4)
                    project(p, 6)
                    select(p, 5)
                    project(p, 7)
                    quad = (B2, B3, B4, B5)
                    pe.wait_ge(kt_kept, 4 * (p + 1))
                    for jj in range(PT // 2):
                        if jj == 1:
                            need(pe, r_out, 4 * p)
                        if jj >= 2:
                            pe.wait_ge(a_kept, 8 * p + 2 * (jj - 1))
                        for c in range(4):
                            s = slice((2 * jj + c // 2) * P, (2 * jj + c // 2 + 1) * P)
                            for par in range(2):
                                kk = k_t[hp(par), c % 2, s]
                                i = mm(quad[2 * (jj % 2) + par][:, c * P:(c + 1) * P], kk, kk, start=True, stop=True)
                                if c == 3:
                                    i.then_inc(a_mm, 1)
                    select(p, 6)
                    select(p, 7)
                    for jj in range(PT // 2):
                        if jj < 2:
                            pe.wait_ge(a_kept, 8 * p + 6 + 2 * jj)
                        else:
                            pe.wait_ge(at_kept, 8 * p + 2 * (jj - 1))
                        for c in range(4):
                            s = slice((2 * jj + c // 2) * P, (2 * jj + c // 2 + 1) * P)
                            for par in range(2):
                                i = mm(quad[2 * (jj % 2) + par][:, c * P:(c + 1) * P], k_t[hp(par), c % 2, s],
                                       q_t[hp(par), c % 2, s], start=True, stop=True)
                                if c == 3:
                                    i.then_inc(at_mm, 1)

                def merges(i):
                    pe.wait_ge(x_back, 128 * (i + 1))
                    pe.wait_ge(a_kept, 8 * (i + 1))
                    pe.wait_ge(at_kept, 8 * (i + 1))
                    pe.nop(nofuse=True)
                    for bank, u0 in ((B2, 0), (B3, 16)):
                        for u in range(u0, u0 + 16):
                            for q in range(2):
                                lo_, hi = q * 64, q * 64 + 32
                                w = mm(bank[lo_:lo_ + 32, (u - u0) * 32:(u - u0 + 1) * 32],
                                       a_sb[hi:hi + 32, u // 4, u % 4, lo_:lo_ + 32], mt[hi:hi + 32, u, hi:hi + 32],
                                       start=True, stop=True)
                        w.then_inc(m_pe, 1)
                    pe.wait_ge(m_dve, 9 * i + 2)
                    pe.wait_ge(m_act, 9 * i + 2)
                    pe.nop(nofuse=True)
                    for bank, u0 in ((B4, 0), (B5, 16)):
                        for u in range(u0, u0 + 16):
                            for q in range(2):
                                s = slice(q * 64, q * 64 + 32)
                                w = mm(bank[s, (u - u0) * 32:(u - u0 + 1) * 32], xf[s, u, 0:32], z1[s, u, :],
                                       start=True, stop=True)
                        w.then_inc(m_pe, 1)
                    for bank, u0 in ((B2, 0), (B3, 16)):
                        for u in range(u0, u0 + 16):
                            w = mm(bank[32:64, (u - u0) * 32:(u - u0 + 1) * 32], z1[0:32, u, :], xf[0:32, u, 0:32],
                                   start=True, stop=True)
                        w.then_inc(m_pe, 1)
                    pe.wait_ge(m_dve, 9 * i + 5)
                    pe.wait_ge(m_act, 9 * i + 5)
                    pe.nop(nofuse=True)
                    for n_, bank in enumerate((B4, B5, B2, B3)):
                        for u in range(8 * n_, 8 * n_ + 8):
                            w = mm(bank[0:64, (u % 8) * 64:(u % 8 + 1) * 64], a_sb[64:128, u // 4, u % 4, 0:64],
                                   mt[64:128, u, 64:128], start=True, stop=True)
                        w.then_inc(m_pe, 1)
                    pe.wait_ge(m_dve, 9 * i + 7)
                    pe.wait_ge(m_act, 9 * i + 7)
                    pe.nop(nofuse=True)
                    for n_, bank in enumerate((B4, B5, B2, B3)):
                        for u in range(8 * n_, 8 * n_ + 8):
                            w = mm(bank[0:64, (u % 8) * 64:(u % 8 + 1) * 64], xf[0:64, u, :], z2[0:64, u, :],
                                   start=True, stop=True)
                        w.then_inc(m_pe, 1)
                    pe.wait_ge(m_dve, 9 * (i + 1))
                    pe.wait_ge(m_act, 9 * (i + 1))

                def recur(i, has_prev, has_next):
                    pe.wait_ge(s_zero, i + 1)
                    for s in range(TPB):
                        if s:
                            pe.wait_ge(r_s, 6 * i + 2 * s)
                        for c in range(4):
                            b, m = c // 2, c % 2
                            tl = slice((b * TPB + s) * P, (b * TPB + s + 1) * P)
                            w = mm(B2[:, c * P:(c + 1) * P], k_t[:, m, tl], s_bd[:, c, :], start=True, stop=True)
                        w.then_inc(r_p, 1)
                        if s:
                            pe.wait_ge(r_out, 4 * i + s)
                        for c in range(4):
                            b, m = c // 2, c % 2
                            tl = slice((b * TPB + s) * P, (b * TPB + s + 1) * P)
                            w = mm(B4[:, c * P:(c + 1) * P], q_t[:, m, tl], s_bd[:, c, :], start=c == 0, stop=False,
                                   skip_group_check=True)
                        w.then_inc(r_q, 1)
                        if has_next:
                            project(i + 1, s)
                            if s:
                                select(i + 1, s - 1)
                        if has_prev and s == 0:
                            project_out(i - 1, 0)
                        if has_prev and s == 3:
                            turn_x1(i - 1, 1)
                        pe.wait_ge(r_r, 4 * i + s + 1)
                        for c in range(8):
                            b, h = c // 4, c % 4
                            w = mm(B2[:, c * DH:(c + 1) * DH], mt[:, (b * TPB + s) * HEADS + h, :], r_sb[:, b, h, :],
                                   start=True, stop=True)
                        w.then_inc(r_u, 1)
                        if has_prev and s == 3:
                            router(i - 1)
                        pe.wait_ge(r_ub, 4 * i + s + 1)
                        if s < TPB - 1:
                            for c in range(4):
                                b, m = c // 2, c % 2
                                w = mm(B5[:, c * P:(c + 1) * P], k_tok[:, b * TPB + s, m * P:(m + 1) * P],
                                       u_sb[:, b, 2 * m:2 * m + 2, :], start=True, stop=True)
                            w.then_inc(r_sx, 1)
                        for c in range(8):
                            b, h = c // 4, c % 4
                            w = mm(B4[:, c * DH:(c + 1) * DH], at_t[:, b * TPB + s, h, :], u_sb[:, b, h, :],
                                   start=False, stop=c == 7, skip_group_check=True)
                        w.then_inc(r_o, 1)
                        if has_prev and s == 0:
                            project_out(i - 1, 1)
                        if has_prev and s == 2:
                            turn_x1(i - 1, 0)

                def gate(i, b, has_next):
                    half = 2 * i + b
                    pe.wait_ge(st_dve, 7 * (i + 1))
                    for j in range(TPB):
                        w = nc.tensor.transpose(TR[0:STATS, j * P:(j + 1) * P], gst[:, b * TPB + j, :], ident[:])
                    w.then_inc(st_turned, 1)
                    pe.wait_ge(xg_in, 16 * (half + 1))
                    for c in range(HID_CH):
                        if b == 0 and c == 0:
                            pe.wait_ge(taps, 24 * (i + 2) if has_next else 24 * (i + 1))
                        if not (b == 0 and c < 2):
                            pe.wait_ge(gelu_ok, 4 * half + c - 1)
                        for k in range(CH):
                            mm(X[c % 2][:], w1x[:, k, c * P:(c + 1) * P], xg[:, k, :], start=k == 0, stop=False)
                        if c == 0:
                            pe.wait_ge(st_kept, half + 1)
                        mm(X[c % 2][:], w1s[:, c * P:(c + 1) * P], st_t[:], start=False, stop=True).then_inc(gate_mm, 1)
                    pe.wait_ge(gelu_ok, 4 * (half + 1))
                    if has_next and b == 0:
                        pe.wait_ge(rooted, 2 * (i + 2))
                    for j in range(TPB):
                        o = 128 + (b * TPB + j) * 16
                        for c in range(HID_CH):
                            w = mm(SM[:, o:o + 16], hid[:, c, j * P:(j + 1) * P], w2[:, c, :], start=c == 0, stop=c == 3)
                    w.then_inc(logit_mm, 1)

                def turn_mix(i):
                    need(pe, rt, RT * i)
                    for b in range(2):
                        pe.wait_ge(mix[b], 7 * (i + 1))
                        for m in range(CH):
                            if b:
                                pe.wait_ge(o_kept, 4 * i + m + 1)
                            for j in range(TPB):
                                w = nc.tensor.transpose(tails[m][:, j * P:(j + 1) * P], lo[:, b, j, m * P:(m + 1) * P], ident[:])
                            w.then_inc(o_turned, 1)

                def project_out(i, b):
                    pe.wait_ge(o_kept, 4 * (i + 1))
                    for jp in range(2):
                        if b:
                            pe.wait_ge(ln, LN * i + jp + 1)
                        for j in (2 * jp, 2 * jp + 1):
                            o = (j % 2) * D
                            for m in range(CH):
                                w = mm(tails[jp][:, o:o + D], o_t[:, b, m, j * P:(j + 1) * P], wo[:, m, :],
                                       start=m == 0, stop=m == 1)
                        w.then_inc(wo_mm, 1)

                def turn_x1(i, b):
                    pe.wait_ge(ln, LN * (i + 1))
                    for m in range(CH):
                        if b:
                            pe.wait_ge(x1_kept, 4 * i + m + 1)
                        for j in range(TPB):
                            w = nc.tensor.transpose(tails[m][:, j * P:(j + 1) * P], x1[:, b, j, m * P:(m + 1) * P], ident[:])
                        w.then_inc(x1_turned, 1)

                def router(i):
                    pe.wait_ge(x1_kept, 4 * (i + 1))
                    for n_ in range(PT):
                        b, j = n_ // TPB, n_ % TPB
                        for m in range(CH):
                            w = mm(TR[:, n_ * NEXP:(n_ + 1) * NEXP], o_t[:, b, m, j * P:(j + 1) * P], rw[:, m, :],
                                   start=m == 0, stop=m == 1)
                    w.then_inc(rt_mm, 1)

                def rank(i):
                    pe.wait_ge(rt, RT * i + 7)
                    end = PT * NEXP
                    mm(B3[:, 0:end], before[:], m_bf[:].rearrange("p t e -> p (t e)"), start=True, stop=False,
                       skip_group_check=True)
                    for j in range(PT - 1):
                        mm(B3[:, NEXP * (j + 1):end].rearrange("p (t e) -> p t e", e=NEXP), ones[:],
                           m_bf[:, j:j + 1, :].to_broadcast([P, PT - 1 - j, NEXP]), start=False, stop=False,
                           skip_group_check=True)
                    mm(B3[:, 0:end].rearrange("p (t e) -> p t e", e=NEXP), ones[:],
                       m_acc[:].unsqueeze(1).to_broadcast([P, PT, NEXP]), start=False, stop=True,
                       skip_group_check=True).then_inc(ranked, 1)

                for g in range(4):
                    project(0, g)
                    if g:
                        select(0, g - 1)
                stage1b(0)
                merges(0)

                def step(i, has_prev, has_next):
                    recur(i, has_prev, has_next)
                    if has_next:
                        stage1b(i + 1, i - 1 if has_prev else None)
                    else:
                        rank(i - 1)
                    for b in range(2):
                        gate(i, b, has_next)
                    if has_next:
                        merges(i + 1)
                    turn_mix(i)
                step(0, False, True)
                with pe.Fori(1, PAIRS - 1) as i:
                    step(i, True, True)
                step(PAIRS - 1, True, False)
                end = PAIRS - 1
                for b in range(2):
                    project_out(end, b)
                for b in range(2):
                    turn_x1(end, b)
                router(end)
                rank(end)

            @block.scalar
            def _(act):
                A = nc.scalar.activation
                act.wait_ge(w_in, 16 * 17)
                A(itemp[:], itemp[:], ACT.Exp).then_inc(act_c, 1)
                act.wait_ge(act_c, 1)
                A(itemp[:], itemp[:], ACT.Ln, bias=1.0).then_inc(act_c, 1)
                A(floor16[:], floor16[:], ACT.Sigmoid).then_inc(act_c, 1)
                act.wait_ge(dve_c, 2)

                def group_a(p, g):
                    gg = g % 4
                    act.wait_ge(projected, 8 * p + g + 1)
                    need(act, raw, 8 * p + g - 1)
                    need(act, squared, 8 * p + g - 1)
                    A(conv[:, g % 2], X[g % 2][:], ACT.Copy, scale=cw[:, g // 4, gg % CH, 3:4]).then_inc(tap3, 1)

                def group_b(p, g):
                    gg = g % 4
                    b, m = gg // CH, gg % CH
                    dst = (kraw if g < 4 else q_t)[:, m, b * SEQ:(b + 1) * SEQ]
                    act.wait_ge(taps, 24 * p + 3 * (g + 1))
                    if g == 0:
                        need(act, k_turned, 4 * p)
                    if g == 4:
                        need(act, r_q, 4 * p)
                        need(act, at_mm, 8 * p)
                    A(dst, conv[:, g % 2], ACT.Silu).then_inc(raw, 1)
                    act.wait_ge(raw, 8 * p + g + 1)
                    need(act, selected, 8 * p + g - 1)
                    A(sq[:, g % 2], dst, ACT.Square).then_inc(squared, 1)

                def stage1b(p):
                    group_b(p, 3)
                    act.wait_ge(beta_mm, p + 1)
                    need(act, beta_ok, 2 * p)
                    A(th[:], SM[:, 64:96], ACT.Tanh, scale=0.5).then_inc(beta_th, 1)
                    group_a(p, 4)
                    group_a(p, 5)
                    act.wait_ge(selected, 8 * p + 4)
                    need(act, rn_ok, 2 * p)
                    A(nrm[:, 0], SM[:, 0:32], ACT.Sqrt, bias=eps6[:, 0:1]).then_inc(rooted, 1)
                    group_b(p, 4)
                    group_b(p, 5)
                    for j in range(4):
                        act.wait_ge(k_back, 4 * p + j + 1)
                        A(k_t[:, j % CH, (j // CH) * SEQ:(j // CH + 1) * SEQ], (B3, B5)[j % 2][:], ACT.Copy).then_inc(kt_kept, 1)
                    group_a(p, 6)
                    group_a(p, 7)
                    group_b(p, 6)
                    group_b(p, 7)
                    act.wait_ge(selected, 8 * p + 8)
                    A(nrm[:, 1], SM[:, 32:64], ACT.Sqrt, bias=eps6[:, 0:1]).then_inc(rooted, 1)

                def merge(i, k):
                    c = lambda x: x.rearrange("p (u k) -> p u k", k=BLK)
                    c2 = lambda x: x.rearrange("p (u k) -> p u k", k=2 * BLK)
                    cp = lambda out, in_: A(out, in_, ACT.Copy).then_inc(m_act, 1)
                    upper_bank = (2, 4, 6, 8, 12)[k]
                    act.wait_ge(m_pe, 14 * i + upper_bank)
                    if k == 0:
                        for q in range(2):
                            s = slice(q * 64, q * 64 + 32)
                            cp(z1[s, 16:32, :], c(B3[s, :]))
                    elif k == 1:
                        for q in range(2):
                            s = slice(q * 64, q * 64 + 32)
                            cp(mt[s, 16:32, q * 64 + 32:q * 64 + 64], c(B5[s, :]))
                    elif k == 2:
                        cp(xf[32:64, 16:32, 0:32], c(B3[32:64, :]))
                    elif k == 3:
                        cp(z2[0:64, 8:16, :], c2(B5[0:64, :]))
                        act.wait_ge(m_pe, 14 * i + 10)
                        cp(z2[0:64, 24:32, :], c2(B3[0:64, :]))
                    else:
                        cp(mt[0:64, 8:16, 64:128], c2(B5[0:64, :]))
                        act.wait_ge(m_pe, 14 * i + 14)
                        cp(mt[0:64, 24:32, 64:128], c2(B3[0:64, :]))

                def recur(i, has_prev, has_next):
                    for s in range(TPB):
                        if has_next:
                            group_a(i + 1, s)
                        if has_prev and s == 2:
                            root_norm(i - 1)
                        if has_prev and s == 3:
                            keep_x1(i - 1)
                        act.wait_ge(r_u, 4 * i + s + 1)
                        A(u_sb[:].rearrange("p b h d -> p (b h d)"), B2[:], ACT.Copy).then_inc(r_ub, 1)
                        if has_next and s < 3:
                            group_b(i + 1, s)

                def gate(i, b):
                    half = 2 * i + b
                    act.wait_ge(st_turned, half + 1)
                    need(act, gate_mm, 4 * half)
                    A(st_t[:], TR[0:STATS, :], ACT.Copy).then_inc(st_kept, 1)
                    need(act, logit_mm, half)
                    for c in range(HID_CH):
                        act.wait_ge(gate_mm, 4 * half + c + 1)
                        A(hid[:, c, :], X[c % 2][:], ACT.Gelu, bias=b1[:, c:c + 1]).then_inc(gelu_ok, 1)

                def rms(i, b):
                    half = 2 * i + b
                    act.wait_ge(mix[b], 7 * i + 4)
                    if b:
                        act.wait_ge(mix[0], 7 * i + 5)
                    A(squares, lo[:, b], ACT.Square).then_inc(sq_ok, 1)
                    act.wait_ge(mix[b], 7 * i + 5)
                    A(s32[:, 16 * b:16 * b + 16], s32[:, 16 * b:16 * b + 16], ACT.Sqrt, bias=eps5[:, 0:1],
                      scale=1.0 / DH).then_inc(rms_rt, 1)

                def merge_and_mix(i, has_next):
                    act.wait_ge(sm_dve, 11 * i + 4)
                    A(lg[:], lg[:], ACT.Exp).then_inc(sm_exp, 1)
                    if has_next:
                        for k in range(3):
                            merge(i + 1, k)
                    rms(i, 0)
                    if has_next:
                        merge(i + 1, 3)
                    rms(i, 1)
                    if has_next:
                        merge(i + 1, 4)
                    for k in range(4):
                        b, m = k // 2, k % 2
                        act.wait_ge(o_turned, 4 * i + k + 1)
                        if k == 0:
                            need(act, rt_mm, i)
                        A(o_t[:, b, m, :], tails[m][:], ACT.Copy).then_inc(o_kept, 1)

                def turn_blocks(p):
                    act.wait_ge(solve, SOLVE * (p + 1))
                    A(zt[:], z[:].rearrange("p i k -> p k i"), ACT.Copy).then_inc(zt_ok, 1)

                def root_norm(i):
                    act.wait_ge(ln, LN * i + 6)
                    A(rstd[:], mv[:, :, 1], ACT.Sqrt, bias=eps5[:, 0:1]).then_inc(ln_rt, 1)

                def keep_x1(i):
                    act.wait_ge(wo_mm, 4 * (i + 1))
                    for k in range(4):
                        b, m = k // 2, k % 2
                        act.wait_ge(x1_turned, 4 * i + k + 1)
                        A(o_t[:, b, m, :], tails[m][:], ACT.Copy).then_inc(x1_kept, 1)

                for g in range(4):
                    group_a(0, g)
                    if g < 3:
                        group_b(0, g)
                stage1b(0)
                turn_blocks(0)
                for k in range(5):
                    merge(0, k)

                def step(i, has_prev, has_next):
                    recur(i, has_prev, has_next)
                    if has_next:
                        stage1b(i + 1)
                    gate(i, 0)
                    if has_next:
                        turn_blocks(i + 1)
                    gate(i, 1)
                    merge_and_mix(i, has_next)
                step(0, False, True)
                with act.Fori(1, PAIRS - 1) as i:
                    step(i, True, True)
                step(PAIRS - 1, True, False)
                root_norm(PAIRS - 1)
                keep_x1(PAIRS - 1)

            @block.vector
            def _(dve):
                V = nc.vector
                dve.wait_ge(w_in, 16 * 17)
                V.memset(eps6[:], 1e-6).then_inc(dve_c, 1)
                V.memset(eps5[:], 1e-5).then_inc(dve_c, 1)
                V.tensor_scalar(wo[:], wo[:], onw[:, 0:1], None, ALU.mult).then_inc(dve_c, 1)
                dve.wait_ge(pool_c, 6)
                V.tensor_copy(iota8[:], mi8[:, 0, :]).then_inc(dve_c, 1)
                dve.wait_ge(dve_c, 4)
                V.tensor_scalar(base8[:], iota8[:], float(CAP), None, ALU.mult).then_inc(dve_c, 1)
                dve.wait_ge(act_c, 3)
                V.tensor_scalar(floor16[:], floor16[:], 0.05, None, ALU.mult).then_inc(dve_c, 1)
                V.tensor_scalar(itemp[:], itemp[:], 1e-4, None, ALU.add).then_inc(dve_c, 1)
                dve.wait_ge(dve_c, 7)
                V.reciprocal(itemp[:], itemp[:]).then_inc(dve_c, 1)
                dve.wait_ge(pool_c, POOL_C + 2)

                def taps_of(p, g):
                    gg = g % 4
                    dve.wait_ge(tap3, 8 * p + g + 1)
                    for k in range(1, TAPS):
                        need(dve, taps, 24 * p + 3 * g + k - 1)
                        V.scalar_tensor_tensor(conv[:, g % 2, k:], X[g % 2][:, :SEQ - k],
                                               cw[:, g // 4, gg % CH, 3 - k:4 - k], conv[:, g % 2, k:],
                                               ALU.mult, ALU.add).then_inc(taps, 1)

                def norm(p, kq):
                    dve.wait_ge(rooted, 2 * p + kq + 1)
                    V.reciprocal(rn[:, kq], nrm[:, kq]).then_inc(rn_ok, 1)

                def stage1b(p, last=None):
                    taps_of(p, 4)
                    dve.wait_ge(beta_th, p + 1)
                    V.tensor_scalar(beta[:].rearrange("p t h -> p (t h)"), th[:], 0.5, 0.5, ALU.mult, ALU.add).then_inc(beta_ok, 1)
                    V.tensor_scalar(nbeta[:].rearrange("p t h -> p (t h)"), th[:], -0.5, -0.5, ALU.mult, ALU.add).then_inc(beta_ok, 1)
                    norm(p, 0)
                    taps_of(p, 5)
                    if last is not None:
                        place(last)
                    dve.wait_ge(rn_ok, 2 * p + 1)
                    for j in range(4):
                        b, m = j // CH, j % CH
                        dve.wait_ge(k_turned, 4 * p + j + 1)
                        r = rn[:, 0].rearrange("p (t h) -> p t h", h=HEADS)[:, b * TPB:(b + 1) * TPB, 2 * m:2 * m + 2]
                        V.tensor_tensor(
                            k_tok[:, b * TPB:(b + 1) * TPB, m * P:(m + 1) * P].rearrange("p t (h d) -> p t h d", d=DH),
                            (TR, B2)[j % 2][:].rearrange("p (t h d) -> p t h d", h=2, d=DH),
                            r.unsqueeze(3).to_broadcast([P, TPB, 2, DH]), ALU.mult).then_inc(k_kept, 1)
                    taps_of(p, 6)
                    taps_of(p, 7)
                    dve.wait_ge(beta_ok, 2 * (p + 1))
                    for n_ in range(PT):
                        jj, par = n_ // 2, n_ % 2
                        ts = slice(2 * jj, 2 * jj + 2)
                        dve.wait_ge(a_mm, 8 * p + n_ + 1)
                        if n_ == 0:
                            need(dve, m_pe, 14 * p)
                        V.tensor_tensor(a_sb[:, ts, par::2, :],
                                        (B2, B3, B4, B5)[n_ % 4][:].rearrange("p (t m s) -> p t m s", t=2, m=2),
                                        nbeta[:, ts, par::2].unsqueeze(3).to_broadcast([P, 2, 2, P]),
                                        ALU.mult).then_inc(a_kept, 1)
                    for n_ in range(PT):
                        jj, par = n_ // 2, n_ % 2
                        dve.wait_ge(at_mm, 8 * p + n_ + 1)
                        V.tensor_tensor(at_t[:, 2 * jj:2 * jj + 2, par::2, :],
                                        (B2, B3, B4, B5)[n_ % 4][:].rearrange("p (t m s) -> p t m s", t=2, m=2),
                                        upper[:].unsqueeze(1).unsqueeze(1).to_broadcast([P, 2, 2, P]),
                                        ALU.mult).then_inc(at_kept, 1)
                    norm(p, 1)

                def solver(p):
                    dve.wait_ge(masked, 2 * (p + 1))
                    need(dve, x_out, 32 * p)
                    k = SOLVE * p
                    for j in range(1, BLK - 1):
                        left = BLK - 1 - j
                        need(dve, solve, k)
                        V.tensor_tensor(zt[:, 0:left, 0:j], z[:, j + 1:, j:j + 1].to_broadcast([P, left, j]),
                                        z[:, j:j + 1, 0:j].to_broadcast([P, left, j]), ALU.mult).then_inc(solve, 1)
                        dve.wait_ge(solve, k + 1)
                        V.tensor_tensor(z[:, j + 1:, 0:j], z[:, j + 1:, 0:j], zt[:, 0:left, 0:j], ALU.add).then_inc(solve, 1)
                        k += 2

                def merge(i, k):
                    c = lambda x: x.rearrange("p (u k) -> p u k", k=BLK)
                    c2 = lambda x: x.rearrange("p (u k) -> p u k", k=2 * BLK)
                    cp = lambda out, in_: V.tensor_copy(out, in_).then_inc(m_dve, 1)
                    lower_bank = (1, 3, 5, 7, 11)[k]
                    dve.wait_ge(m_pe, 14 * i + lower_bank)
                    if k == 0:
                        for q in range(2):
                            s = slice(q * 64, q * 64 + 32)
                            cp(z1[s, 0:16, :], c(B2[s, :]))
                    elif k == 1:
                        for q in range(2):
                            s = slice(q * 64, q * 64 + 32)
                            cp(mt[s, 0:16, q * 64 + 32:q * 64 + 64], c(B4[s, :]))
                    elif k == 2:
                        cp(xf[32:64, 0:16, 0:32], c(B2[32:64, :]))
                    elif k == 3:
                        cp(z2[0:64, 0:8, :], c2(B4[0:64, :]))
                        dve.wait_ge(m_pe, 14 * i + 9)
                        cp(z2[0:64, 16:24, :], c2(B2[0:64, :]))
                    else:
                        cp(mt[0:64, 0:8, 64:128], c2(B4[0:64, :]))
                        dve.wait_ge(m_pe, 14 * i + 13)
                        cp(mt[0:64, 16:24, 64:128], c2(B2[0:64, :]))

                def bn(i, s, part):
                    for b in range(2):
                        n_ = b * TPB + s
                        srcs = (sh[:, b, s], lo[:, b, s], v_tok[:, n_], delta[:, n_])
                        for k in ((0,), (1,), (3, 2))[part]:
                            for h in range(HEADS):
                                w = V.bn_stats(bnst[:, n_, (0, 1, 3, 2)[k], h, :], srcs[k][:, h * DH:(h + 1) * DH])
                    return w

                def recur(i, has_prev, has_next):
                    vv = v_tok[:].rearrange("p (b t) c -> p b t c", t=TPB)
                    bb = beta[:].rearrange("p (b t) h -> p b t h", t=TPB)
                    qn = rn[:, 1].rearrange("p (b t h) -> p b t h", t=TPB, h=HEADS)
                    dl = delta[:].rearrange("p (b t) c -> p b t c", t=TPB)
                    dve.wait_ge(v_in, 16 * (i + 1))
                    dve.wait_ge(rn_ok, 2 * (i + 1))
                    for s in range(TPB):
                        dve.wait_ge(r_p, 4 * i + s + 1)
                        V.tensor_tensor(r_sb[:].rearrange("p b h d -> p b (h d)"), vv[:, :, s, :],
                                        B2[:].rearrange("p (b c) -> p b c", b=2), ALU.subtract).then_inc(r_r1, 1)
                        dve.wait_ge(r_r1, 4 * i + s + 1)
                        V.tensor_tensor(r_sb[:], r_sb[:], bb[:, :, s, :].unsqueeze(3).to_broadcast([P, 2, HEADS, DH]),
                                        ALU.mult).then_inc(r_r, 1)
                        if has_next:
                            taps_of(i + 1, s)
                        if has_prev and s < 2:
                            add_out(i - 1, s)
                        if has_prev and s == 2:
                            scale_norm(i - 1)
                        if s:
                            if s == 1:
                                for b in range(2):
                                    dve.wait_ge(sl_in[b], 32 * (i + 1))
                            dve.wait_ge(r_out, 4 * i + s)
                            bn(i, s - 1, 0)
                        if s < TPB - 1:
                            dve.wait_ge(r_sx, 3 * i + s + 1)
                            dve.wait_ge(r_q, 4 * i + s + 1)
                            for q in range(2):
                                hs = slice(q * DH, (q + 1) * DH)
                                V.tensor_tensor(s_bd[hs, :, hs], s_bd[hs, :, hs],
                                                B5[hs, :].rearrange("p (c d) -> p c d", d=P)[:, :, hs],
                                                ALU.add).then_inc(r_s, 1)
                        if s:
                            bn(i, s - 1, 1)
                        dve.wait_ge(r_o, 4 * i + s + 1)
                        V.tensor_tensor(dl[:, :, s, :].rearrange("p b (h d) -> p b h d", d=DH),
                                        B4[:].rearrange("p (b h d) -> p b h d", h=HEADS, d=DH),
                                        qn[:, :, s, :].unsqueeze(3).to_broadcast([P, 2, HEADS, DH]),
                                        ALU.mult).then_inc(r_out, 1)
                        if has_prev and s == 1:
                            norm_stats(i - 1)
                        if s:
                            bn(i, s - 1, 2)
                        if has_prev and s == 3:
                            choose(i - 1)
                    dve.wait_ge(r_out, 4 * (i + 1))
                    for part in range(3):
                        w = bn(i, TPB - 1, part)
                    w.then_inc(st_dve, 1)

                def stats(i):
                    f = bnst[:].rearrange("p t k h s -> p t (k h) s")
                    g = gst[:].rearrange("p t (a s) -> p t a s", s=2)
                    c = 7 * i
                    dve.wait_ge(st_dve, c + 1)
                    need(dve, st_turned, 2 * i)
                    V.tensor_tensor(g[:, :, :, 0], f[:, :, :, 1], f[:, :, :, 4], ALU.add).then_inc(st_dve, 1)
                    V.tensor_tensor(dm[:], f[:, :, :, 1], f[:, :, :, 4], ALU.subtract).then_inc(st_dve, 1)
                    V.tensor_tensor(g[:, :, :, 1], f[:, :, :, 2], f[:, :, :, 5], ALU.add).then_inc(st_dve, 1)
                    dve.wait_ge(st_dve, c + 4)
                    V.scalar_tensor_tensor(dm[:], dm[:], 0.25, dm[:], ALU.mult, ALU.mult).then_inc(st_dve, 1)
                    V.tensor_scalar(g[:, :, :, 0], g[:, :, :, 0], 0.5, None, ALU.mult).then_inc(st_dve, 1)
                    dve.wait_ge(st_dve, c + 6)
                    V.scalar_tensor_tensor(g[:, :, :, 1], g[:, :, :, 1], 1.0 / DH, dm[:], ALU.mult,
                                           ALU.add).then_inc(st_dve, 1)

                def softmax(i):
                    c = 11 * i
                    t4 = lambda x: x[:].rearrange("p (t h) k -> p t h k", h=HEADS)
                    t16 = lambda x: x[:].rearrange("p (t h) k -> p t (h k)", h=HEADS)
                    g3 = [P, UNITS, PATHS]
                    dve.wait_ge(logit_mm, 2 * (i + 1))
                    need(dve, mixp, 6 * i)
                    V.tensor_tensor(t16(lg), SM[:, 128:256].rearrange("p (t k) -> p t k", t=PT),
                                    bias16[:].unsqueeze(1).to_broadcast([P, PT, 16]), ALU.add).then_inc(sm_dve, 1)
                    dve.wait_ge(sm_dve, c + 1)
                    V.tensor_tensor(t4(lg), t4(lg), itemp[:].unsqueeze(1).unsqueeze(3).to_broadcast([P, PT, HEADS, PATHS]),
                                    ALU.mult).then_inc(sm_dve, 1)
                    dve.wait_ge(sm_dve, c + 2)
                    V.tensor_reduce(s32[:], lg[:], AX.X, ALU.max).then_inc(sm_dve, 1)
                    dve.wait_ge(sm_dve, c + 3)
                    V.tensor_tensor(lg[:], lg[:], s32[:].unsqueeze(2).to_broadcast(g3), ALU.subtract).then_inc(sm_dve, 1)
                    dve.wait_ge(sm_exp, i + 1)
                    V.tensor_reduce(s32[:], lg[:], AX.X, ALU.add).then_inc(sm_dve, 1)
                    dve.wait_ge(sm_dve, c + 5)
                    V.reciprocal(r32[:], s32[:]).then_inc(sm_dve, 1)
                    dve.wait_ge(sm_dve, c + 6)
                    V.tensor_tensor(lg[:], lg[:], r32[:].unsqueeze(2).to_broadcast(g3), ALU.mult).then_inc(sm_dve, 1)
                    dve.wait_ge(sm_dve, c + 7)
                    V.tensor_tensor(t16(lg), t16(lg), floor16[:].unsqueeze(1).to_broadcast([P, PT, 16]),
                                    ALU.max).then_inc(sm_dve, 1)
                    dve.wait_ge(sm_dve, c + 8)
                    V.tensor_reduce(s32[:], lg[:], AX.X, ALU.add).then_inc(sm_dve, 1)
                    dve.wait_ge(sm_dve, c + 9)
                    V.reciprocal(r32[:], s32[:]).then_inc(sm_dve, 1)
                    dve.wait_ge(sm_dve, c + 10)
                    V.tensor_tensor(lg[:], lg[:], r32[:].unsqueeze(2).to_broadcast(g3), ALU.mult).then_inc(sm_dve, 1)

                v3 = lambda x: x.rearrange("p t (h d) -> p (t h) d", d=DH)

                def weigh(i, b):
                    p3 = lambda k: lg[:, 16 * b:16 * b + 16, k:k + 1].to_broadcast([P, 16, DH])
                    dlt = delta[:, b * TPB:(b + 1) * TPB]
                    dve.wait_ge(sm_dve, 11 * (i + 1))
                    V.tensor_tensor(v3(lo[:, b]), v3(lo[:, b]), p3(1), ALU.mult).then_inc(mix[b], 1)
                    V.tensor_tensor(v3(dlt), v3(dlt), p3(2), ALU.mult).then_inc(mix[b], 1)

                def add_two(i, b):
                    dve.wait_ge(mix[b], 7 * i + 2)
                    V.tensor_tensor(lo[:, b], lo[:, b], delta[:, b * TPB:(b + 1) * TPB], ALU.add).then_inc(mix[b], 1)

                def add_pool(i, b):
                    dve.wait_ge(mix[b], 7 * i + 3)
                    dve.wait_ge(mixp, 3 * (2 * i + b + 1))
                    V.tensor_tensor(lo[:, b], lo[:, b], sh[:, b], ALU.add).then_inc(mix[b], 1)

                def sum_squares(i, b):
                    dve.wait_ge(sq_ok, 2 * i + b + 1)
                    V.tensor_reduce(s32[:, 16 * b:16 * b + 16], v3(squares), AX.X, ALU.add).then_inc(mix[b], 1)

                def scale_mix(i, b):
                    r = r32[:, 16 * b:16 * b + 16]
                    dve.wait_ge(rms_rt, 2 * i + b + 1)
                    V.reciprocal(r, s32[:, 16 * b:16 * b + 16]).then_inc(mix[b], 1)
                    dve.wait_ge(mix[b], 7 * i + 6)
                    V.tensor_tensor(v3(lo[:, b]), v3(lo[:, b]), r.unsqueeze(2).to_broadcast([P, 16, DH]),
                                    ALU.mult).then_inc(mix[b], 1)

                def merge_and_mix(i, has_next):
                    softmax(i)
                    weigh(i, 0)
                    if has_next:
                        merge(i + 1, 0)
                    add_two(i, 0)
                    weigh(i, 1)
                    if has_next:
                        merge(i + 1, 1)
                        merge(i + 1, 2)
                    add_pool(i, 0)
                    add_two(i, 1)
                    sum_squares(i, 0)
                    if has_next:
                        merge(i + 1, 3)
                    scale_mix(i, 0)
                    add_pool(i, 1)
                    sum_squares(i, 1)
                    if has_next:
                        merge(i + 1, 4)
                    scale_mix(i, 1)

                def add_out(i, b):
                    dve.wait_ge(x_in[b], 16 * (i + 1))
                    for j in range(2):
                        dve.wait_ge(wo_mm, 4 * i + 2 * b + j + 1)
                        V.tensor_tensor(x1[:, b, 2 * j:2 * j + 2], x1[:, b, 2 * j:2 * j + 2],
                                        tails[j][:].rearrange("p (t c) -> p t c", c=D), ALU.add).then_inc(ln, 1)

                def norm_stats(i):
                    dve.wait_ge(ln, LN * i + 4)
                    for n_ in range(PT):
                        w = V.bn_stats(lbn[:, n_], x1[:, n_ // TPB, n_ % TPB])
                    w.then_inc(ln, 1)
                    hold(dve, ln, LN * i + 5)
                    for n_ in range(PT):
                        w = V.bn_aggr(mv[:, n_], lbn[:, n_])
                    w.then_inc(ln, 1)

                def scale_norm(i):
                    dve.wait_ge(ln_rt, i + 1)
                    V.reciprocal(rstd[:], rstd[:]).then_inc(ln, 1)
                    dve.wait_ge(ln, LN * i + 7)
                    for n_ in range(PT):
                        b, j = n_ // TPB, n_ % TPB
                        w = V.tensor_scalar(x1[:, b, j], x1[:, b, j], mv[:, n_, 0:1], rstd[:, n_:n_ + 1],
                                            ALU.subtract, ALU.mult)
                    w.then_inc(ln, 1)

                def choose(i):
                    c = RT * i
                    at = bass.ds(i * (PT * TOPK), PT * TOPK)
                    dve.wait_ge(rt_mm, i + 1)
                    V.tensor_tensor(rl[:], TR[:, 0:PT * NEXP].rearrange("p (t e) -> p t e", e=NEXP),
                                    rb[:].unsqueeze(1).to_broadcast([P, PT, NEXP]), ALU.add).then_inc(rt, 1)
                    hold(dve, rt, c + 1)
                    dve.nop(nofuse=True)
                    for j in range(PT):
                        w = V.max(mx8[:, j], rl[:, j])
                    w.then_inc(rt, 1)
                    hold(dve, rt, c + 2)
                    dve.nop(nofuse=True)
                    for j in range(PT):
                        w = V.max_index(mi8[:, j], mx8[:, j], rl[:, j])
                    w.then_inc(rt, 1)
                    hold(dve, rt, c + 3)
                    dve.nop(nofuse=True)
                    V.tensor_copy(ef[:].rearrange("p (t k) -> p t k", k=TOPK), mi8[:, :, 0:TOPK]).then_inc(rt, 1)
                    V.tensor_copy(top2[:, at].rearrange("p (t k) -> p t k", k=TOPK), mx8[:, :, 0:TOPK]).then_inc(rt, 1)
                    dve.wait_ge(rt, c + 4)
                    V.tensor_tensor(oh[:], ef[:].unsqueeze(2).to_broadcast([P, PT * TOPK, NEXP]),
                                    iota8[:].unsqueeze(1).to_broadcast([P, PT * TOPK, NEXP]), ALU.is_equal).then_inc(rt, 1)
                    dve.wait_ge(rt, c + 6)
                    o4 = oh[:].rearrange("p (t k) e -> p t k e", k=TOPK)
                    V.tensor_tensor(m_bf[:], o4[:, :, 0, :], o4[:, :, 1, :], ALU.add).then_inc(rt, 1)

                def place(i):
                    c = RT * i
                    at = bass.ds(i * (PT * TOPK), PT * TOPK)
                    o4 = oh[:].rearrange("p (t k) e -> p t k e", k=TOPK)
                    dve.wait_ge(ranked, i + 1)
                    V.tensor_tensor(rk[:], B3[:, 0:PT * NEXP].rearrange("p (t e) -> p t e", e=NEXP),
                                    base8[:].unsqueeze(1).to_broadcast([P, PT, NEXP]), ALU.add).then_inc(rt, 1)
                    dve.wait_ge(rt, c + 8)
                    V.tensor_tensor(o4, o4, rk[:].unsqueeze(2).to_broadcast([P, PT, TOPK, NEXP]), ALU.mult).then_inc(rt, 1)
                    dve.wait_ge(rt, c + 9)
                    V.tensor_reduce(slotf[:, at], oh[:], AX.X, ALU.add).then_inc(rt, 1)
                    dve.wait_ge(rt, c + 10)
                    dve.nop(nofuse=True)
                    V.tensor_copy(slot_u[:], slotf[:, at]).then_inc(rt, 1)
                    V.tensor_reduce(m_sum[:], m_bf[:].rearrange("p t e -> p e t"), AX.X, ALU.add).then_inc(rt, 1)
                    dve.wait_ge(rt, c + 12)
                    V.tensor_tensor(m_acc[:], m_acc[:], m_sum[:], ALU.add).then_inc(rt, 1)
                    V.tensor_copy(eidx[:, at], ef[:]).then_inc(rt, 1)

                for g in range(4):
                    taps_of(0, g)
                stage1b(0)
                solver(0)
                for k in range(5):
                    merge(0, k)

                def step(i, has_prev, has_next):
                    recur(i, has_prev, has_next)
                    if has_next:
                        stage1b(i + 1, i - 1 if has_prev else None)
                    else:
                        place(i - 1)
                    stats(i)
                    if has_next:
                        solver(i + 1)
                    merge_and_mix(i, has_next)
                step(0, False, True)
                with dve.Fori(1, PAIRS - 1) as i:
                    step(i, True, True)
                step(PAIRS - 1, True, False)
                end = PAIRS - 1
                for b in range(2):
                    add_out(end, b)
                norm_stats(end)
                scale_norm(end)
                choose(end)
                place(end)


EXTRA = NEXP
NMOE = TOKENS * TOPK // P + EXTRA
SPARE = NEXP * CAP
GU = 2 * D


def experts_and_combine(nc, t, keep):
    with ExitStack() as ctx:
        def sb(name, shape, dt=F32):
            return ctx.enter_context(nc.sbuf_tensor("C_" + name, shape, dt))

        def ps(name):
            return ctx.enter_context(nc.psum_tensor("C_ps_" + name, [P, 512], F32))

        def sem(name):
            return ctx.enter_context(nc.semaphore("C_" + name))

        eidx, slotf, top2, m_acc = keep["eidx"], keep["slotf"], keep["top2"], keep["m_acc"]
        wgu = sb("wgu", [P, NEXP, CH, GU]); wd = sb("wd", [P, NEXP, CH, D])
        ident = sb("ident", [P, P]); ones = sb("ones", [P, P], BF16); zero = sb("zero", [P, D])
        i8 = sb("i8", [P, NEXP], I32); it = sb("it", [P, NMOE], I32); i64 = sb("i64", [P, TILES], I32)
        ip = sb("ip", [P, 1], I32)
        f8 = sb("f8", [P, NEXP]); ft = sb("ft", [P, NMOE]); f64 = sb("f64", [P, TILES]); fp = sb("fp", [P, 1])
        cnt = sb("cnt", [P, NEXP]); gt = sb("gt", [P, NEXP, TILES]); tiles = sb("tiles", [P, NEXP])
        below = sb("below", [P, NEXP, NEXP]); tbase = sb("tbase", [P, NEXP]); tend = sb("tend", [P, NEXP])
        ge = sb("ge", [P, NMOE, NEXP]); ex = sb("ex", [P, NMOE]); tb = sb("tb", [P, NMOE])
        xrow = sb("xrow", [P, NMOE]); xrow_i = sb("xrow_i", [P, NMOE], I32); ex_i = sb("ex_i", [P, NMOE], I32)
        pad = sb("pad", [P, NEXP]); pad_u = sb("pad_u", [P, NEXP], U32)
        oh = sb("oh", [P, TILES * TOPK, NEXP]); off = sb("off", [P, NEXP])
        yr = sb("yr", [P, TILES * TOPK]); yr_u = sb("yr_u", [P, TILES * TOPK], U32)
        ev = sb("ev", [P, TILES]); wts = sb("wts", [P, TILES, TOPK]); den = sb("den", [P, TILES])
        xb = sb("xb", [P, 2, D]); xt = sb("xt", [P, 2, CH, P]); sg = sb("sg", [P, 2, D]); av = sb("av", [P, 2, D])
        avt = sb("avt", [P, 2, CH, P]); yb = sb("yb", [P, 2, D])
        G4 = 4
        gy = sb("gy", [P, 2, G4 * TOPK, D]); gx = sb("gx", [P, 2, G4, D])
        now = sb("now", [P, 2, G4 * TOPK], U32)
        lbn = sb("lbn", [P, 2, G4, 6]); mv = sb("mv", [P, 2, G4, 2]); rstd = sb("rstd", [P, 2, G4])
        eps = sb("eps", [P, 1])
        ps_x = [ps(f"x{i}") for i in range(2)]; ps_g = [ps(f"g{i}") for i in range(2)]
        ps_a = [ps(f"a{i}") for i in range(2)]; ps_y = [ps(f"y{i}") for i in range(2)]

        w_in, pool_c, idx, counted = sem("weights_in"), sem("pool_const"), sem("tables"), sem("counted")
        tiles_ok, pads_ok, gap_ok, rows_ok = sem("tiles_ok"), sem("pads_ok"), sem("gap_ok"), sem("rows_ok")
        exps, zeroed = sem("gate_exp"), sem("pads_zeroed")
        x_in = [sem(f"x_in{i}") for i in range(2)]; y_out = [sem(f"y_out{i}") for i in range(2)]
        x_turned, x_kept, gu_mm, silu_ok, act_ok = (sem(n) for n in ("x_turned", "x_kept", "gu_mm", "silu_ok", "act_ok"))
        a_turned, a_kept, y_mm, y_kept = (sem(n) for n in ("a_turned", "a_kept", "y_mm", "y_kept"))
        gy_in = [sem(f"gy_in{i}") for i in range(2)]; gx_in = [sem(f"gx_in{i}") for i in range(2)]
        now_ok = sem("now_ok")
        fin, rooted = sem("final_dve"), sem("final_rooted")
        out_ok = [sem(f"out{i}") for i in range(2)]
        groups = TILES // G4
        FIN = 5 * G4 + 1
        xs = t["xs_d"]
        tok = lambda n: t[n].rearrange("(t p) c -> p t c", p=P)

        with nc.Block() as block:
            @block.sync
            def _(sp):
                for name, lo_ in (("we_gate", 0), ("we_up", D)):
                    for e in range(NEXP):
                        sp.dma_start(wgu[:, e, :, lo_:lo_ + D], t[name][e].rearrange("(c p) n -> p c n", p=P)).then_inc(w_in, 16)
                for e in range(NEXP):
                    sp.dma_start(wd[:, e], t["we_down"][e].rearrange("(c p) n -> p c n", p=P)).then_inc(w_in, 16)
                sp.wait_ge(tiles_ok, 2)
                sp.wait_ge(zeroed, 16 * (NEXP + EXTRA))

                def load(j, u):
                    hold(sp, x_turned, j - 1)
                    row = sp.value_load(xrow_i[0:1, bass.ds(j, 1)], min_val=0, max_val=SPARE + (EXTRA - 1) * P)
                    sp.dma_start(xb[:, u], xs[bass.ds(row, P), :]).then_inc(x_in[u], 16)
                load(0, 0)
                load(1, 1)
                with sp.Fori(1, NMOE // 2) as i:
                    for u in range(2):
                        load(2 * i + u, u)

                def group(g, u):
                    if not isinstance(g, int) or g > 1:
                        hold(sp, out_ok[u], 8 * (g - u))
                    sp.dma_start(gx[:, u], tok("x1_d")[:, bass.ds(g * G4, G4), :]).then_inc(gx_in[u], 16)

                def store(g, u):
                    hold(sp, fin, FIN * (g + 1))
                    sp.dma_start(tok("out")[:, bass.ds(g * G4, G4), :], gx[:, u]).then_inc(out_ok[u], 16)
                group(0, 0)
                group(1, 1)
                with sp.Fori(0, groups // 2 - 1) as i:
                    for u in range(2):
                        store(2 * i + u, u)
                        group(2 * i + u + 2, u)
                for u in range(2):
                    store(groups - 2 + u, u)
                for u in range(2):
                    sp.wait_ge(out_ok[u], 16 * groups // 2)

            @block.gpsimd
            def _(pool):
                pool.memset(ident[:], 0.0).then_inc(pool_c, 1)
                pool.memset(ones[:], 1.0).then_inc(pool_c, 1)
                pool.memset(zero[:], 0.0).then_inc(pool_c, 1)
                pool.iota(i8[:], [[1, NEXP]], base=0, channel_multiplier=0).then_inc(pool_c, 1)
                pool.iota(it[:], [[1, NMOE]], base=0, channel_multiplier=0).then_inc(pool_c, 1)
                pool.iota(i64[:], [[P, TILES]], base=0, channel_multiplier=0).then_inc(pool_c, 1)
                pool.iota(ip[:], [[0, 1]], base=0, channel_multiplier=1).then_inc(pool_c, 1)
                pool.wait_ge(pool_c, 7)
                pool.affine_select(out=ident[:], in_=ident[:], compare_op=ALU.not_equal, fill=1.0, base=0,
                                   pattern=[[-1, P]], channel_multiplier=1).then_inc(pool_c, 1)
                for k in range(EXTRA):
                    pool.dma_start(xs[SPARE + k * P:SPARE + (k + 1) * P, :], zero[:]).then_inc(zeroed, 16)
                pool.wait_ge(pads_ok, 1)
                for e in range(NEXP):
                    pool.indirect_dma_start(xs[:, :], bass.IndirectOffsetOnAxis(ap=pad_u[:, e:e + 1], axis=0),
                                            zero[:], None).then_inc(zeroed, 16)

                def store(j, u):
                    hold(pool, y_kept, j + 1)
                    pool.dma_start(t["y_d"][bass.ds(j * P, P), :], yb[:, u]).then_inc(y_out[u], 16)
                with pool.Fori(0, NMOE // 2) as i:
                    for u in range(2):
                        store(2 * i + u, u)
                for u in range(2):
                    pool.wait_ge(y_out[u], 16 * NMOE // 2)
                pool.wait_ge(rows_ok, 1)

                def gather(g, u):
                    if not isinstance(g, int) or g > 1:
                        hold(pool, fin, FIN * (g - 1))
                    pool.tensor_copy(now[:, u], yr_u[:, bass.ds(g * (G4 * TOPK), G4 * TOPK)]).then_inc(now_ok, 1)
                    hold(pool, now_ok, g + 1)
                    for c in range(G4 * TOPK):
                        pool.indirect_dma_start(gy[:, u, c, :], None, t["y_d"][:, :], bass.IndirectOffsetOnAxis(
                            ap=now[:, u, c:c + 1], axis=0)).then_inc(gy_in[u], 16)
                gather(0, 0)
                gather(1, 1)
                with pool.Fori(1, groups // 2) as i:
                    for u in range(2):
                        gather(2 * i + u, u)

            @block.tensor
            def _(pe):
                mm = nc.tensor.matmul
                pe.wait_ge(pool_c, 8)
                mm(ps_y[0][:, 0:NEXP], ones[:], m_acc[:], start=True, stop=True).then_inc(counted, 1)
                pe.wait_ge(w_in, 16 * 3 * NEXP)
                pe.wait_ge(tiles_ok, 2)

                def turn_x(j, u):
                    pe.wait_ge(x_in[u], 8 * (j - u) + 16)
                    need(pe, x_kept, j - 1)
                    for c in range(CH):
                        w = nc.tensor.transpose(ps_x[u][:, c * P:(c + 1) * P], xb[:, u, c * P:(c + 1) * P], ident[:])
                    w.then_inc(x_turned, 1)

                def expert(j):
                    return pe.value_load(ex_i[0:1, bass.ds(j, 1)], min_val=0, max_val=NEXP - 1)

                def gate_up(j, u):
                    e = expert(j)
                    pe.wait_ge(x_kept, j + 1)
                    need(pe, act_ok, j - 1)
                    for c in range(CH):
                        w = mm(ps_g[u][:], xt[:, u, c, :], wgu[:, bass.ds(e, 1), c, :], start=c == 0, stop=c == CH - 1)
                    w.then_inc(gu_mm, 1)

                def turn_act(j, u):
                    pe.wait_ge(act_ok, j + 1)
                    need(pe, a_kept, j - 1)
                    for c in range(CH):
                        w = nc.tensor.transpose(ps_a[u][:, c * P:(c + 1) * P], av[:, u, c * P:(c + 1) * P], ident[:])
                    w.then_inc(a_turned, 1)

                def down(j, u):
                    e = expert(j)
                    pe.wait_ge(a_kept, j + 1)
                    need(pe, y_kept, j - 1)
                    for c in range(CH):
                        w = mm(ps_y[u][:, 0:D], avt[:, u, c, :], wd[:, bass.ds(e, 1), c, :], start=c == 0, stop=c == CH - 1)
                    w.then_inc(y_mm, 1)
                turn_x(0, 0)
                turn_x(1, 1)
                gate_up(0, 0)

                def step(j, u):
                    turn_x(j + 1, 1 - u)
                    turn_act(j - 1, 1 - u)
                    gate_up(j, u)
                    down(j - 1, 1 - u)
                step(1, 1)
                step(2, 0)
                with pe.Fori(1, NMOE // 2 - 1) as i:
                    step(2 * i + 1, 1)
                    step(2 * i + 2, 0)
                j = NMOE - 1
                turn_act(j - 1, 0)
                gate_up(j, 1)
                down(j - 1, 0)
                turn_act(j, 1)
                down(j, 1)

            @block.scalar
            def _(act):
                A = nc.scalar.activation
                act.wait_ge(gap_ok, 1)
                A(ev[:], ev[:], ACT.Exp).then_inc(exps, 1)

                def keep_x(j, u):
                    act.wait_ge(x_turned, j + 1)
                    need(act, gu_mm, j - 1)
                    A(xt[:, u].rearrange("p c n -> p (c n)"), ps_x[u][:, 0:D], ACT.Copy).then_inc(x_kept, 1)

                def silu(j, u):
                    act.wait_ge(gu_mm, j + 1)
                    need(act, act_ok, j - 1)
                    A(sg[:, u], ps_g[u][:, 0:D], ACT.Silu).then_inc(silu_ok, 1)

                def keep_y(j, u):
                    act.wait_ge(y_mm, j + 1)
                    if not isinstance(j, int) or j > 1:
                        act.wait_ge(y_out[u], 8 * (j - u))
                    A(yb[:, u], ps_y[u][:, 0:D], ACT.Copy).then_inc(y_kept, 1)

                def step(j, u):
                    keep_x(j + 1, 1 - u)
                    silu(j, u)
                    keep_y(j - 1, 1 - u)
                keep_x(0, 0)
                keep_x(1, 1)
                silu(0, 0)
                step(1, 1)
                step(2, 0)
                with act.Fori(1, NMOE // 2 - 1) as i:
                    step(2 * i + 1, 1)
                    step(2 * i + 2, 0)
                j = NMOE - 1
                silu(j, 1)
                keep_y(j - 1, 0)
                keep_y(j, 1)

                def root(g, u):
                    act.wait_ge(fin, FIN * g + 4 * G4)
                    A(rstd[:, u], mv[:, u, :, 1], ACT.Sqrt, bias=eps[:, 0:1]).then_inc(rooted, 1)
                root(0, 0)
                root(1, 1)
                with act.Fori(1, groups // 2) as i:
                    for u in range(2):
                        root(2 * i + u, u)

            @block.vector
            def _(dve):
                V = nc.vector
                count = [0]

                def then(ins):
                    ins.then_inc(idx, 1)
                    count[0] += 1
                    dve.wait_ge(idx, count[0])
                dve.wait_ge(pool_c, 7)
                bc = lambda x, d, shape: x.unsqueeze(d).to_broadcast(shape)
                V.memset(eps[:], 1e-5).then_inc(idx, 1)
                V.tensor_copy(f8[:], i8[:]).then_inc(idx, 1)
                V.tensor_copy(ft[:], it[:]).then_inc(idx, 1)
                V.tensor_copy(f64[:], i64[:]).then_inc(idx, 1)
                V.tensor_copy(fp[:], ip[:]).then_inc(idx, 1)
                count[0] = 5
                dve.wait_ge(counted, 1)
                then(V.tensor_copy(cnt[:], ps_y[0][:, 0:NEXP]))
                then(V.scalar_tensor_tensor(pad[:], f8[:], float(CAP), cnt[:], ALU.mult, ALU.add))
                V.tensor_scalar(pad_u[:], pad[:], fp[:, 0:1], None, ALU.add).then_inc(pads_ok, 1)
                s = [P, NEXP, TILES]
                then(V.tensor_tensor(gt[:], bc(cnt[:], 2, s), bc(f64[:], 1, s), ALU.is_gt))
                then(V.tensor_reduce(tiles[:], gt[:], AX.X, ALU.add))
                s = [P, NEXP, NEXP]
                then(V.tensor_tensor(below[:], bc(f8[:], 2, s), bc(f8[:], 1, s), ALU.is_gt))
                then(V.tensor_tensor(below[:], below[:], bc(tiles[:], 1, s), ALU.mult))
                then(V.tensor_reduce(tbase[:], below[:], AX.X, ALU.add))
                then(V.tensor_tensor(tend[:], tbase[:], tiles[:], ALU.add))
                s = [P, NMOE, NEXP]
                then(V.tensor_tensor(ge[:], bc(ft[:], 2, s), bc(tend[:], 1, s), ALU.is_ge))
                then(V.tensor_reduce(ex[:], ge[:], AX.X, ALU.add))
                V.tensor_scalar(ex_i[:], ex[:], float(NEXP - 1), None, ALU.min).then_inc(tiles_ok, 1)
                then(V.tensor_tensor(ge[:], ge[:], bc(tiles[:], 1, s), ALU.mult))
                then(V.tensor_reduce(tb[:], ge[:], AX.X, ALU.add))
                then(V.tensor_tensor(tb[:], ft[:], tb[:], ALU.subtract))
                then(V.tensor_scalar(xrow[:], ex[:], float(CAP), None, ALU.mult))
                V.scalar_tensor_tensor(xrow_i[:], tb[:], float(P), xrow[:], ALU.mult, ALU.add).then_inc(tiles_ok, 1)
                t2 = top2[:].rearrange("p (t k) -> p t k", k=TOPK)
                V.tensor_tensor(ev[:], t2[:, :, 1], t2[:, :, 0], ALU.subtract).then_inc(gap_ok, 1)
                then(V.tensor_scalar(off[:], f8[:], -float(CAP), None, ALU.mult))
                then(V.scalar_tensor_tensor(off[:], tbase[:], float(P), off[:], ALU.mult, ALU.add))
                s = [P, TILES * TOPK, NEXP]
                then(V.tensor_tensor(oh[:], bc(eidx[:], 2, s), bc(f8[:], 1, s), ALU.is_equal))
                then(V.tensor_tensor(oh[:], oh[:], bc(off[:], 1, s), ALU.mult))
                then(V.tensor_reduce(yr[:], oh[:], AX.X, ALU.add))
                V.tensor_tensor(yr_u[:], yr[:], slotf[:], ALU.add).then_inc(rows_ok, 1)
                dve.wait_ge(exps, 1)
                then(V.tensor_scalar(den[:], ev[:], 1.0, None, ALU.add))
                then(V.reciprocal(den[:], den[:]))
                then(V.tensor_copy(wts[:, :, 0], den[:]))
                then(V.tensor_tensor(wts[:, :, 1], ev[:], den[:], ALU.mult))

                def gated(j, u):
                    dve.wait_ge(silu_ok, j + 1)
                    need(dve, a_turned, j - 1)
                    V.tensor_tensor(av[:, u], sg[:, u], ps_g[u][:, D:GU], ALU.mult).then_inc(act_ok, 1)

                def keep_a(j, u):
                    dve.wait_ge(a_turned, j + 1)
                    need(dve, y_mm, j - 1)
                    V.tensor_copy(avt[:, u].rearrange("p c n -> p (c n)"), ps_a[u][:, 0:D]).then_inc(a_kept, 1)
                gated(0, 0)

                def step(j, u):
                    keep_a(j - 1, 1 - u)
                    gated(j, u)
                step(1, 1)
                step(2, 0)
                with dve.Fori(1, NMOE // 2 - 1) as i:
                    step(2 * i + 1, 1)
                    step(2 * i + 2, 0)
                step(NMOE - 1, 1)
                keep_a(NMOE - 1, 1)

                def combine(g, u):
                    c = FIN * g
                    wt = wts[:].rearrange("p t k -> p (t k)")
                    dve.wait_ge(gy_in[u], 64 * (g - u) + 128)
                    dve.wait_ge(gx_in[u], 8 * (g - u) + 16)
                    for k in range(TOPK):
                        if k:
                            dve.wait_ge(fin, c + G4)
                        for j in range(G4):
                            V.scalar_tensor_tensor(gx[:, u, j], gy[:, u, j * TOPK + k],
                                                   wt[:, bass.ds(g * (G4 * TOPK) + j * TOPK + k, 1)], gx[:, u, j],
                                                   ALU.mult, ALU.add).then_inc(fin, 1)
                    for j in range(G4):
                        dve.wait_ge(fin, c + G4 + j + 1)
                        V.bn_stats(lbn[:, u, j], gx[:, u, j]).then_inc(fin, 1)
                    for j in range(G4):
                        hold(dve, fin, c + 2 * G4 + j + 1)
                        V.bn_aggr(mv[:, u, j], lbn[:, u, j]).then_inc(fin, 1)

                def combined(g, u):
                    c = FIN * g
                    dve.wait_ge(rooted, g + 1)
                    V.reciprocal(rstd[:, u], rstd[:, u]).then_inc(fin, 1)
                    dve.wait_ge(fin, c + 4 * G4 + 1)
                    for j in range(G4):
                        V.tensor_scalar(gx[:, u, j], gx[:, u, j], mv[:, u, j, 0:1], rstd[:, u, j:j + 1],
                                        ALU.subtract, ALU.mult).then_inc(fin, 1)

                def both(g, u):
                    combine(g, u)
                    combined(g, u)
                both(0, 0)
                both(1, 1)
                with dve.Fori(1, groups // 2) as i:
                    for u in range(2):
                        both(2 * i + u, u)


def post_norm_layer(nc, t):
    t = dict(t)
    for name, shape in (
        ("v_d", (TOKENS, D)), ("short_d", (TOKENS, D)), ("long_d", (TOKENS, D)), ("x1_d", (TOKENS, D)),
        ("scr_a", (NBLK, BLK, UNITS, BLK)), ("scr_x", (P, BLK, BLK)), ("scr_xt", (P, BLK, BLK)),
        ("xs_d", (SPARE + EXTRA * P, D)), ("y_d", (NMOE * P, D)),
    ):
        t[name] = nc.dram_tensor(name, shape, F32, kind="Internal").ap()
    with ExitStack() as ctx:
        def sb(name, shape, dt=F32):
            return ctx.enter_context(nc.sbuf_tensor(name, shape, dt))
        keep = {"eidx": sb("eidx", [P, TILES * TOPK]), "slotf": sb("slotf", [P, TILES * TOPK]),
                "top2": sb("top2", [P, TILES * TOPK]), "m_acc": sb("m_acc", [P, NEXP], BF16)}
        conv_and_fir(nc, t)
        delta_and_gate(nc, t, keep)
        experts_and_combine(nc, t, keep)


def kernel(**inputs):
    import numpy as np
    import concourse.bacc as bacc
    from concourse.bass_utils import run_bass_kernel_spmd

    def arr(name):
        return np.asarray(inputs[name])

    def turned(name):
        return np.ascontiguousarray(arr(name).T)
    x = np.ascontiguousarray(arr("L0_attn_hidden_states").reshape(TOKENS, D))
    fir_long = np.zeros((D, FPAD), x.dtype)
    fir_long[:, P - 1:P - 1 + FIR] = arr("L0_attn_fir_long_w").reshape(D, FIR)[:, ::-1]
    arrays = {
        "x": x, "xT": np.ascontiguousarray(x.T),
        "WqT": turned("L0_attn_Wq"), "WkT": turned("L0_attn_Wk"), "WvT": turned("L0_attn_Wv"),
        "WbT": turned("L0_attn_Wb"), "WoT": turned("L0_attn_Wo"),
        "qconv": arr("L0_attn_qconv_w"), "kconv": arr("L0_attn_kconv_w"), "vconv": arr("L0_attn_vconv_w"),
        "fir_short": np.ascontiguousarray(arr("L0_attn_fir_short_w").reshape(D, SHORT)), "fir_long": fir_long,
        "w1T": turned("L0_attn_gate_w1"), "w2T": turned("L0_attn_gate_w2"),
        "b1": np.ascontiguousarray(arr("L0_attn_gate_b1").reshape(HID_CH, P).T),
        "bias": np.ascontiguousarray(arr("L0_attn_base_bias").reshape(-1)),
        "floor": np.ascontiguousarray(arr("L0_attn_floor_raw").reshape(-1)),
        "log_temp": arr("L0_attn_log_temp"), "onorm": arr("L0_attn_onorm_w"),
        "rw": arr("L0_ffn_router_w"), "rb": arr("L0_ffn_router_b"),
        "we_gate": arr("L0_ffn_we_gate"), "we_up": arr("L0_ffn_we_up"), "we_down": arr("L0_ffn_we_down"),
    }
    nc = bacc.Bacc("TRN2", target_bir_lowering=False, num_devices=1)
    t = {name: nc.dram_tensor(name, a.shape, mybir.dt.from_np(a.dtype), kind="ExternalInput").ap()
         for name, a in arrays.items()}
    t["out"] = nc.dram_tensor("out", (TOKENS, D), F32, kind="ExternalOutput").ap()
    post_norm_layer(nc, t)
    r = run_bass_kernel_spmd(nc, [arrays], core_ids=[0])
    return r.results[0]["out"].reshape(BATCH, SEQ, D)
```

```python
from contextlib import ExitStack

import concourse.bass as bass
from concourse import mybir

F32 = mybir.dt.float32
F32R = mybir.dt.float32r
BF16 = mybir.dt.bfloat16
U32 = mybir.dt.uint32
I32 = mybir.dt.int32
ALU = mybir.AluOpType
ACT = mybir.ActivationFunctionType
AX = mybir.AxisListType

P = 128
BATCH, SEQ, D = 16, 512, 256
HEADS, DH = 4, 64
TOKENS = BATCH * SEQ
TILES = TOKENS // P
TPB = SEQ // P
CH = D // P
PAIRS = BATCH // 2
PT = 2 * TPB
PTOK = 2 * SEQ
FIR = 63
SHORT = 3
TAPS = 4
FPAD = 320
OCT = 8


def need(eng, sem, value):
    if isinstance(value, int) and value <= 0:
        return
    eng.wait_ge(sem, value)


def hold(eng, sem, value):
    need(eng, sem, value)
    if not isinstance(value, int):
        eng.nop(nofuse=True)


def back(it, g, k, per):
    q = g - k
    n = 0
    while q < 0:
        q += per
        n += 1
    return (it - n if n else it), q


def conv_and_fir(nc, t):
    UN = 4
    STEPS = BATCH // UN
    TB = 4
    OPC = P // OCT
    LAG_TURN, LAG_KEEP, LAG_FLIP, LAG_LONG, LAG_STORE = 3, 4, 5, 6, 5
    with ExitStack() as ctx:
        def sb(name, shape, dt=F32):
            return ctx.enter_context(nc.sbuf_tensor("A_" + name, shape, dt))

        def ps(name, shape):
            return ctx.enter_context(nc.psum_tensor("A_ps_" + name, shape, F32))

        def sem(name):
            return ctx.enter_context(nc.semaphore("A_" + name))

        v_back = sb("v_back", [P, TILES, D])
        long_sb = sb("long", [P, TILES, D])
        toep = sb("toep", [P, TB, OCT, 192])
        x_t = sb("x", [P, 2, CH, SEQ])
        wv = sb("wv", [P, CH, D])
        cw = sb("cw", [P, CH, TAPS])
        fw = sb("fw", [P, CH, SHORT])
        ident = sb("ident", [P, P])
        flip = sb("flip", [P, P])
        conv = sb("conv", [P, UN, SEQ])
        v_t = sb("v_t", [P, UN, SEQ])
        sh_t = sb("sh_t", [P, UN, SEQ])
        mid = sb("mid", [P, SEQ - 1])
        v_tok = sb("v_tok", [P, 2, TPB, P])
        sh_tok = sb("sh_tok", [P, 2, TPB, P])
        ps_x = [ps(f"x{i}", [P, SEQ]) for i in range(2)]
        ps_v = ps("v", [P, TPB, P])
        ps_r = ps("back", [P, TPB, P])
        ps_s = ps("short", [P, TPB, P])
        ps_f = [ps(f"f{i}", [P, OCT, TILES]) for i in range(2)]

        weights_in = sem("weights_in")
        x_in = [sem(f"x_in{i}") for i in range(2)]
        toep_in = [sem(f"toep_in{i}") for i in range(TB)]
        ident_ok = sem("ident_ok")
        projected = sem("projected")
        tap3 = sem("tap3")
        taps = sem("taps")
        v_ready = sem("v_ready")
        sh_start = sem("sh_start")
        sh_prod = sem("sh_prod")
        sh_mid = sem("sh_mid")
        sh_ready = sem("sh_ready")
        v_turned, sh_turned = sem("v_turned"), sem("sh_turned")
        v_kept, sh_kept = sem("v_kept"), sem("sh_kept")
        flipped = sem("flipped")
        back_kept = sem("back_kept")
        stored = [sem(f"stored{i}") for i in range(2)]
        fir_done = sem("fir_done")
        long_kept = [sem(f"long_kept{i}") for i in range(2)]
        long_out = sem("long_out")

        tok = lambda n: t[n].rearrange("(t p) c -> p t c", p=P)
        windows = bass.AP(t["fir_long"].tensor, 0, [[1, P], [FPAD, D], [1, 192]])

        def slots(eng, m, body, lag):
            for g in range(2 * UN):
                body(STEPS * m + g // UN, g % UN, lambda k, g=g: g >= k)
            with eng.Fori(STEPS * m + 2, STEPS * (m + 1)) as p:
                for g in range(UN):
                    body(p, g, lambda k: True)
            for g in range(lag):
                body(STEPS * (m + 1) + g // UN, g % UN, lambda k, g=g: k > g)

        with nc.Block() as block:
            @block.sync
            def _(sp):
                sp.dma_start(wv[:], t["WvT"].rearrange("(c p) n -> p c n", p=P)).then_inc(weights_in, 16)
                sp.dma_start(cw[:], t["vconv"].rearrange("(c p) k -> p c k", p=P)).then_inc(weights_in, 16)
                sp.dma_start(fw[:], t["fir_short"].rearrange("(c p) k -> p c k", p=P)).then_inc(weights_in, 16)
                xd = t["xT"].rearrange("(c p) n -> p c n", p=P)

                def chunk(m):
                    def slot(p, g, has):
                        if has(0):
                            need(sp, projected, UN * p + g - 1)
                            seq = (p - STEPS * m) * UN + g
                            sp.dma_start(x_t[:, g % 2], xd[:, :, bass.ds(seq * SEQ, SEQ)]).then_inc(x_in[g % 2], 16)
                        if has(LAG_STORE):
                            q, h = back(p, g, LAG_STORE, UN)
                            n = UN * q + h
                            rows = bass.ds(((q - STEPS * m) * UN + h) * TPB, TPB)
                            cols = slice(m * P, (m + 1) * P)
                            sp.wait_ge(v_kept, n + 1)
                            sp.dma_start(tok("v_d")[:, rows, cols], v_tok[:, h % 2]).then_inc(stored[h % 2], 16)
                            sp.wait_ge(sh_kept, n + 1)
                            sp.dma_start(tok("short_d")[:, rows, cols], sh_tok[:, h % 2]).then_inc(stored[h % 2], 16)
                    slots(sp, m, slot, LAG_STORE)
                for m in range(CH):
                    chunk(m)

                def store_long(c0, c1, pieces):
                    for k in long_kept:
                        sp.wait_ge(k, c1 // OCT // 2)
                    for q in range(pieces):
                        rows = slice(q * TILES // pieces, (q + 1) * TILES // pieces)
                        sp.dma_start(tok("long_d")[:, rows, c0:c1], long_sb[:, rows, c0:c1]).then_inc(long_out, 16)
                store_long(0, P, 4)
                store_long(P, P + P // 2, 2)
                store_long(P + P // 2, D, 2)
                sp.wait_ge(long_out, 16 * 8)
                for k in stored:
                    sp.wait_ge(k, 32 * BATCH)

            @block.gpsimd
            def _(pool):
                def load_toep(o, u):
                    pool.dma_start(toep[:, u], windows[:, bass.ds(o * OCT, OCT), :]).then_inc(toep_in[u], 16)
                pool.memset(ident[:], 0.0).then_inc(ident_ok, 1)
                pool.memset(flip[:], 0.0).then_inc(ident_ok, 1)
                pool.wait_ge(ident_ok, 2)
                pool.affine_select(out=ident[:], in_=ident[:], compare_op=ALU.not_equal, fill=1.0, base=0,
                                   pattern=[[-1, P]], channel_multiplier=1).then_inc(ident_ok, 1)
                pool.affine_select(out=flip[:], in_=flip[:], compare_op=ALU.not_equal, fill=1.0, base=1 - P,
                                   pattern=[[1, P]], channel_multiplier=1).then_inc(ident_ok, 1)
                for u in range(TB):
                    load_toep(u, u)
                pool.wait_ge(weights_in, 48)

                def chunk(m):
                    def slot(p, g, has):
                        if has(0):
                            n = UN * p + g
                            pool.wait_ge(sh_start, n + 1)
                            need(pool, sh_mid, n)
                            pool.tensor_tensor(mid[:], v_t[:, g, :SEQ - 1],
                                               fw[:, m, 1:2].to_broadcast([P, SEQ - 1]), ALU.mult).then_inc(sh_prod, 1)
                            pool.wait_ge(sh_prod, n + 1)
                            pool.tensor_tensor(sh_t[:, g, 1:], sh_t[:, g, 1:], mid[:], ALU.add).then_inc(sh_mid, 1)
                        if m and has(1):
                            q, h = back(p, g, 1, UN)
                            o = (q - STEPS) * UN + h
                            hold(pool, fir_done, o + 1)
                            load_toep(o + TB, h)
                    slots(pool, m, slot, 1 if m else 0)
                for m in range(CH):
                    chunk(m)
                with pool.Fori(OPC // TB, D // OCT // TB - 1) as k:
                    for u in range(TB):
                        hold(pool, fir_done, TB * k + u + 1)
                        load_toep(TB * (k + 1) + u, u)

            @block.tensor
            def _(pe):
                pe.wait_ge(weights_in, 48)
                pe.wait_ge(ident_ok, 4)
                byseq = v_back[:].rearrange("p (b t) c -> p b t c", t=TPB)

                def octet(k, u):
                    o = TB * k + u
                    pe.wait_ge(toep_in[u], 16 * (k + 1))
                    need(pe, long_kept[u % 2], TB // 2 * k + u // 2)
                    for c in range(OCT):
                        ch = o * OCT + c
                        nc.tensor.matmul(ps_f[u % 2][:, c, :], toep[:, u, c, 0:P],
                                         v_back[:, :, bass.ds(ch, 1)], start=True, stop=True)
                        out = ps_f[u % 2][0:64, c, :].rearrange("p (b t) -> p b t", t=TPB)[:, :, 1:TPB]
                        mm = nc.tensor.matmul(out, toep[:, u, c, P:192],
                                              byseq[:, :, 0:TPB - 1, bass.ds(ch, 1)], start=False, stop=True,
                                              skip_group_check=True)
                    mm.then_inc(fir_done, 1)

                def chunk(m):
                    def slot(p, g, has):
                        if has(0):
                            n = UN * p + g
                            pe.wait_ge(x_in[g % 2], 16 * (UN // 2 * p + g // 2 + 1))
                            need(pe, taps, 3 * (n - 1))
                            for c in range(CH):
                                mm = nc.tensor.matmul(ps_x[g % 2][:], wv[:, c, m * P:(m + 1) * P],
                                                      x_t[:, g % 2, c, :], start=c == 0, stop=c == CH - 1)
                            mm.then_inc(projected, 1)
                        if has(LAG_TURN):
                            q, h = back(p, g, LAG_TURN, UN)
                            n = UN * q + h
                            pe.wait_ge(v_ready, n + 1)
                            need(pe, v_kept, n)
                            for j in range(TPB):
                                mm = nc.tensor.transpose(ps_v[:, j, :], v_t[:, h, j * P:(j + 1) * P], ident[:])
                            mm.then_inc(v_turned, 1)
                            pe.wait_ge(sh_ready, n + 1)
                            need(pe, sh_kept, n)
                            for j in range(TPB):
                                mm = nc.tensor.transpose(ps_s[:, j, :], sh_t[:, h, j * P:(j + 1) * P], ident[:])
                            mm.then_inc(sh_turned, 1)
                        if has(LAG_FLIP):
                            q, h = back(p, g, LAG_FLIP, UN)
                            n = UN * q + h
                            pe.wait_ge(v_kept, n + 1)
                            need(pe, back_kept, n)
                            nc.tensor.matmul(ps_r[:], flip[:], v_tok[:, h % 2], start=True,
                                             stop=True).then_inc(flipped, 1)
                        if m and has(0):
                            octet(p - STEPS, g)
                    slots(pe, m, slot, LAG_FLIP)
                    pe.wait_ge(back_kept, BATCH * (m + 1))
                for m in range(CH):
                    chunk(m)
                with pe.Fori(OPC // TB, D // OCT // TB) as k:
                    for u in range(TB):
                        octet(k, u)

            def keep_long(eng, copy, k, u):
                o = TB * k + u
                eng.wait_ge(fir_done, o + 1)
                copy(long_sb[:, :, bass.ds(o * OCT, OCT)],
                     ps_f[u % 2][:].rearrange("p c t -> p t c")).then_inc(long_kept[u % 2], 1)

            @block.scalar
            def _(act):
                A = nc.scalar.activation
                act.wait_ge(weights_in, 48)

                def copy(out, in_):
                    return A(out, in_, ACT.Copy)

                def chunk(m):
                    def slot(p, g, has):
                        if has(LAG_KEEP):
                            q, h = back(p, g, LAG_KEEP, UN)
                            n = UN * q + h
                            act.wait_ge(v_turned, n + 1)
                            need(act, flipped, n - 1)
                            need(act, stored[h % 2], 32 * (UN // 2 * q + h // 2))
                            A(v_tok[:, h % 2], ps_v[:], ACT.Copy).then_inc(v_kept, 1)
                            act.wait_ge(sh_turned, n + 1)
                            A(sh_tok[:, h % 2], ps_s[:], ACT.Copy).then_inc(sh_kept, 1)
                        if has(0):
                            n = UN * p + g
                            act.wait_ge(projected, n + 1)
                            need(act, v_ready, n - UN + 1)
                            A(conv[:, g], ps_x[g % 2][:], ACT.Copy, scale=cw[:, m, 3:4]).then_inc(tap3, 1)
                        if has(1):
                            q, h = back(p, g, 1, UN)
                            n = UN * q + h
                            act.wait_ge(taps, 3 * (n + 1))
                            need(act, v_turned, n - UN + 1)
                            need(act, sh_turned, n - UN + 1)
                            A(v_t[:, h], conv[:, h], ACT.Silu).then_inc(v_ready, 1)
                            act.wait_ge(v_ready, n + 1)
                            A(sh_t[:, h], v_t[:, h], ACT.Copy, scale=fw[:, m, 2:3]).then_inc(sh_start, 1)
                        if m and has(1):
                            q, h = back(p, g, 1, UN)
                            if h % 2:
                                keep_long(act, copy, q - STEPS, h)
                    slots(act, m, slot, LAG_KEEP)
                for m in range(CH):
                    chunk(m)
                with act.Fori(OPC // TB, D // OCT // TB) as k:
                    for u in range(1, TB, 2):
                        keep_long(act, copy, k, u)

            @block.vector
            def _(dve):
                dve.wait_ge(weights_in, 48)

                def chunk(m):
                    def slot(p, g, has):
                        if has(LAG_LONG):
                            q, h = back(p, g, LAG_LONG, UN)
                            dve.wait_ge(flipped, UN * q + h + 1)
                            rows = bass.ds(((q - STEPS * m) * UN + h) * TPB, TPB)
                            nc.vector.tensor_copy(v_back[:, rows, m * P:(m + 1) * P], ps_r[:]).then_inc(back_kept, 1)
                        if has(2):
                            q, h = back(p, g, 2, UN)
                            dve.wait_ge(sh_mid, UN * q + h + 1)
                            nc.vector.scalar_tensor_tensor(
                                sh_t[:, h, 2:], v_t[:, h, :SEQ - 2], fw[:, m, 0:1], sh_t[:, h, 2:],
                                ALU.mult, ALU.add).then_inc(sh_ready, 1)
                        if has(0):
                            n = UN * p + g
                            dve.wait_ge(tap3, n + 1)
                            for k in range(1, TAPS):
                                need(dve, taps, 3 * n + k - 1)
                                nc.vector.scalar_tensor_tensor(
                                    conv[:, g, k:], ps_x[g % 2][:, :SEQ - k], cw[:, m, 3 - k:4 - k],
                                    conv[:, g, k:], ALU.mult, ALU.add).then_inc(taps, 1)
                        if m and has(1):
                            q, h = back(p, g, 1, UN)
                            if h % 2 == 0:
                                keep_long(dve, nc.vector.tensor_copy, q - STEPS, h)
                    slots(dve, m, slot, LAG_LONG)
                for m in range(CH):
                    chunk(m)
                with dve.Fori(OPC // TB, D // OCT // TB) as k:
                    for u in range(0, TB, 2):
                        keep_long(dve, nc.vector.tensor_copy, k, u)


NEXP, TOPK = 8, 2
CAP = TOKENS + P
GATE_HID = 512
STATS = 32
PATHS = 4
HID_CH = GATE_HID // P
BLK = 32
NBLK = P // BLK
UNITS = PT * HEADS
ROW = D + 8
TOK2, SECOND = D, D + 1


def dispatch(pool, t, x1, slot_u, done):
    for b in range(2):
        for j in range(TPB):
            for k in range(TOPK):
                c = (b * TPB + j) * TOPK + k
                pool.indirect_dma_start(t["xs_d"][:, :], bass.IndirectOffsetOnAxis(ap=slot_u[:, c:c + 1], axis=0),
                                        x1[:, b, j, :], None).then_inc(done[b], 16)


def delta_and_gate(nc, t, keep):
    with ExitStack() as ctx:
        def sb(name, shape, dt=F32):
            return ctx.enter_context(nc.sbuf_tensor("B_" + name, shape, dt))

        def ps(name, shape=(P, 512)):
            return ctx.enter_context(nc.psum_tensor("B_ps_" + name, list(shape), F32))

        def sem(name):
            return ctx.enter_context(nc.semaphore("B_" + name))

        wq = sb("wq", [P, CH, D]); wk = sb("wk", [P, CH, D]); wb = sb("wb", [P, CH, HEADS])
        cw = sb("cw", [P, 2, CH, TAPS])
        w1x = sb("w1x", [P, CH, GATE_HID]); w1s = sb("w1s", [STATS, GATE_HID])
        b1 = sb("b1", [P, HID_CH]); w2 = sb("w2", [P, HID_CH, HEADS * PATHS])
        wo = sb("wo", [P, CH, D]); onw = sb("onw", [P, 1])
        rw = sb("rw", [P, CH, NEXP]); rb = sb("rb", [P, NEXP])
        bias16 = sb("bias16", [P, 16]); floor16 = sb("floor16", [P, 16]); itemp = sb("itemp", [P, HEADS])
        ident = sb("ident", [P, P]); upper = sb("upper", [P, P])
        before = sb("before", [P, P], BF16); ones = sb("ones", [P, P], BF16)
        headsel = sb("headsel", [P, 2]); iota8 = sb("iota8", [P, NEXP]); base8 = sb("base8", [P, NEXP])
        eps6 = sb("eps6", [P, 1]); eps5 = sb("eps5", [P, 1])
        xa = sb("xa", [P, CH, PTOK])
        conv = sb("conv", [P, 2, SEQ]); sq = sb("sq", [P, 2, SEQ])
        kraw = sb("kraw", [P, CH, PTOK]); k_t = sb("k_t", [P, CH, PTOK]); q_t = sb("q_t", [P, CH, PTOK])
        k_tok = sb("k_tok", [P, PT, D])
        nrm = sb("nrm", [P, 2, PT * HEADS]); rn = sb("rn", [P, 2, PT * HEADS])
        th = sb("th", [P, PT * HEADS]); beta = sb("beta", [P, PT, HEADS]); nbeta = sb("nbeta", [P, PT, HEADS])
        area = keep["area"][:].rearrange("p (a t h s) -> p a t h s", a=3, t=PT, h=HEADS)
        a_sb, at_t = area[:, 0], area[:, 1]
        mt = area[:, 2].rearrange("p t h s -> p (t h) s")
        z = sb("z", [P, BLK, BLK]); zt = sb("zt", [P, BLK, BLK])
        xf = sb("xf", [P, UNITS, 2 * BLK])
        s_bd = sb("s_bd", [P, 4, P])
        r_sb = sb("r_sb", [P, 2, HEADS, DH]); u_sb = sb("u_sb", [P, 2, HEADS, DH])
        v_tok = sb("v_tok", [P, PT, D]); delta = sb("delta", [P, PT, D])
        xg = sb("xg", [P, CH, SEQ])
        sh = sb("sh", [P, 2, TPB, D]); lo = sb("lo", [P, 2, TPB, D]); x1, slot_u = keep["x1"], keep["slot_u"]
        hid = sb("hid", [P, HID_CH, SEQ])
        bnst = sb("bn", [P, PT, PATHS, HEADS, 6]); dm = sb("dm", [P, PT, STATS // 2]); gst = sb("gst", [P, PT, STATS])
        st_t = sb("st_t", [STATS, SEQ])
        lg = sb("lg", [P, UNITS, PATHS]); s32 = sb("s32", [P, UNITS]); r32 = sb("r32", [P, UNITS])
        o_t = sb("o_t", [P, 2, CH, SEQ])
        lbn = sb("lbn", [P, PT, 6]); mv = sb("mv", [P, PT, 2]); rstd = sb("rstd", [P, PT]); shift = sb("shift", [P, PT])
        rl = sb("rl", [P, PT, NEXP]); mx8 = sb("mx8", [P, PT, 8]); mi8 = sb("mi8", [P, PT, 8], U32)
        ef = sb("ef", [P, PT * TOPK]); oh = sb("oh", [P, PT * TOPK, NEXP])
        m_bf = sb("m_bf", [P, PT, NEXP], BF16); m_sum = sb("m_sum", [P, NEXP])
        tok2 = sb("tok2", [P, PT]); slot_f = sb("slot_f", [P, PT * TOPK])
        rk = sb("rk", [P, PT, NEXP])
        z1 = conv[:].rearrange("p c (a b) -> p (c a) b", b=BLK)
        tmp = kraw[:, 0, :].rearrange("p (t c) -> p t c", c=D)
        squares = sq[:].rearrange("p c (a b) -> p (c a) b", b=D)
        z2 = hid[:].rearrange("p c (a b) -> p (c a) b", b=2 * BLK)

        X = [ps("x0"), ps("x1")]
        B2, B3, B4, B5, SM, TR = (ps(n) for n in ("b2", "b3", "b4", "b5", "small", "turn"))

        w_in = sem("weights_in"); pool_c = sem("pool_const"); dve_c = sem("dve_const"); act_c = sem("act_const")
        xa_in, xg_in = sem("xa_in"), sem("xg_in")
        v_in = sem("v_in")
        sl_in = [sem(f"short_long_in{i}") for i in range(2)]; x_in = [sem(f"x_in{i}") for i in range(2)]
        projected, tap3, taps, raw = sem("projected"), sem("tap3"), sem("taps"), sem("silu_done")
        squared, selected = sem("squared"), sem("selected")
        beta_mm, beta_th, beta_ok = sem("beta_mm"), sem("beta_th"), sem("beta_ok")
        rooted, rn_ok = sem("norm_rooted"), sem("norm_ok")
        k_turned, k_kept, k_back, kt_kept = sem("k_turned"), sem("k_kept"), sem("k_back"), sem("kt_kept")
        a_mm, a_kept, at_mm, at_kept = sem("a_mm"), sem("a_kept"), sem("at_mm"), sem("at_kept")
        a_out, z_in, masked, solve, zt_ok = sem("a_out"), sem("z_in"), sem("z_masked"), sem("solve"), sem("zt_ok")
        x_out, x_back = sem("x_out"), sem("x_back")
        m_pe, m_dve, m_act = sem("merge_pe"), sem("merge_dve"), sem("merge_act")
        s_zero, r_p, r_q, r_r1, r_r, r_u, r_ub = (sem(n) for n in (
            "s_zero", "rec_p", "rec_q", "rec_r1", "rec_r", "rec_u", "rec_ub"))
        r_sx, r_s, r_o, r_out = sem("rec_sx"), sem("rec_s"), sem("rec_o"), sem("rec_out")
        st_dve, st_turned, st_kept = sem("stats_dve"), sem("stats_turned"), sem("stats_kept")
        gate_mm, gelu_ok, logit_mm = sem("gate_mm"), sem("gelu_ok"), sem("logit_mm")
        sm_dve, sm_exp = sem("softmax_dve"), sem("softmax_exp")
        mixp, mix = sem("mix_pool"), [sem(f"mix_dve{i}") for i in range(2)]
        sq_ok, rms_rt = sem("rms_squared"), sem("rms_rooted")
        o_turned, o_kept, wo_mm = sem("o_turned"), sem("o_kept"), sem("wo_mm")
        ln, ln_rt, x1_ok = sem("ln_dve"), sem("ln_rooted"), sem("x1_normed")
        x1_turned, x1_kept, rt_mm = sem("x1_turned"), sem("x1_kept"), sem("router_mm")
        rt, ranked, carried = sem("route_dve"), sem("ranked"), sem("carried")
        scattered = [sem(f"scattered{i}") for i in range(2)]; x1_out = [sem(f"x1_out{i}") for i in range(2)]

        xd = t["xT"].rearrange("(c p) n -> p c n", p=P)
        tok = lambda n: t[n].rearrange("(t p) c -> p t c", p=P)
        POOL_C = 14
        SOLVE = 2 * (BLK - 2)
        LN, RT = 8, 13
        tails = (TR, B3)
        top2, m_acc = keep["top2"], keep["m_acc"]

        def hp(h):
            return slice((h % 2) * DH, (h % 2 + 1) * DH)

        with nc.Block() as block:
            @block.sync
            def _(sp):
                bc = lambda name, n: t[name].rearrange("(o n) -> o n", o=1).to_broadcast([P, n])
                rows = lambda name: t[name].rearrange("(c p) n -> p c n", p=P)
                for dst, src in (
                    (wq[:], rows("WqT")), (wk[:], rows("WkT")), (wb[:], rows("WbT")),
                    (cw[:, 0], rows("kconv")), (cw[:, 1], rows("qconv")),
                    (w1x[:], t["w1T"][0:D, :].rearrange("(c p) n -> p c n", p=P)), (w1s[:], t["w1T"][D:D + STATS, :]),
                    (b1[:], t["b1"]), (w2[:], rows("w2T")), (wo[:], rows("WoT")),
                    (onw[0:DH, :], t["onorm"].rearrange("(p o) -> p o", o=1)),
                    (onw[DH:P, :], t["onorm"].rearrange("(p o) -> p o", o=1)),
                    (rw[:], rows("rw")), (rb[:], bc("rb", NEXP)), (bias16[:], bc("bias", 16)),
                    (floor16[:], bc("floor", 16)), (itemp[:], bc("log_temp", HEADS)),
                ):
                    sp.dma_start(dst, src).then_inc(w_in, 16)

                def load_xa(p):
                    hold(sp, beta_mm, p)
                    hold(sp, projected, 8 * p)
                    sp.dma_start(xa[:], xd[:, :, bass.ds(p * PTOK, PTOK)]).then_inc(xa_in, 16)

                def load_paths(i):
                    hold(sp, o_turned, 4 * i)
                    for b in range(2):
                        r = bass.ds(i * PT + b * TPB, TPB)
                        sp.dma_start(sh[:, b], tok("short_d")[:, r, :]).then_inc(sl_in[b], 16)
                        sp.dma_start(lo[:, b], tok("long_d")[:, r, :]).then_inc(sl_in[b], 16)

                def load_x1(i):
                    for b in range(2):
                        hold(sp, scattered[b], 16 * 8 * i)
                        hold(sp, x1_out[b], 16 * i)
                        r = bass.ds(i * PT + b * TPB, TPB)
                        sp.dma_start(x1[:, b, :, 0:D], tok("x")[:, r, :]).then_inc(x_in[b], 16)

                def load_xg(i, b):
                    hold(sp, gate_mm, 4 * (2 * i + b))
                    sp.dma_start(xg[:], xd[:, :, bass.ds(i * PTOK + b * SEQ, SEQ)]).then_inc(xg_in, 16)

                def load_v(i):
                    hold(sp, mixp, 6 * i)
                    hold(sp, st_dve, 7 * i)
                    sp.dma_start(v_tok[:], tok("v_d")[:, bass.ds(i * PT, PT), :]).then_inc(v_in, 16)

                def solve_dmas(p):
                    hold(sp, a_kept, 8 * (p + 1))
                    for k in range(NBLK):
                        s = slice(k * BLK, (k + 1) * BLK)
                        sp.dma_start(t["scr_a"][k], a_sb[s, :, :, s].rearrange("i t h k -> i (t h) k")).then_inc(a_out, 16)
                    hold(sp, a_out, 64 * (p + 1))
                    for k in range(NBLK):
                        sp.dma_start(z[k * BLK:(k + 1) * BLK], t["scr_a"][k].rearrange("i u k -> u i k")).then_inc(z_in, 16)

                def solved_dmas(p):
                    hold(sp, zt_ok, p + 1)
                    sp.dma_start(t["scr_x"][:], z[:]).then_inc(x_out, 16)
                    sp.dma_start(t["scr_xt"][:], zt[:]).then_inc(x_out, 16)
                    hold(sp, x_out, 32 * (p + 1))
                    for k in range(NBLK):
                        s = slice(k * BLK, (k + 1) * BLK)
                        c = (k % 2) * BLK
                        sp.dma_start(xf[s, :, c:c + BLK], t["scr_x"][s].rearrange("u i k -> i u k")).then_inc(x_back, 16)
                        sp.dma_start(mt[s, :, s], t["scr_xt"][s].rearrange("u k i -> k u i")).then_inc(x_back, 16)

                def store_x1(i):
                    hold(sp, x1_ok, i + 1)
                    for b in range(2):
                        sp.dma_start(tok("x1_d")[:, bass.ds(i * PT + b * TPB, TPB), :], x1[:, b, :, 0:D]).then_inc(x1_out[b], 16)

                load_xa(0)
                load_v(0)
                load_paths(0)
                solve_dmas(0)
                solved_dmas(0)
                load_xa(1)

                def step(i, has_prev, has_next, has_after):
                    load_xg(i, 0)
                    if has_prev:
                        store_x1(i - 1)
                    if has_next:
                        solve_dmas(i + 1)
                    load_xg(i, 1)
                    if has_next:
                        solved_dmas(i + 1)
                    if has_after:
                        load_xa(i + 2)
                    if has_next:
                        load_v(i + 1)
                    load_x1(i)
                    if has_next:
                        load_paths(i + 1)
                step(0, False, True, True)
                with sp.Fori(1, PAIRS - 2) as i:
                    step(i, True, True, True)
                step(PAIRS - 2, True, True, False)
                step(PAIRS - 1, True, False, False)
                sp.wait_ge(r_out, 4 * PAIRS)
                for dst, name in ((keep["wg"], "we_gate"), (keep["wu"], "we_up"), (keep["wd"], "we_down")):
                    for e in range(NEXP):
                        sp.dma_start(dst[:, e], t[name][e].rearrange("(c p) n -> p c n", p=P)).then_inc(keep["experts_in"], 16)
                store_x1(PAIRS - 1)
                for b in range(2):
                    hold(sp, x1_out[b], 16 * PAIRS)

            @block.gpsimd
            def _(pool):
                pool.memset(ident[:], 0.0).then_inc(pool_c, 1)
                pool.memset(upper[:], 1.0).then_inc(pool_c, 1)
                pool.memset(before[:], 1.0).then_inc(pool_c, 1)
                pool.memset(ones[:], 1.0).then_inc(pool_c, 1)
                pool.memset(headsel[:], 1.0).then_inc(pool_c, 1)
                pool.iota(mi8[:, 0, :], [[1, NEXP]], base=0, channel_multiplier=0).then_inc(pool_c, 1)
                pool.iota(mi8[:, 1, :], [[2 * P, PT]], base=0, channel_multiplier=2).then_inc(pool_c, 1)
                pool.memset(x1[:], 0.0).then_inc(pool_c, 1)
                pool.wait_ge(pool_c, 8)
                pool.affine_select(out=ident[:], in_=ident[:], compare_op=ALU.not_equal, fill=1.0, base=0,
                                   pattern=[[-1, P]], channel_multiplier=1).then_inc(pool_c, 1)
                pool.affine_select(out=upper[:], in_=upper[:], compare_op=ALU.is_ge, fill=0.0, base=0,
                                   pattern=[[1, P]], channel_multiplier=-1).then_inc(pool_c, 1)
                pool.affine_select(out=before[:], in_=before[:], compare_op=ALU.is_gt, fill=0.0, base=0,
                                   pattern=[[1, P]], channel_multiplier=-1).then_inc(pool_c, 1)
                pool.affine_select(out=headsel[:, 0:1], in_=headsel[:, 0:1], compare_op=ALU.is_gt, fill=0.0, base=DH,
                                   pattern=[[0, 1]], channel_multiplier=-1).then_inc(pool_c, 1)
                pool.affine_select(out=headsel[:, 1:2], in_=headsel[:, 1:2], compare_op=ALU.is_ge, fill=0.0, base=-DH,
                                   pattern=[[0, 1]], channel_multiplier=1).then_inc(pool_c, 1)
                pool.memset(m_acc[:], 0.0).then_inc(pool_c, 1)

                def zero_state(p):
                    need(pool, r_q, 4 * p)
                    pool.nop(nofuse=True)
                    pool.memset(s_bd[:], 0.0).then_inc(s_zero, 1)

                def mask_blocks(p):
                    pool.wait_ge(z_in, 64 * (p + 1))
                    pool.nop(nofuse=True)
                    pool.affine_select(out=z[:], in_=z[:], compare_op=ALU.is_gt, fill=0.0, base=0,
                                       pattern=[[1, BLK], [-1, BLK]], channel_multiplier=0).then_inc(masked, 1)
                    pool.wait_ge(masked, 2 * p + 1)
                    pool.nop(nofuse=True)
                    pool.affine_select(out=z[:], in_=z[:], compare_op=ALU.not_equal, fill=1.0, base=0,
                                       pattern=[[1, BLK], [-1, BLK]], channel_multiplier=0).then_inc(masked, 1)

                def mix_pool(i, b):
                    half = 2 * i + b
                    p3 = lambda k: lg[:, 16 * b:16 * b + 16, k:k + 1].to_broadcast([P, 16, DH])
                    v3 = lambda x: x.rearrange("p t (h d) -> p (t h) d", d=DH)
                    pool.wait_ge(sm_dve, 11 * (i + 1))
                    pool.wait_ge(st_dve, 7 * (i + 1))
                    need(pool, mixp, 3 * half)
                    pool.tensor_tensor(v3(tmp[:]), v3(v_tok[:, b * TPB:(b + 1) * TPB]), p3(3), ALU.mult).then_inc(mixp, 1)
                    pool.tensor_tensor(v3(sh[:, b]), v3(sh[:, b]), p3(0), ALU.mult).then_inc(mixp, 1)
                    pool.wait_ge(mixp, 3 * half + 2)
                    pool.tensor_tensor(sh[:, b], sh[:, b], tmp[:], ALU.add).then_inc(mixp, 1)

                def scatter(i):
                    pool.wait_ge(rt, RT * (i + 1))
                    pool.nop(nofuse=True)
                    dispatch(pool, t, x1, slot_u, scattered)

                pool.memset(mt[:], 0.0).then_inc(pool_c, 1)
                pool.memset(xf[:], 0.0).then_inc(pool_c, 1)
                zero_state(0)
                pool.wait_ge(pool_c, POOL_C + 2)
                mask_blocks(0)

                def step(i, has_prev, has_next):
                    if has_prev:
                        scatter(i - 1)
                    if has_next:
                        zero_state(i + 1)
                        mask_blocks(i + 1)
                    for b in range(2):
                        mix_pool(i, b)
                step(0, False, True)
                with pool.Fori(1, PAIRS - 1) as i:
                    step(i, True, True)
                step(PAIRS - 1, True, False)
                for b in range(2):
                    pool.wait_ge(scattered[b], 16 * 8 * (PAIRS - 1))

            @block.tensor
            def _(pe):
                mm = nc.tensor.matmul
                pe.wait_ge(w_in, 16 * 17)
                pe.wait_ge(pool_c, POOL_C + 2)
                pe.wait_ge(dve_c, 8)

                def project(p, g):
                    gg = g % 4
                    b, m = gg // CH, gg % CH
                    w = wk if g < 4 else wq
                    if g == 0:
                        pe.wait_ge(xa_in, 16 * (p + 1))
                    if g < 2:
                        need(pe, gelu_ok, 8 * (p - 1))
                    else:
                        pe.wait_ge(taps, 24 * p + 3 * (g - 1))
                    for c in range(CH):
                        i = mm(X[g % 2][:], w[:, c, m * P:(m + 1) * P], xa[:, c, b * SEQ:(b + 1) * SEQ],
                               start=c == 0, stop=c == CH - 1)
                    i.then_inc(projected, 1)

                def select(p, g):
                    kq, gg = g // 4, g % 4
                    b, m = gg // CH, gg % CH
                    pe.wait_ge(squared, 8 * p + g + 1)
                    for j in range(TPB):
                        c = kq * 32 + (b * TPB + j) * HEADS + m * 2
                        i = mm(SM[:, c:c + 2], sq[:, g % 2, j * P:(j + 1) * P], headsel[:], start=True, stop=True)
                    i.then_inc(selected, 1)

                def betas(p):
                    for j in range(PT):
                        for c in range(CH):
                            i = mm(SM[:, 64 + 4 * j:68 + 4 * j], xa[:, c, j * P:(j + 1) * P], wb[:, c, :],
                                   start=c == 0, stop=c == CH - 1)
                    i.then_inc(beta_mm, 1)

                def turn_k(p, j):
                    b, m = j // CH, j % CH
                    for q in range(TPB):
                        s = slice((b * TPB + q) * P, (b * TPB + q + 1) * P)
                        i = nc.tensor.transpose((TR, B2)[j % 2][:, q * P:(q + 1) * P], kraw[:, m, s], ident[:])
                    i.then_inc(k_turned, 1)

                def stage1b(p, last=None):
                    select(p, 3)
                    turn_k(p, 0)
                    turn_k(p, 1)
                    project(p, 4)
                    pe.wait_ge(rooted, 2 * p + 1)
                    betas(p)
                    if last is not None:
                        router(last)
                    project(p, 5)
                    for j in (2, 3):
                        pe.wait_ge(k_kept, 4 * p + j - 1)
                        turn_k(p, j)
                    if last is not None:
                        rank(last)
                    for j in range(4):
                        b, m = j // CH, j % CH
                        pe.wait_ge(k_kept, 4 * p + j + 1)
                        if j == 1 and last is not None:
                            pe.wait_ge(rt, RT * last + 8)
                        if j >= 2:
                            pe.wait_ge(kt_kept, 4 * p + j - 1)
                        for q in range(TPB):
                            i = nc.tensor.transpose((B5, B3)[j % 2][:, q * P:(q + 1) * P],
                                                    k_tok[:, b * TPB + q, m * P:(m + 1) * P], ident[:])
                        i.then_inc(k_back, 1)
                    pe.wait_ge(beta_th, p + 1)
                    select(p, 4)
                    project(p, 6)
                    select(p, 5)
                    project(p, 7)
                    quad = (B2, B3, B4, B5)
                    pe.wait_ge(kt_kept, 4 * (p + 1))
                    for jj in range(PT // 2):
                        if jj == 1:
                            need(pe, r_out, 4 * p)
                        if jj >= 2:
                            pe.wait_ge(a_kept, 8 * p + 2 * (jj - 1))
                        for c in range(4):
                            s = slice((2 * jj + c // 2) * P, (2 * jj + c // 2 + 1) * P)
                            for par in range(2):
                                kk = k_t[hp(par), c % 2, s]
                                i = mm(quad[2 * (jj % 2) + par][:, c * P:(c + 1) * P], kk, kk, start=True, stop=True)
                                if c == 3:
                                    i.then_inc(a_mm, 1)
                    select(p, 6)
                    select(p, 7)
                    for jj in range(PT // 2):
                        if jj < 2:
                            pe.wait_ge(a_kept, 8 * p + 6 + 2 * jj)
                        else:
                            pe.wait_ge(at_kept, 8 * p + 2 * (jj - 1))
                        for c in range(4):
                            s = slice((2 * jj + c // 2) * P, (2 * jj + c // 2 + 1) * P)
                            for par in range(2):
                                i = mm(quad[2 * (jj % 2) + par][:, c * P:(c + 1) * P], k_t[hp(par), c % 2, s],
                                       q_t[hp(par), c % 2, s], start=True, stop=True)
                                if c == 3:
                                    i.then_inc(at_mm, 1)

                def merges(i):
                    pe.wait_ge(x_back, 128 * (i + 1))
                    pe.wait_ge(a_kept, 8 * (i + 1))
                    pe.wait_ge(at_kept, 8 * (i + 1))
                    pe.nop(nofuse=True)
                    for bank, u0 in ((B2, 0), (B3, 16)):
                        for u in range(u0, u0 + 16):
                            for q in range(2):
                                lo_, hi = q * 64, q * 64 + 32
                                w = mm(bank[lo_:lo_ + 32, (u - u0) * 32:(u - u0 + 1) * 32],
                                       a_sb[hi:hi + 32, u // 4, u % 4, lo_:lo_ + 32], mt[hi:hi + 32, u, hi:hi + 32],
                                       start=True, stop=True)
                        w.then_inc(m_pe, 1)
                    pe.wait_ge(m_dve, 9 * i + 2)
                    pe.wait_ge(m_act, 9 * i + 2)
                    pe.nop(nofuse=True)
                    for bank, u0 in ((B4, 0), (B5, 16)):
                        for u in range(u0, u0 + 16):
                            for q in range(2):
                                s = slice(q * 64, q * 64 + 32)
                                w = mm(bank[s, (u - u0) * 32:(u - u0 + 1) * 32], xf[s, u, 0:32], z1[s, u, :],
                                       start=True, stop=True)
                        w.then_inc(m_pe, 1)
                    for bank, u0 in ((B2, 0), (B3, 16)):
                        for u in range(u0, u0 + 16):
                            w = mm(bank[32:64, (u - u0) * 32:(u - u0 + 1) * 32], z1[0:32, u, :], xf[0:32, u, 0:32],
                                   start=True, stop=True)
                        w.then_inc(m_pe, 1)
                    pe.wait_ge(m_dve, 9 * i + 5)
                    pe.wait_ge(m_act, 9 * i + 5)
                    pe.nop(nofuse=True)
                    for n_, bank in enumerate((B4, B5, B2, B3)):
                        for u in range(8 * n_, 8 * n_ + 8):
                            w = mm(bank[0:64, (u % 8) * 64:(u % 8 + 1) * 64], a_sb[64:128, u // 4, u % 4, 0:64],
                                   mt[64:128, u, 64:128], start=True, stop=True)
                        w.then_inc(m_pe, 1)
                    pe.wait_ge(m_dve, 9 * i + 7)
                    pe.wait_ge(m_act, 9 * i + 7)
                    pe.nop(nofuse=True)
                    for n_, bank in enumerate((B4, B5, B2, B3)):
                        for u in range(8 * n_, 8 * n_ + 8):
                            w = mm(bank[0:64, (u % 8) * 64:(u % 8 + 1) * 64], xf[0:64, u, :], z2[0:64, u, :],
                                   start=True, stop=True)
                        w.then_inc(m_pe, 1)
                    pe.wait_ge(m_dve, 9 * (i + 1))
                    pe.wait_ge(m_act, 9 * (i + 1))

                def recur(i, has_prev, has_next):
                    pe.wait_ge(s_zero, i + 1)
                    for s in range(TPB):
                        if s:
                            pe.wait_ge(r_s, 6 * i + 2 * s)
                        for c in range(4):
                            b, m = c // 2, c % 2
                            tl = slice((b * TPB + s) * P, (b * TPB + s + 1) * P)
                            w = mm(B2[:, c * P:(c + 1) * P], k_t[:, m, tl], s_bd[:, c, :], start=True, stop=True)
                        w.then_inc(r_p, 1)
                        if s:
                            pe.wait_ge(r_out, 4 * i + s)
                        for c in range(4):
                            b, m = c // 2, c % 2
                            tl = slice((b * TPB + s) * P, (b * TPB + s + 1) * P)
                            w = mm(B4[:, c * P:(c + 1) * P], q_t[:, m, tl], s_bd[:, c, :], start=c == 0, stop=False,
                                   skip_group_check=True)
                        w.then_inc(r_q, 1)
                        if has_next:
                            project(i + 1, s)
                            if s:
                                select(i + 1, s - 1)
                        if has_prev and s == 0:
                            project_out(i - 1, 0)
                        if has_prev and s == 3:
                            turn_x1(i - 1, 0)
                        pe.wait_ge(r_r, 4 * i + s + 1)
                        for c in range(8):
                            b, h = c // 4, c % 4
                            w = mm(B2[:, c * DH:(c + 1) * DH], mt[:, (b * TPB + s) * HEADS + h, :], r_sb[:, b, h, :],
                                   start=True, stop=True)
                        w.then_inc(r_u, 1)
                        if has_prev and s == 3:
                            turn_x1(i - 1, 1)
                        pe.wait_ge(r_ub, 4 * i + s + 1)
                        if s < TPB - 1:
                            for c in range(4):
                                b, m = c // 2, c % 2
                                w = mm(B5[:, c * P:(c + 1) * P], k_tok[:, b * TPB + s, m * P:(m + 1) * P],
                                       u_sb[:, b, 2 * m:2 * m + 2, :], start=True, stop=True)
                            w.then_inc(r_sx, 1)
                        for c in range(8):
                            b, h = c // 4, c % 4
                            w = mm(B4[:, c * DH:(c + 1) * DH], at_t[:, b * TPB + s, h, :], u_sb[:, b, h, :],
                                   start=False, stop=c == 7, skip_group_check=True)
                        w.then_inc(r_o, 1)
                        if has_prev and s == 0:
                            project_out(i - 1, 1)

                def gate(i, b, has_next):
                    half = 2 * i + b
                    pe.wait_ge(st_dve, 7 * (i + 1))
                    for j in range(TPB):
                        w = nc.tensor.transpose(TR[0:STATS, j * P:(j + 1) * P], gst[:, b * TPB + j, :], ident[:])
                    w.then_inc(st_turned, 1)
                    pe.wait_ge(xg_in, 16 * (half + 1))
                    for c in range(HID_CH):
                        if b == 0 and c == 0:
                            pe.wait_ge(taps, 24 * (i + 2) if has_next else 24 * (i + 1))
                        if not (b == 0 and c < 2):
                            pe.wait_ge(gelu_ok, 4 * half + c - 1)
                        for k in range(CH):
                            mm(X[c % 2][:], w1x[:, k, c * P:(c + 1) * P], xg[:, k, :], start=k == 0, stop=False)
                        if c == 0:
                            pe.wait_ge(st_kept, half + 1)
                        mm(X[c % 2][:], w1s[:, c * P:(c + 1) * P], st_t[:], start=False, stop=True).then_inc(gate_mm, 1)
                    pe.wait_ge(gelu_ok, 4 * (half + 1))
                    if has_next and b == 0:
                        pe.wait_ge(rooted, 2 * (i + 2))
                    for j in range(TPB):
                        o = 128 + (b * TPB + j) * 16
                        for c in range(HID_CH):
                            w = mm(SM[:, o:o + 16], hid[:, c, j * P:(j + 1) * P], w2[:, c, :], start=c == 0, stop=c == 3)
                    w.then_inc(logit_mm, 1)

                def turn_mix(i):
                    need(pe, rt, RT * i)
                    for b in range(2):
                        pe.wait_ge(mix[b], 7 * (i + 1))
                        for m in range(CH):
                            if b:
                                pe.wait_ge(o_kept, 4 * i + m + 1)
                            for j in range(TPB):
                                w = nc.tensor.transpose(tails[m][:, j * P:(j + 1) * P], lo[:, b, j, m * P:(m + 1) * P], ident[:])
                            w.then_inc(o_turned, 1)

                def project_out(i, b):
                    pe.wait_ge(o_kept, 4 * (i + 1))
                    for jp in range(2):
                        if b:
                            pe.wait_ge(ln, LN * i + jp + 1)
                        for j in (2 * jp, 2 * jp + 1):
                            o = (j % 2) * D
                            for m in range(CH):
                                w = mm(tails[jp][:, o:o + D], o_t[:, b, m, j * P:(j + 1) * P], wo[:, m, :],
                                       start=m == 0, stop=m == 1)
                        w.then_inc(wo_mm, 1)

                def turn_x1(i, b):
                    pe.wait_ge(x1_ok, i + 1)
                    for m in range(CH):
                        if b:
                            pe.wait_ge(x1_kept, 4 * i + m + 1)
                        for j in range(TPB):
                            w = nc.tensor.transpose(tails[m][:, j * P:(j + 1) * P], x1[:, b, j, m * P:(m + 1) * P], ident[:])
                        w.then_inc(x1_turned, 1)

                def router(i):
                    pe.wait_ge(x1_kept, 4 * (i + 1))
                    for n_ in range(PT):
                        b, j = n_ // TPB, n_ % TPB
                        for m in range(CH):
                            w = mm(B3[:, n_ * NEXP:(n_ + 1) * NEXP], o_t[:, b, m, j * P:(j + 1) * P], rw[:, m, :],
                                   start=m == 0, stop=m == 1)
                    w.then_inc(rt_mm, 1)

                def rank(i):
                    pe.wait_ge(rt, RT * i + 7)
                    at, end = PT * NEXP, 2 * PT * NEXP
                    mm(B3[:, at:end], before[:], m_bf[:].rearrange("p t e -> p (t e)"), start=True, stop=False,
                       skip_group_check=True)
                    for j in range(PT - 1):
                        mm(B3[:, at + NEXP * (j + 1):end].rearrange("p (t e) -> p t e", e=NEXP), ones[:],
                           m_bf[:, j:j + 1, :].to_broadcast([P, PT - 1 - j, NEXP]), start=False, stop=False,
                           skip_group_check=True)
                    mm(B3[:, at:end].rearrange("p (t e) -> p t e", e=NEXP), ones[:],
                       m_acc[:].unsqueeze(1).to_broadcast([P, PT, NEXP]), start=False, stop=True,
                       skip_group_check=True).then_inc(ranked, 1)

                for g in range(4):
                    project(0, g)
                    if g:
                        select(0, g - 1)
                stage1b(0)
                merges(0)

                def step(i, has_prev, has_next):
                    recur(i, has_prev, has_next)
                    if has_next:
                        stage1b(i + 1, i - 1 if has_prev else None)
                    else:
                        router(i - 1)
                        rank(i - 1)
                    for b in range(2):
                        gate(i, b, has_next)
                    if has_next:
                        merges(i + 1)
                    turn_mix(i)
                step(0, False, True)
                with pe.Fori(1, PAIRS - 1) as i:
                    step(i, True, True)
                step(PAIRS - 1, True, False)
                end = PAIRS - 1
                for b in range(2):
                    project_out(end, b)
                for b in range(2):
                    turn_x1(end, b)
                router(end)
                rank(end)

            @block.scalar
            def _(act):
                A = nc.scalar.activation
                act.wait_ge(w_in, 16 * 17)
                A(itemp[:], itemp[:], ACT.Exp).then_inc(act_c, 1)
                act.wait_ge(act_c, 1)
                A(itemp[:], itemp[:], ACT.Ln, bias=1.0).then_inc(act_c, 1)
                A(floor16[:], floor16[:], ACT.Sigmoid).then_inc(act_c, 1)
                act.wait_ge(dve_c, 2)

                def group_a(p, g):
                    gg = g % 4
                    act.wait_ge(projected, 8 * p + g + 1)
                    need(act, raw, 8 * p + g - 1)
                    need(act, squared, 8 * p + g - 1)
                    A(conv[:, g % 2], X[g % 2][:], ACT.Copy, scale=cw[:, g // 4, gg % CH, 3:4]).then_inc(tap3, 1)

                def group_b(p, g):
                    gg = g % 4
                    b, m = gg // CH, gg % CH
                    dst = (kraw if g < 4 else q_t)[:, m, b * SEQ:(b + 1) * SEQ]
                    act.wait_ge(taps, 24 * p + 3 * (g + 1))
                    if g == 0:
                        need(act, k_turned, 4 * p)
                    if g == 4:
                        need(act, r_q, 4 * p)
                        need(act, at_mm, 8 * p)
                    A(dst, conv[:, g % 2], ACT.Silu).then_inc(raw, 1)
                    act.wait_ge(raw, 8 * p + g + 1)
                    need(act, selected, 8 * p + g - 1)
                    A(sq[:, g % 2], dst, ACT.Square).then_inc(squared, 1)

                def stage1b(p):
                    group_b(p, 3)
                    act.wait_ge(selected, 8 * p + 4)
                    need(act, rn_ok, 2 * p)
                    A(nrm[:, 0], SM[:, 0:32], ACT.Sqrt, bias=eps6[:, 0:1]).then_inc(rooted, 1)
                    group_a(p, 4)
                    act.wait_ge(beta_mm, p + 1)
                    need(act, beta_ok, 2 * p)
                    A(th[:], SM[:, 64:96], ACT.Tanh, scale=0.5).then_inc(beta_th, 1)
                    group_a(p, 5)
                    group_b(p, 4)
                    group_b(p, 5)
                    for j in range(4):
                        act.wait_ge(k_back, 4 * p + j + 1)
                        A(k_t[:, j % CH, (j // CH) * SEQ:(j // CH + 1) * SEQ], (B5, B3)[j % 2][:], ACT.Copy).then_inc(kt_kept, 1)
                    group_a(p, 6)
                    group_a(p, 7)
                    group_b(p, 6)
                    group_b(p, 7)
                    act.wait_ge(selected, 8 * p + 8)
                    A(nrm[:, 1], SM[:, 32:64], ACT.Sqrt, bias=eps6[:, 0:1]).then_inc(rooted, 1)

                def merge(i, k):
                    c = lambda x: x.rearrange("p (u k) -> p u k", k=BLK)
                    c2 = lambda x: x.rearrange("p (u k) -> p u k", k=2 * BLK)
                    cp = lambda out, in_: A(out, in_, ACT.Copy).then_inc(m_act, 1)
                    upper_bank = (2, 4, 6, 8, 12)[k]
                    act.wait_ge(m_pe, 14 * i + upper_bank)
                    if k == 0:
                        for q in range(2):
                            s = slice(q * 64, q * 64 + 32)
                            cp(z1[s, 16:32, :], c(B3[s, :]))
                    elif k == 1:
                        for q in range(2):
                            s = slice(q * 64, q * 64 + 32)
                            cp(mt[s, 16:32, q * 64 + 32:q * 64 + 64], c(B5[s, :]))
                    elif k == 2:
                        cp(xf[32:64, 16:32, 0:32], c(B3[32:64, :]))
                    elif k == 3:
                        cp(z2[0:64, 8:16, :], c2(B5[0:64, :]))
                        act.wait_ge(m_pe, 14 * i + 10)
                        cp(z2[0:64, 24:32, :], c2(B3[0:64, :]))
                    else:
                        cp(mt[0:64, 8:16, 64:128], c2(B5[0:64, :]))
                        act.wait_ge(m_pe, 14 * i + 14)
                        cp(mt[0:64, 24:32, 64:128], c2(B3[0:64, :]))

                def recur(i, has_prev, has_next):
                    for s in range(TPB):
                        if has_next:
                            group_a(i + 1, s)
                        if has_prev and s == 2:
                            root_norm(i - 1)
                        if has_prev and s == 3:
                            keep_x1(i - 1, 0)
                        act.wait_ge(r_u, 4 * i + s + 1)
                        A(u_sb[:].rearrange("p b h d -> p (b h d)"), B2[:], ACT.Copy).then_inc(r_ub, 1)
                        if has_next and s < 3:
                            group_b(i + 1, s)
                        if has_prev and s == 2:
                            apply_norm(i - 1)
                        if has_prev and s == 3:
                            keep_x1(i - 1, 1)

                def gate(i, b):
                    half = 2 * i + b
                    act.wait_ge(st_turned, half + 1)
                    need(act, gate_mm, 4 * half)
                    A(st_t[:], TR[0:STATS, :], ACT.Copy).then_inc(st_kept, 1)
                    need(act, logit_mm, half)
                    for c in range(HID_CH):
                        act.wait_ge(gate_mm, 4 * half + c + 1)
                        A(hid[:, c, :], X[c % 2][:], ACT.Gelu, bias=b1[:, c:c + 1]).then_inc(gelu_ok, 1)

                def rms(i, b):
                    half = 2 * i + b
                    act.wait_ge(mix[b], 7 * i + 4)
                    if b:
                        act.wait_ge(mix[0], 7 * i + 5)
                    A(squares, lo[:, b], ACT.Square).then_inc(sq_ok, 1)
                    act.wait_ge(mix[b], 7 * i + 5)
                    A(s32[:, 16 * b:16 * b + 16], s32[:, 16 * b:16 * b + 16], ACT.Sqrt, bias=eps5[:, 0:1],
                      scale=1.0 / DH).then_inc(rms_rt, 1)

                def merge_and_mix(i, has_next):
                    act.wait_ge(sm_dve, 11 * i + 4)
                    A(lg[:], lg[:], ACT.Exp).then_inc(sm_exp, 1)
                    if has_next:
                        for k in range(3):
                            merge(i + 1, k)
                    rms(i, 0)
                    if has_next:
                        merge(i + 1, 3)
                    rms(i, 1)
                    if has_next:
                        merge(i + 1, 4)
                    for k in range(4):
                        b, m = k // 2, k % 2
                        act.wait_ge(o_turned, 4 * i + k + 1)
                        if k == 0:
                            need(act, rt_mm, i)
                        A(o_t[:, b, m, :], tails[m][:], ACT.Copy).then_inc(o_kept, 1)

                def turn_blocks(p):
                    act.wait_ge(solve, SOLVE * (p + 1))
                    A(zt[:], z[:].rearrange("p i k -> p k i"), ACT.Copy).then_inc(zt_ok, 1)

                def root_norm(i):
                    act.wait_ge(ln, LN * i + 6)
                    A(rstd[:], mv[:, :, 1], ACT.Sqrt, bias=eps5[:, 0:1]).then_inc(ln_rt, 1)

                def apply_norm(i):
                    act.wait_ge(ln, LN * (i + 1))
                    for n_ in range(PT):
                        row = x1[:, n_ // TPB, n_ % TPB, 0:D]
                        w = A(row, row, ACT.Identity, bias=shift[:, n_:n_ + 1], scale=rstd[:, n_:n_ + 1])
                    w.then_inc(x1_ok, 1)

                def keep_x1(i, b):
                    act.wait_ge(wo_mm, 4 * (i + 1))
                    for m in range(CH):
                        act.wait_ge(x1_turned, 4 * i + 2 * b + m + 1)
                        A(o_t[:, b, m, :], tails[m][:], ACT.Copy).then_inc(x1_kept, 1)

                for g in range(4):
                    group_a(0, g)
                    if g < 3:
                        group_b(0, g)
                stage1b(0)
                turn_blocks(0)
                for k in range(5):
                    merge(0, k)

                def step(i, has_prev, has_next):
                    recur(i, has_prev, has_next)
                    if has_next:
                        stage1b(i + 1)
                    gate(i, 0)
                    if has_next:
                        turn_blocks(i + 1)
                    gate(i, 1)
                    merge_and_mix(i, has_next)
                step(0, False, True)
                with act.Fori(1, PAIRS - 1) as i:
                    step(i, True, True)
                step(PAIRS - 1, True, False)
                root_norm(PAIRS - 1)
                apply_norm(PAIRS - 1)
                for b in range(2):
                    keep_x1(PAIRS - 1, b)

            @block.vector
            def _(dve):
                V = nc.vector
                dve.wait_ge(w_in, 16 * 17)
                V.memset(eps6[:], 1e-6).then_inc(dve_c, 1)
                V.memset(eps5[:], 1e-5).then_inc(dve_c, 1)
                V.tensor_scalar(wo[:], wo[:], onw[:, 0:1], None, ALU.mult).then_inc(dve_c, 1)
                dve.wait_ge(pool_c, 8)
                V.tensor_copy(tok2[:], mi8[:, 1, :])
                V.tensor_copy(iota8[:], mi8[:, 0, :]).then_inc(dve_c, 1)
                dve.wait_ge(dve_c, 4)
                V.tensor_scalar(base8[:], iota8[:], float(CAP), None, ALU.mult).then_inc(dve_c, 1)
                dve.wait_ge(act_c, 3)
                V.tensor_scalar(floor16[:], floor16[:], 0.05, None, ALU.mult).then_inc(dve_c, 1)
                V.tensor_scalar(itemp[:], itemp[:], 1e-4, None, ALU.add).then_inc(dve_c, 1)
                dve.wait_ge(dve_c, 7)
                V.reciprocal(itemp[:], itemp[:]).then_inc(dve_c, 1)
                dve.wait_ge(pool_c, POOL_C + 2)

                def taps_of(p, g):
                    gg = g % 4
                    dve.wait_ge(tap3, 8 * p + g + 1)
                    for k in range(1, TAPS):
                        need(dve, taps, 24 * p + 3 * g + k - 1)
                        V.scalar_tensor_tensor(conv[:, g % 2, k:], X[g % 2][:, :SEQ - k],
                                               cw[:, g // 4, gg % CH, 3 - k:4 - k], conv[:, g % 2, k:],
                                               ALU.mult, ALU.add).then_inc(taps, 1)

                def norm(p, kq):
                    dve.wait_ge(rooted, 2 * p + kq + 1)
                    V.reciprocal(rn[:, kq], nrm[:, kq]).then_inc(rn_ok, 1)

                def keep_k(p, j):
                    b, m = j // CH, j % CH
                    dve.wait_ge(k_turned, 4 * p + j + 1)
                    rk_ = rn[:, 0].rearrange("p (t h) -> p t h", h=HEADS)[:, b * TPB:(b + 1) * TPB, 2 * m:2 * m + 2]
                    V.tensor_tensor(
                        k_tok[:, b * TPB:(b + 1) * TPB, m * P:(m + 1) * P].rearrange("p t (h d) -> p t h d", d=DH),
                        (TR, B2)[j % 2][:].rearrange("p (t h d) -> p t h d", h=2, d=DH),
                        rk_.unsqueeze(3).to_broadcast([P, TPB, 2, DH]), ALU.mult).then_inc(k_kept, 1)

                def last_stats(i):
                    dve.wait_ge(r_out, 4 * (i + 1))
                    for part in range(3):
                        w = bn(i, TPB - 1, part)
                    w.then_inc(st_dve, 1)

                def stage1b(p, last=None, first=False):
                    norm(p, 0)
                    dve.wait_ge(rn_ok, 2 * p + 1)
                    keep_k(p, 0)
                    keep_k(p, 1)
                    taps_of(p, 4)
                    dve.wait_ge(beta_th, p + 1)
                    V.tensor_scalar(beta[:].rearrange("p t h -> p (t h)"), th[:], 0.5, 0.5, ALU.mult, ALU.add).then_inc(beta_ok, 1)
                    V.tensor_scalar(nbeta[:].rearrange("p t h -> p (t h)"), th[:], -0.5, -0.5, ALU.mult, ALU.add).then_inc(beta_ok, 1)
                    if last is not None:
                        choose(last)
                    taps_of(p, 5)
                    keep_k(p, 2)
                    keep_k(p, 3)
                    if last is not None:
                        place(last)
                    if not first:
                        last_stats(p - 1)
                    taps_of(p, 6)
                    taps_of(p, 7)
                    dve.wait_ge(beta_ok, 2 * (p + 1))
                    for n_ in range(PT):
                        jj, par = n_ // 2, n_ % 2
                        ts = slice(2 * jj, 2 * jj + 2)
                        dve.wait_ge(a_mm, 8 * p + n_ + 1)
                        if n_ == 0:
                            need(dve, m_pe, 14 * p)
                        V.tensor_tensor(a_sb[:, ts, par::2, :],
                                        (B2, B3, B4, B5)[n_ % 4][:].rearrange("p (t m s) -> p t m s", t=2, m=2),
                                        nbeta[:, ts, par::2].unsqueeze(3).to_broadcast([P, 2, 2, P]),
                                        ALU.mult).then_inc(a_kept, 1)
                    for n_ in range(PT):
                        jj, par = n_ // 2, n_ % 2
                        dve.wait_ge(at_mm, 8 * p + n_ + 1)
                        V.tensor_tensor(at_t[:, 2 * jj:2 * jj + 2, par::2, :],
                                        (B2, B3, B4, B5)[n_ % 4][:].rearrange("p (t m s) -> p t m s", t=2, m=2),
                                        upper[:].unsqueeze(1).unsqueeze(1).to_broadcast([P, 2, 2, P]),
                                        ALU.mult).then_inc(at_kept, 1)
                    norm(p, 1)

                def solver(p):
                    dve.wait_ge(masked, 2 * (p + 1))
                    need(dve, x_out, 32 * p)
                    k = SOLVE * p
                    for j in range(1, BLK - 1):
                        left = BLK - 1 - j
                        need(dve, solve, k)
                        V.tensor_tensor(zt[:, 0:left, 0:j], z[:, j + 1:, j:j + 1].to_broadcast([P, left, j]),
                                        z[:, j:j + 1, 0:j].to_broadcast([P, left, j]), ALU.mult).then_inc(solve, 1)
                        dve.wait_ge(solve, k + 1)
                        V.tensor_tensor(z[:, j + 1:, 0:j], z[:, j + 1:, 0:j], zt[:, 0:left, 0:j], ALU.add).then_inc(solve, 1)
                        k += 2

                def merge(i, k):
                    c = lambda x: x.rearrange("p (u k) -> p u k", k=BLK)
                    c2 = lambda x: x.rearrange("p (u k) -> p u k", k=2 * BLK)
                    cp = lambda out, in_: V.tensor_copy(out, in_).then_inc(m_dve, 1)
                    lower_bank = (1, 3, 5, 7, 11)[k]
                    dve.wait_ge(m_pe, 14 * i + lower_bank)
                    if k == 0:
                        for q in range(2):
                            s = slice(q * 64, q * 64 + 32)
                            cp(z1[s, 0:16, :], c(B2[s, :]))
                    elif k == 1:
                        for q in range(2):
                            s = slice(q * 64, q * 64 + 32)
                            cp(mt[s, 0:16, q * 64 + 32:q * 64 + 64], c(B4[s, :]))
                    elif k == 2:
                        cp(xf[32:64, 0:16, 0:32], c(B2[32:64, :]))
                    elif k == 3:
                        cp(z2[0:64, 0:8, :], c2(B4[0:64, :]))
                        dve.wait_ge(m_pe, 14 * i + 9)
                        cp(z2[0:64, 16:24, :], c2(B2[0:64, :]))
                    else:
                        cp(mt[0:64, 0:8, 64:128], c2(B4[0:64, :]))
                        dve.wait_ge(m_pe, 14 * i + 13)
                        cp(mt[0:64, 16:24, 64:128], c2(B2[0:64, :]))

                def bn(i, s, part):
                    for b in range(2):
                        n_ = b * TPB + s
                        srcs = (sh[:, b, s], lo[:, b, s], v_tok[:, n_], delta[:, n_])
                        for k in ((0,), (1,), (3, 2))[part]:
                            for h in range(HEADS):
                                w = V.bn_stats(bnst[:, n_, (0, 1, 3, 2)[k], h, :], srcs[k][:, h * DH:(h + 1) * DH])
                    return w

                def recur(i, has_prev, has_next):
                    vv = v_tok[:].rearrange("p (b t) c -> p b t c", t=TPB)
                    bb = beta[:].rearrange("p (b t) h -> p b t h", t=TPB)
                    qn = rn[:, 1].rearrange("p (b t h) -> p b t h", t=TPB, h=HEADS)
                    dl = delta[:].rearrange("p (b t) c -> p b t c", t=TPB)
                    dve.wait_ge(v_in, 16 * (i + 1))
                    dve.wait_ge(rn_ok, 2 * (i + 1))
                    for s in range(TPB):
                        dve.wait_ge(r_p, 4 * i + s + 1)
                        V.tensor_tensor(r_sb[:].rearrange("p b h d -> p b (h d)"), vv[:, :, s, :],
                                        B2[:].rearrange("p (b c) -> p b c", b=2), ALU.subtract).then_inc(r_r1, 1)
                        dve.wait_ge(r_r1, 4 * i + s + 1)
                        V.tensor_tensor(r_sb[:], r_sb[:], bb[:, :, s, :].unsqueeze(3).to_broadcast([P, 2, HEADS, DH]),
                                        ALU.mult).then_inc(r_r, 1)
                        if has_next:
                            taps_of(i + 1, s)
                        if has_prev and s < 2:
                            add_out(i - 1, s)
                        if has_prev and s == 2:
                            scale_norm(i - 1)
                        if s:
                            if s == 1:
                                for b in range(2):
                                    dve.wait_ge(sl_in[b], 32 * (i + 1))
                            dve.wait_ge(r_out, 4 * i + s)
                            bn(i, s - 1, 0)
                        if s < TPB - 1:
                            dve.wait_ge(r_sx, 3 * i + s + 1)
                            dve.wait_ge(r_q, 4 * i + s + 1)
                            for q in range(2):
                                hs = slice(q * DH, (q + 1) * DH)
                                V.tensor_tensor(s_bd[hs, :, hs], s_bd[hs, :, hs],
                                                B5[hs, :].rearrange("p (c d) -> p c d", d=P)[:, :, hs],
                                                ALU.add).then_inc(r_s, 1)
                        if s:
                            bn(i, s - 1, 1)
                        dve.wait_ge(r_o, 4 * i + s + 1)
                        V.tensor_tensor(dl[:, :, s, :].rearrange("p b (h d) -> p b h d", d=DH),
                                        B4[:].rearrange("p (b h d) -> p b h d", h=HEADS, d=DH),
                                        qn[:, :, s, :].unsqueeze(3).to_broadcast([P, 2, HEADS, DH]),
                                        ALU.mult).then_inc(r_out, 1)
                        if has_prev and s == 1:
                            norm_stats(i - 1)
                        if s:
                            bn(i, s - 1, 2)

                def stats(i):
                    f = bnst[:].rearrange("p t k h s -> p t (k h) s")
                    g = gst[:].rearrange("p t (a s) -> p t a s", s=2)
                    c = 7 * i
                    dve.wait_ge(st_dve, c + 1)
                    need(dve, st_turned, 2 * i)
                    V.tensor_tensor(g[:, :, :, 0], f[:, :, :, 1], f[:, :, :, 4], ALU.add).then_inc(st_dve, 1)
                    V.tensor_tensor(dm[:], f[:, :, :, 1], f[:, :, :, 4], ALU.subtract).then_inc(st_dve, 1)
                    V.tensor_tensor(g[:, :, :, 1], f[:, :, :, 2], f[:, :, :, 5], ALU.add).then_inc(st_dve, 1)
                    dve.wait_ge(st_dve, c + 4)
                    V.scalar_tensor_tensor(dm[:], dm[:], 0.25, dm[:], ALU.mult, ALU.mult).then_inc(st_dve, 1)
                    V.tensor_scalar(g[:, :, :, 0], g[:, :, :, 0], 0.5, None, ALU.mult).then_inc(st_dve, 1)
                    dve.wait_ge(st_dve, c + 6)
                    V.scalar_tensor_tensor(g[:, :, :, 1], g[:, :, :, 1], 1.0 / DH, dm[:], ALU.mult,
                                           ALU.add).then_inc(st_dve, 1)

                def softmax(i):
                    c = 11 * i
                    t4 = lambda x: x[:].rearrange("p (t h) k -> p t h k", h=HEADS)
                    t16 = lambda x: x[:].rearrange("p (t h) k -> p t (h k)", h=HEADS)
                    g3 = [P, UNITS, PATHS]
                    dve.wait_ge(logit_mm, 2 * (i + 1))
                    need(dve, mixp, 6 * i)
                    V.tensor_tensor(t16(lg), SM[:, 128:256].rearrange("p (t k) -> p t k", t=PT),
                                    bias16[:].unsqueeze(1).to_broadcast([P, PT, 16]), ALU.add).then_inc(sm_dve, 1)
                    dve.wait_ge(sm_dve, c + 1)
                    V.tensor_tensor(t4(lg), t4(lg), itemp[:].unsqueeze(1).unsqueeze(3).to_broadcast([P, PT, HEADS, PATHS]),
                                    ALU.mult).then_inc(sm_dve, 1)
                    dve.wait_ge(sm_dve, c + 2)
                    V.tensor_reduce(s32[:], lg[:], AX.X, ALU.max).then_inc(sm_dve, 1)
                    dve.wait_ge(sm_dve, c + 3)
                    V.tensor_tensor(lg[:], lg[:], s32[:].unsqueeze(2).to_broadcast(g3), ALU.subtract).then_inc(sm_dve, 1)
                    dve.wait_ge(sm_exp, i + 1)
                    V.tensor_reduce(s32[:], lg[:], AX.X, ALU.add).then_inc(sm_dve, 1)
                    dve.wait_ge(sm_dve, c + 5)
                    V.reciprocal(r32[:], s32[:]).then_inc(sm_dve, 1)
                    dve.wait_ge(sm_dve, c + 6)
                    V.tensor_tensor(lg[:], lg[:], r32[:].unsqueeze(2).to_broadcast(g3), ALU.mult).then_inc(sm_dve, 1)
                    dve.wait_ge(sm_dve, c + 7)
                    V.tensor_tensor(t16(lg), t16(lg), floor16[:].unsqueeze(1).to_broadcast([P, PT, 16]),
                                    ALU.max).then_inc(sm_dve, 1)
                    dve.wait_ge(sm_dve, c + 8)
                    V.tensor_reduce(s32[:], lg[:], AX.X, ALU.add).then_inc(sm_dve, 1)
                    dve.wait_ge(sm_dve, c + 9)
                    V.reciprocal(r32[:], s32[:]).then_inc(sm_dve, 1)
                    dve.wait_ge(sm_dve, c + 10)
                    V.tensor_tensor(lg[:], lg[:], r32[:].unsqueeze(2).to_broadcast(g3), ALU.mult).then_inc(sm_dve, 1)

                v3 = lambda x: x.rearrange("p t (h d) -> p (t h) d", d=DH)

                def weigh(i, b):
                    p3 = lambda k: lg[:, 16 * b:16 * b + 16, k:k + 1].to_broadcast([P, 16, DH])
                    dlt = delta[:, b * TPB:(b + 1) * TPB]
                    dve.wait_ge(sm_dve, 11 * (i + 1))
                    V.tensor_tensor(v3(lo[:, b]), v3(lo[:, b]), p3(1), ALU.mult).then_inc(mix[b], 1)
                    V.tensor_tensor(v3(dlt), v3(dlt), p3(2), ALU.mult).then_inc(mix[b], 1)

                def add_two(i, b):
                    dve.wait_ge(mix[b], 7 * i + 2)
                    V.tensor_tensor(lo[:, b], lo[:, b], delta[:, b * TPB:(b + 1) * TPB], ALU.add).then_inc(mix[b], 1)

                def add_pool(i, b):
                    dve.wait_ge(mix[b], 7 * i + 3)
                    dve.wait_ge(mixp, 3 * (2 * i + b + 1))
                    V.tensor_tensor(lo[:, b], lo[:, b], sh[:, b], ALU.add).then_inc(mix[b], 1)

                def sum_squares(i, b):
                    dve.wait_ge(sq_ok, 2 * i + b + 1)
                    V.tensor_reduce(s32[:, 16 * b:16 * b + 16], v3(squares), AX.X, ALU.add).then_inc(mix[b], 1)

                def scale_mix(i, b):
                    r = r32[:, 16 * b:16 * b + 16]
                    dve.wait_ge(rms_rt, 2 * i + b + 1)
                    V.reciprocal(r, s32[:, 16 * b:16 * b + 16]).then_inc(mix[b], 1)
                    dve.wait_ge(mix[b], 7 * i + 6)
                    V.tensor_tensor(v3(lo[:, b]), v3(lo[:, b]), r.unsqueeze(2).to_broadcast([P, 16, DH]),
                                    ALU.mult).then_inc(mix[b], 1)

                def merge_and_mix(i, has_next):
                    softmax(i)
                    weigh(i, 0)
                    if has_next:
                        merge(i + 1, 0)
                    add_two(i, 0)
                    weigh(i, 1)
                    if has_next:
                        merge(i + 1, 1)
                        merge(i + 1, 2)
                    add_pool(i, 0)
                    add_two(i, 1)
                    sum_squares(i, 0)
                    if has_next:
                        merge(i + 1, 3)
                    scale_mix(i, 0)
                    add_pool(i, 1)
                    sum_squares(i, 1)
                    if has_next:
                        merge(i + 1, 4)
                    scale_mix(i, 1)

                def add_out(i, b):
                    dve.wait_ge(x_in[b], 16 * (i + 1))
                    for j in range(2):
                        dve.wait_ge(wo_mm, 4 * i + 2 * b + j + 1)
                        V.tensor_tensor(x1[:, b, 2 * j:2 * j + 2, 0:D], x1[:, b, 2 * j:2 * j + 2, 0:D],
                                        tails[j][:].rearrange("p (t c) -> p t c", c=D), ALU.add).then_inc(ln, 1)

                def norm_stats(i):
                    dve.wait_ge(ln, LN * i + 4)
                    for n_ in range(PT):
                        w = V.bn_stats(lbn[:, n_], x1[:, n_ // TPB, n_ % TPB, 0:D])
                    w.then_inc(ln, 1)
                    hold(dve, ln, LN * i + 5)
                    for n_ in range(PT):
                        w = V.bn_aggr(mv[:, n_], lbn[:, n_])
                    w.then_inc(ln, 1)

                def scale_norm(i):
                    dve.wait_ge(ln_rt, i + 1)
                    V.reciprocal(rstd[:], rstd[:]).then_inc(ln, 1)
                    dve.wait_ge(ln, LN * i + 7)
                    V.scalar_tensor_tensor(shift[:], mv[:, :, 0], -1.0, rstd[:], ALU.mult, ALU.mult).then_inc(ln, 1)

                def choose(i):
                    c = RT * i
                    at = bass.ds(i * (PT * TOPK), PT * TOPK)
                    dve.wait_ge(rt_mm, i + 1)
                    V.tensor_tensor(rl[:], B3[:, 0:PT * NEXP].rearrange("p (t e) -> p t e", e=NEXP),
                                    rb[:].unsqueeze(1).to_broadcast([P, PT, NEXP]), ALU.add).then_inc(rt, 1)
                    hold(dve, rt, c + 1)
                    dve.nop(nofuse=True)
                    for j in range(PT):
                        w = V.max(mx8[:, j], rl[:, j])
                    w.then_inc(rt, 1)
                    hold(dve, rt, c + 2)
                    dve.nop(nofuse=True)
                    for j in range(PT):
                        w = V.max_index(mi8[:, j], mx8[:, j], rl[:, j])
                    w.then_inc(rt, 1)
                    hold(dve, rt, c + 3)
                    dve.nop(nofuse=True)
                    V.tensor_copy(ef[:].rearrange("p (t k) -> p t k", k=TOPK), mi8[:, :, 0:TOPK]).then_inc(rt, 1)
                    V.tensor_copy(top2[:, at].rearrange("p (t k) -> p t k", k=TOPK), mx8[:, :, 0:TOPK]).then_inc(rt, 1)
                    dve.wait_ge(rt, c + 4)
                    V.tensor_tensor(oh[:], ef[:].unsqueeze(2).to_broadcast([P, PT * TOPK, NEXP]),
                                    iota8[:].unsqueeze(1).to_broadcast([P, PT * TOPK, NEXP]), ALU.is_equal).then_inc(rt, 1)
                    dve.wait_ge(rt, c + 6)
                    o4 = oh[:].rearrange("p (t k) e -> p t k e", k=TOPK)
                    V.tensor_tensor(m_bf[:], o4[:, :, 0, :], o4[:, :, 1, :], ALU.add).then_inc(rt, 1)
                    xr = x1[:].rearrange("p b t c -> p (b t) c")
                    V.tensor_copy(xr[:, :, TOK2], tok2[:])
                    V.tensor_copy(xr[:, :, SECOND], ef[:].rearrange("p (t k) -> p t k", k=TOPK)[:, :, 1]).then_inc(carried, 1)
                    dve.wait_ge(carried, 2 * i + 1)
                    V.tensor_scalar(tok2[:], tok2[:], float(2 * PTOK), None, ALU.add).then_inc(carried, 1)

                def place(i):
                    c = RT * i
                    o4 = oh[:].rearrange("p (t k) e -> p t k e", k=TOPK)
                    dve.wait_ge(ranked, i + 1)
                    V.tensor_tensor(rk[:], B3[:, PT * NEXP:2 * PT * NEXP].rearrange("p (t e) -> p t e", e=NEXP),
                                    base8[:].unsqueeze(1).to_broadcast([P, PT, NEXP]), ALU.add).then_inc(rt, 1)
                    dve.wait_ge(rt, c + 8)
                    V.tensor_tensor(o4, o4, rk[:].unsqueeze(2).to_broadcast([P, PT, TOPK, NEXP]), ALU.mult).then_inc(rt, 1)
                    dve.wait_ge(rt, c + 9)
                    V.tensor_reduce(slot_f[:], oh[:], AX.X, ALU.add).then_inc(rt, 1)
                    dve.wait_ge(rt, c + 10)
                    dve.nop(nofuse=True)
                    V.tensor_copy(slot_u[:], slot_f[:]).then_inc(rt, 1)
                    V.tensor_reduce(m_sum[:], m_bf[:].rearrange("p t e -> p e t"), AX.X, ALU.add).then_inc(rt, 1)
                    dve.wait_ge(rt, c + 12)
                    V.tensor_tensor(m_acc[:], m_acc[:], m_sum[:], ALU.add).then_inc(rt, 1)

                for g in range(4):
                    taps_of(0, g)
                stage1b(0, first=True)
                solver(0)
                for k in range(5):
                    merge(0, k)

                def step(i, has_prev, has_next):
                    recur(i, has_prev, has_next)
                    if has_next:
                        stage1b(i + 1, i - 1 if has_prev else None)
                    else:
                        choose(i - 1)
                        place(i - 1)
                        last_stats(i)
                    stats(i)
                    if has_next:
                        solver(i + 1)
                    merge_and_mix(i, has_next)
                step(0, False, True)
                with dve.Fori(1, PAIRS - 1) as i:
                    step(i, True, True)
                step(PAIRS - 1, True, False)
                end = PAIRS - 1
                for b in range(2):
                    add_out(end, b)
                norm_stats(end)
                scale_norm(end)
                choose(end)
                place(end)


EXTRA = NEXP
NMOE = TOKENS * TOPK // P + EXTRA
SPARE = NEXP * CAP
GU = 2 * D


def experts_and_combine(nc, t, keep):
    with ExitStack() as ctx:
        def sb(name, shape, dt=F32):
            return ctx.enter_context(nc.sbuf_tensor("C_" + name, shape, dt))

        def ps(name):
            return ctx.enter_context(nc.psum_tensor("C_ps_" + name, [P, 512], F32))

        def sem(name):
            return ctx.enter_context(nc.semaphore("C_" + name))

        top2, m_acc = keep["top2"], keep["m_acc"]
        def parts(name, shape):
            return [sb(f"{name}_{x}", shape, F32R) for x in ("high", "low")]
        wide, narrow = NEXP * CH * GU, NEXP * CH * D
        w_parts = parts("w", [P, wide + narrow])
        wgu = [w[:, 0:wide].rearrange("p (e c n) -> p e c n", e=NEXP, c=CH) for w in w_parts]
        wd = [w[:, wide:].rearrange("p (e c n) -> p e c n", e=NEXP, c=CH) for w in w_parts]
        PRODUCTS = ((0, 0), (0, 1), (1, 0))
        WP = 6
        ident = sb("ident", [P, P]); ones = sb("ones", [P, P], BF16); zero = sb("zero", [P, NEXP + EXTRA, ROW]); inowhere = sb("inowhere", [P, NEXP + EXTRA], I32)
        i8 = sb("i8", [P, NEXP], I32); it = sb("it", [P, NMOE], I32); i64 = sb("i64", [P, TILES], I32)
        ip = sb("ip", [P, 1], I32)
        f8 = sb("f8", [P, NEXP]); ft = sb("ft", [P, NMOE]); f64 = sb("f64", [P, TILES]); fp = sb("fp", [P, 1])
        cnt = sb("cnt", [P, NEXP]); gt = sb("gt", [P, NEXP, TILES]); tiles = sb("tiles", [P, NEXP])
        below = sb("below", [P, NEXP, NEXP]); tbase = sb("tbase", [P, NEXP]); tend = sb("tend", [P, NEXP])
        ge = sb("ge", [P, NMOE, NEXP]); ex = sb("ex", [P, NMOE]); tb = sb("tb", [P, NMOE])
        xrow = sb("xrow", [P, NMOE]); xrow_i = sb("xrow_i", [P, NMOE], I32); ex_i = sb("ex_i", [P, NMOE], I32); exc = sb("exc", [P, NMOE]); exb = sb("exb", [P, NMOE])
        pad = sb("pad", [P, NEXP]); pad_u = sb("pad_u", [P, NEXP], U32)
        ev = sb("ev", [P, TILES]); wts = sb("wts", [P, TILES, TOPK]); den = sb("den", [P, TILES])
        XB = 4
        xb = sb("xb", [P, XB, ROW]); dest = sb("dest", [P, 4], U32); xt = parts("xt", [P, 2, CH, P]); sg = sb("sg", [P, 2, D]); av = sb("av", [P, 2, D])
        avt = parts("avt", [P, 2, CH, P]); yb = sb("yb", [P, 2, D])
        G4 = 4
        GB = 4
        gy = keep["area"][:, 0:GB * G4 * TOPK * D].rearrange("p (g t c) -> p g t c", g=GB, t=G4)
        gx = keep["area"][:, GB * G4 * TOPK * D:GB * G4 * (TOPK + 1) * D].rearrange("p (g t c) -> p g t c", g=GB, t=G4)
        lbn = sb("lbn", [P, 2, G4, 6]); mv = sb("mv", [P, 2, G4, 2]); rstd = sb("rstd", [P, 2, G4]); shift = sb("shift", [P, 2, G4])
        eps = sb("eps", [P, 1])
        ps_x = [ps(f"x{i}") for i in range(2)]; ps_g = [ps(f"g{i}") for i in range(2)]
        ps_a = [ps(f"a{i}") for i in range(2)]; ps_y = [ps(f"y{i}") for i in range(2)]

        w_in, pool_c, idx, counted = keep["experts_in"], sem("pool_const"), sem("tables"), sem("counted")
        tiles_ok, pads_ok, dest_ok = sem("tiles_ok"), sem("pads_ok"), sem("dest_ok")
        zero_ok, normed, pool_i = sem("zero_ok"), sem("normed"), sem("ident")
        rest = [sem(f"last_rows{i}") for i in range(2)]
        exps, zeroed, spare_ok = sem("gate_exp"), sem("pads_zeroed"), sem("spare_zeroed")
        x_in = [sem(f"x_in{i}") for i in range(XB)]; w_high, w_low, x_low, a_low = sem("w_high"), sem("w_low"), sem("x_low"), sem("a_low")
        y_out = [sem(f"y_out{i}") for i in range(2)]
        x_turned, x_kept, gu_mm, silu_ok, act_ok = (sem(n) for n in ("x_turned", "x_kept", "gu_mm", "silu_ok", "act_ok"))
        a_turned, a_kept, y_mm, y_kept = (sem(n) for n in ("a_turned", "a_kept", "y_mm", "y_kept"))
        gy_in = [sem(f"gy_in{i}") for i in range(GB)]; gx_in = [sem(f"gx_in{i}") for i in range(GB)]
        fin, rooted, scaled = sem("final_dve"), sem("final_rooted"), sem("final_scaled")
        out_ok = [sem(f"out{i}") for i in range(GB)]
        groups = TILES // G4
        FIN = 4 * G4
        xs = t["xs_d"]
        ytok = t["y_d"][0:TOPK * TOKENS].rearrange("(t p k) c -> p t (k c)", p=P, k=TOPK)
        tok = lambda n: t[n].rearrange("(t p) c -> p t c", p=P)

        with nc.Block() as block:
            @block.sync
            def _(sp):
                sp.wait_ge(zero_ok, 4)
                for k in range(EXTRA):
                    sp.dma_start(xs[SPARE + k * P:SPARE + (k + 1) * P, :], zero[:, NEXP + k]).then_inc(spare_ok, 16)
                for k in rest:
                    sp.wait_ge(k, 16 * PT * TOPK // 2)
                sp.wait_ge(tiles_ok, 2)
                sp.wait_ge(zeroed, 16 * NEXP)
                sp.wait_ge(spare_ok, 16 * EXTRA)

                def load(j, q):
                    hold(sp, x_turned, j - XB + 1)
                    hold(sp, dest_ok, j - XB + 1)
                    row = sp.value_load(xrow_i[0:1, bass.ds(j, 1)], min_val=0, max_val=SPARE + (EXTRA - 1) * P)
                    sp.dma_start(xb[:, q], xs[bass.ds(row, P), :]).then_inc(x_in[q], 16)
                for q in range(XB):
                    load(q, q)
                with sp.Fori(1, NMOE // XB) as i:
                    for q in range(XB):
                        load(XB * i + q, q)

                def load_x1(g, u):
                    if not isinstance(g, int) or g >= GB:
                        hold(sp, out_ok[u], 4 * (g - u))
                    sp.dma_start(gx[:, u], tok("x1_d")[:, bass.ds(g * G4, G4), :]).then_inc(gx_in[u], 16)

                def store(g, u):
                    hold(sp, normed, g + 1)
                    sp.dma_start(tok("out")[:, bass.ds(g * G4, G4), :], gx[:, u]).then_inc(out_ok[u], 16)

                def slot(g, u):
                    load_x1(g + 2, (u + 2) % GB)
                    store(g, u)
                for u in range(2):
                    load_x1(u, u)
                for u in range(2):
                    sp.wait_ge(y_out[u], 16 * NMOE // 2)
                for u in range(GB):
                    sp.dma_start(gy[:, u], ytok[:, u * G4:(u + 1) * G4, :]).then_inc(gy_in[u], 16)
                for g in range(2):
                    slot(g, g)
                with sp.Fori(0, groups // GB - 1) as i:
                    for k in range(GB):
                        slot(GB * i + k + 2, (k + 2) % GB)
                for g in range(groups - 2, groups):
                    store(g, g % GB)
                for u in range(GB):
                    sp.wait_ge(out_ok[u], 16 * groups // GB)

            @block.gpsimd
            def _(pool):
                pool.iota(i8[:], [[1, NEXP]], base=0, channel_multiplier=0).then_inc(pool_c, 1)
                pool.iota(it[:], [[1, NMOE]], base=0, channel_multiplier=0).then_inc(pool_c, 1)
                pool.iota(i64[:], [[P, TILES]], base=0, channel_multiplier=0).then_inc(pool_c, 1)
                pool.iota(ip[:], [[0, 1]], base=0, channel_multiplier=1).then_inc(pool_c, 1)
                pool.iota(inowhere[:], [[P, NEXP + EXTRA]], base=TOPK * TOKENS, channel_multiplier=1).then_inc(pool_c, 1)
                dispatch(pool, t, keep["x1"], keep["slot_u"], rest)
                pool.memset(ident[:], 0.0).then_inc(pool_i, 1)
                pool.wait_ge(pool_i, 1)
                pool.affine_select(out=ident[:], in_=ident[:], compare_op=ALU.not_equal, fill=1.0, base=0,
                                   pattern=[[-1, P]], channel_multiplier=1).then_inc(pool_i, 1)
                pool.wait_ge(zero_ok, 4)
                pool.wait_ge(pads_ok, 1)
                for e in range(NEXP):
                    pool.indirect_dma_start(xs[:, :], bass.IndirectOffsetOnAxis(ap=pad_u[:, e:e + 1], axis=0),
                                            zero[:, e], None).then_inc(zeroed, 16)

                def scatter(j, u, q):
                    hold(pool, dest_ok, j + 1)
                    hold(pool, y_kept, j + 1)
                    pool.indirect_dma_start(t["y_d"][:, :], bass.IndirectOffsetOnAxis(ap=dest[:, q:q + 1], axis=0),
                                            yb[:, u], None).then_inc(y_out[u], 16)
                with pool.Fori(0, NMOE // 4) as i:
                    for q in range(4):
                        scatter(4 * i + q, q % 2, q)
                for u in range(2):
                    pool.wait_ge(y_out[u], 16 * NMOE // 2)

            @block.tensor
            def _(pe):
                mm = nc.tensor.matmul
                pe.wait_ge(zero_ok, 1)
                mm(ps_y[0][:, 0:NEXP], ones[:], m_acc[:], start=True, stop=True).then_inc(counted, 1)
                pe.wait_ge(w_low, WP)
                pe.wait_ge(pool_i, 2)
                pe.wait_ge(tiles_ok, 2)

                def turn_x(j, q):
                    u = q % 2
                    pe.wait_ge(x_in[q], 4 * (j - q) + 16)
                    need(pe, x_low, j - 1)
                    for c in range(CH):
                        w = nc.tensor.transpose(ps_x[u][:, c * P:(c + 1) * P], xb[:, q, c * P:(c + 1) * P], ident[:])
                    w.then_inc(x_turned, 1)

                def experts(j):
                    both = pe.value_load(ex_i[0:1, bass.ds(j, 1)], min_val=0, max_val=NEXP * NEXP - 1)
                    return both % NEXP, both // NEXP

                def products(out, left, right, u, e, done):
                    n_ = 0
                    for c in range(CH):
                        for lp, rp in PRODUCTS:
                            w = mm(out, left[lp][:, u, c, :], right[rp][:, bass.ds(e, 1), c, :], start=n_ == 0,
                                   stop=n_ == CH * len(PRODUCTS) - 1)
                            n_ += 1
                    w.then_inc(done, 1)

                def gate_up(j, u, e):
                    pe.wait_ge(x_low, j + 1)
                    need(pe, act_ok, j - 1)
                    products(ps_g[u][:], xt, wgu, u, e, gu_mm)

                def turn_act(j, u):
                    pe.wait_ge(act_ok, j + 1)
                    need(pe, a_low, j - 1)
                    for c in range(CH):
                        w = nc.tensor.transpose(ps_a[u][:, c * P:(c + 1) * P], av[:, u, c * P:(c + 1) * P], ident[:])
                    w.then_inc(a_turned, 1)

                def down(j, u, e):
                    pe.wait_ge(a_low, j + 1)
                    need(pe, y_kept, j - 1)
                    products(ps_y[u][:, 0:D], avt, wd, u, e, y_mm)
                turn_x(0, 0)
                turn_x(1, 1)
                gate_up(0, 0, experts(0)[0])

                def step(j, q):
                    u = q % 2
                    e, e_down = experts(j)
                    if not isinstance(j, int) or j > 2:
                        down(j - 3, 1 - u, e_down)
                    if not isinstance(j, int) or j + 1 < NMOE:
                        turn_x(j + 1, (q + 1) % XB)
                    if not isinstance(j, int) or j > 1:
                        turn_act(j - 2, u)
                    gate_up(j, u, e)
                for j in range(1, 3 + XB):
                    step(j, j % XB)
                with pe.Fori(1, NMOE // XB - 1) as i:
                    for k in range(XB):
                        step(XB * i + 3 + k, (3 + k) % XB)
                step(NMOE - 1, 3)
                for j in range(NMOE - 3, NMOE):
                    if j > NMOE - 3:
                        turn_act(j, j % 2)
                    down(j, j % 2, experts(j)[0])

            @block.scalar
            def _(act):
                A = nc.scalar.activation
                act.wait_ge(w_in, 16 * 3 * NEXP)
                for k in range(WP):
                    piece = slice(k * (wide + narrow) // WP, (k + 1) * (wide + narrow) // WP)
                    A(w_parts[0][:, piece], keep["area"][:, piece], ACT.Copy).then_inc(w_high, 1)
                act.wait_ge(pads_ok, 2)
                A(ev[:], ev[:], ACT.Exp).then_inc(exps, 1)

                def keep_x(j, u):
                    act.wait_ge(x_turned, j + 1)
                    need(act, gu_mm, j - 1)
                    A(xt[0][:, u].rearrange("p c n -> p (c n)"), ps_x[u][:, 0:D], ACT.Copy).then_inc(x_kept, 1)

                def keep_a(j, u):
                    act.wait_ge(a_turned, j + 1)
                    need(act, y_mm, j - 1)
                    A(avt[0][:, u].rearrange("p c n -> p (c n)"), ps_a[u][:, 0:D], ACT.Copy).then_inc(a_kept, 1)

                def silu(j, u):
                    act.wait_ge(gu_mm, j + 1)
                    need(act, act_ok, j - 1)
                    A(sg[:, u], ps_g[u][:, 0:D], ACT.Silu).then_inc(silu_ok, 1)

                def keep_y(j, u):
                    act.wait_ge(y_mm, j + 1)
                    if not isinstance(j, int) or j > 1:
                        act.wait_ge(y_out[u], 8 * (j - u))
                    A(yb[:, u], ps_y[u][:, 0:D], ACT.Copy).then_inc(y_kept, 1)

                def step(j, u):
                    if not isinstance(j, int) or j + 1 < NMOE:
                        keep_x(j + 1, 1 - u)
                    if not isinstance(j, int) or j > 1:
                        keep_a(j - 2, u)
                    silu(j, u)
                    if not isinstance(j, int) or j > 1:
                        keep_y(j - 2, u)
                keep_x(0, 0)
                keep_x(1, 1)
                silu(0, 0)
                for j in range(1, 4):
                    step(j, j % 2)
                with act.Fori(2, NMOE // 2 - 1) as i:
                    step(2 * i, 0)
                    step(2 * i + 1, 1)
                for j in (NMOE - 2, NMOE - 1):
                    step(j, j % 2)
                for j in (NMOE - 2, NMOE - 1):
                    keep_a(j, j % 2)
                    keep_y(j, j % 2)

                def root(g, u):
                    act.wait_ge(fin, FIN * (g + 1))
                    A(rstd[:, u % 2], mv[:, u % 2, :, 1], ACT.Sqrt, bias=eps[:, 0:1]).then_inc(rooted, 1)

                def norm(g, u):
                    act.wait_ge(scaled, 2 * (g + 1))
                    for j in range(G4):
                        w = A(gx[:, u, j], gx[:, u, j], ACT.Identity, bias=shift[:, u % 2, j:j + 1],
                              scale=rstd[:, u % 2, j:j + 1])
                    w.then_inc(normed, 1)

                def load_y(g, u):
                    act.dma_start(gy[:, u], ytok[:, bass.ds(g * G4, G4), :]).then_inc(gy_in[u], 16)

                def finish(g, u, more=True):
                    root(g, u)
                    if more:
                        load_y(g + GB, u)
                    norm(g - 1, (u - 1) % GB)
                root(0, 0)
                load_y(GB, 0)
                for g in range(1, GB):
                    finish(g, g)
                with act.Fori(1, groups // GB - 1) as i:
                    for u in range(GB):
                        finish(GB * i + u, u)
                for g in range(groups - GB, groups):
                    finish(g, g % GB, False)
                norm(groups - 1, GB - 1)

            @block.vector
            def _(dve):
                V = nc.vector
                count = [0]

                def then(ins):
                    ins.then_inc(idx, 1)
                    count[0] += 1
                    dve.wait_ge(idx, count[0])
                V.memset(ones[:], 1.0).then_inc(zero_ok, 1)
                V.memset(zero[:], 0.0).then_inc(zero_ok, 1)
                dve.wait_ge(pool_c, 5)
                bc = lambda x, d, shape: x.unsqueeze(d).to_broadcast(shape)
                V.memset(eps[:], 1e-5).then_inc(idx, 1)
                V.tensor_copy(f8[:], i8[:]).then_inc(idx, 1)
                V.tensor_copy(ft[:], it[:]).then_inc(idx, 1)
                V.tensor_copy(f64[:], i64[:]).then_inc(idx, 1)
                V.tensor_copy(fp[:], ip[:]).then_inc(idx, 1)
                count[0] = 5
                dve.wait_ge(zero_ok, 2)
                V.tensor_copy(zero[:, :, TOK2], inowhere[:]).then_inc(zero_ok, 1)
                V.memset(zero[:, :, SECOND:SECOND + 1], -1.0).then_inc(zero_ok, 1)
                dve.wait_ge(counted, 1)
                then(V.tensor_copy(cnt[:], ps_y[0][:, 0:NEXP]))
                then(V.scalar_tensor_tensor(pad[:], f8[:], float(CAP), cnt[:], ALU.mult, ALU.add))
                V.tensor_scalar(pad_u[:], pad[:], fp[:, 0:1], None, ALU.add).then_inc(pads_ok, 1)
                s = [P, NEXP, TILES]
                then(V.tensor_tensor(gt[:], bc(cnt[:], 2, s), bc(f64[:], 1, s), ALU.is_gt))
                then(V.tensor_reduce(tiles[:], gt[:], AX.X, ALU.add))
                s = [P, NEXP, NEXP]
                then(V.tensor_tensor(below[:], bc(f8[:], 2, s), bc(f8[:], 1, s), ALU.is_gt))
                then(V.tensor_tensor(below[:], below[:], bc(tiles[:], 1, s), ALU.mult))
                then(V.tensor_reduce(tbase[:], below[:], AX.X, ALU.add))
                then(V.tensor_tensor(tend[:], tbase[:], tiles[:], ALU.add))
                s = [P, NMOE, NEXP]
                then(V.tensor_tensor(ge[:], bc(ft[:], 2, s), bc(tend[:], 1, s), ALU.is_ge))
                then(V.tensor_reduce(ex[:], ge[:], AX.X, ALU.add))
                then(V.tensor_scalar(exc[:], ex[:], float(NEXP - 1), None, ALU.min))
                then(V.tensor_copy(exb[:, 0:3], exc[:, 0:3]))
                then(V.scalar_tensor_tensor(exb[:, 3:NMOE], exc[:, 0:NMOE - 3], float(NEXP), exc[:, 3:NMOE], ALU.mult, ALU.add))
                V.tensor_copy(ex_i[:], exb[:]).then_inc(tiles_ok, 1)
                then(V.tensor_tensor(ge[:], ge[:], bc(tiles[:], 1, s), ALU.mult))
                then(V.tensor_reduce(tb[:], ge[:], AX.X, ALU.add))
                then(V.tensor_tensor(tb[:], ft[:], tb[:], ALU.subtract))
                then(V.tensor_scalar(xrow[:], ex[:], float(CAP), None, ALU.mult))
                V.scalar_tensor_tensor(xrow_i[:], tb[:], float(P), xrow[:], ALU.mult, ALU.add).then_inc(tiles_ok, 1)
                t2 = top2[:].rearrange("p (t k) -> p t k", k=TOPK)
                V.tensor_tensor(ev[:], t2[:, :, 1], t2[:, :, 0], ALU.subtract).then_inc(pads_ok, 1)
                dve.wait_ge(exps, 1)
                then(V.tensor_scalar(den[:], ev[:], 1.0, None, ALU.add))
                then(V.reciprocal(den[:], den[:]))
                then(V.tensor_copy(wts[:, :, 0], den[:]))
                then(V.tensor_tensor(wts[:, :, 1], ev[:], den[:], ALU.mult))

                def gated(j, u):
                    dve.wait_ge(silu_ok, j + 1)
                    need(dve, a_turned, j - 1)
                    V.tensor_tensor(av[:, u], sg[:, u], ps_g[u][:, D:GU], ALU.mult).then_inc(act_ok, 1)

                def low_x(j, u):
                    dve.wait_ge(x_kept, j + 1)
                    need(dve, gu_mm, j - 1)
                    flat = lambda x: x[:, u].rearrange("p c n -> p (c n)")
                    V.tensor_tensor(flat(xt[1]), ps_x[u][:, 0:D], flat(xt[0]), ALU.subtract).then_inc(x_low, 1)

                def low_a(j, u):
                    dve.wait_ge(a_kept, j + 1)
                    need(dve, y_mm, j - 1)
                    flat = lambda x: x[:, u].rearrange("p c n -> p (c n)")
                    V.tensor_tensor(flat(avt[1]), ps_a[u][:, 0:D], flat(avt[0]), ALU.subtract).then_inc(a_low, 1)
                def place(j, q):
                    u = q % 2
                    dve.wait_ge(x_in[q], 4 * (j - q) + 16)
                    if not isinstance(j, int) or j > 3:
                        dve.wait_ge(y_out[u], 8 * (j - u) - 16)
                    V.scalar_tensor_tensor(dest[:, q:q + 1], xb[:, q, SECOND:SECOND + 1], ex[:, bass.ds(j, 1)],
                                           xb[:, q, TOK2:TOK2 + 1], ALU.is_equal, ALU.add).then_inc(dest_ok, 1)
                for k in range(WP):
                    piece = slice(k * (wide + narrow) // WP, (k + 1) * (wide + narrow) // WP)
                    dve.wait_ge(w_high, k + 1)
                    V.tensor_tensor(w_parts[1][:, piece], keep["area"][:, piece], w_parts[0][:, piece],
                                    ALU.subtract).then_inc(w_low, 1)
                low_x(0, 0)
                low_x(1, 1)
                gated(0, 0)

                def step(j, k):
                    if not isinstance(j, int) or j + 1 < NMOE:
                        low_x(j + 1, (k + 1) % 2)
                    if not isinstance(j, int) or j > 1:
                        low_a(j - 2, k % 2)
                    gated(j, k % 2)
                    place(j - 1, (k + 3) % 4)
                for j in range(1, 7):
                    step(j, j % 4)
                with dve.Fori(1, NMOE // 4 - 1) as i:
                    for k in range(4):
                        step(4 * i + 3 + k, (3 + k) % 4)
                step(NMOE - 1, 3)
                place(NMOE - 1, 3)
                for j in (NMOE - 2, NMOE - 1):
                    low_a(j, j % 2)

                def combine(g, u):
                    c = FIN * g
                    wt = wts[:].rearrange("p t k -> p (t k)")
                    dve.wait_ge(gx_in[u], 4 * (g - u) + 16)
                    dve.wait_ge(gy_in[u], 4 * (g - u) + 16)
                    for k in range(TOPK):
                        if k:
                            dve.wait_ge(fin, c + G4)
                        for j in range(G4):
                            V.scalar_tensor_tensor(gx[:, u, j], gy[:, u, j, k * D:(k + 1) * D],
                                                   wt[:, bass.ds(g * (G4 * TOPK) + j * TOPK + k, 1)], gx[:, u, j],
                                                   ALU.mult, ALU.add).then_inc(fin, 1)
                    for j in range(G4):
                        dve.wait_ge(fin, c + G4 + j + 1)
                        V.bn_stats(lbn[:, u % 2, j], gx[:, u, j]).then_inc(fin, 1)
                    if not isinstance(g, int) or g > 1:
                        dve.wait_ge(normed, g - 1)
                    for j in range(G4):
                        hold(dve, fin, c + 2 * G4 + j + 1)
                        V.bn_aggr(mv[:, u % 2, j], lbn[:, u % 2, j]).then_inc(fin, 1)

                def combined(g, u):
                    dve.wait_ge(rooted, g + 1)
                    V.reciprocal(rstd[:, u % 2], rstd[:, u % 2]).then_inc(scaled, 1)
                    dve.wait_ge(scaled, 2 * g + 1)
                    V.scalar_tensor_tensor(shift[:, u % 2], mv[:, u % 2, :, 0], -1.0, rstd[:, u % 2], ALU.mult, ALU.mult).then_inc(scaled, 1)

                def both(g, u):
                    combine(g, u)
                    combined(g - 1, (u - 1) % GB)
                combine(0, 0)
                for g in range(1, GB):
                    both(g, g)
                with dve.Fori(1, groups // GB) as i:
                    for u in range(GB):
                        both(GB * i + u, u)
                combined(groups - 1, GB - 1)


def post_norm_layer(nc, t):
    t = dict(t)
    for name, shape in (
        ("v_d", (TOKENS, D)), ("short_d", (TOKENS, D)), ("long_d", (TOKENS, D)), ("x1_d", (TOKENS, D)),
        ("scr_a", (NBLK, BLK, UNITS, BLK)), ("scr_x", (P, BLK, BLK)), ("scr_xt", (P, BLK, BLK)),
        ("xs_d", (SPARE + EXTRA * P, ROW)), ("y_d", (TOPK * TOKENS + (NEXP + EXTRA) * P, D)),
    ):
        t[name] = nc.dram_tensor(name, shape, F32, kind="Internal").ap()
    conv_and_fir(nc, t)
    with ExitStack() as ctx:
        def sb(name, shape, dt=F32):
            return ctx.enter_context(nc.sbuf_tensor(name, shape, dt))
        area = sb("area", [P, 3 * UNITS * P])
        wgu = area[:, 0:NEXP * CH * GU].rearrange("p (e c n) -> p e c n", e=NEXP, c=CH)
        wd = area[:, NEXP * CH * GU:NEXP * CH * (GU + D)].rearrange("p (e c n) -> p e c n", e=NEXP, c=CH)
        keep = {
            "area": area, "wgu": wgu, "wg": wgu[:, :, :, 0:D], "wu": wgu[:, :, :, D:GU], "wd": wd,
            "experts_in": ctx.enter_context(nc.semaphore("experts_in")),
            "x1": sb("x1", [P, 2, TPB, ROW]), "slot_u": sb("slot_u", [P, PT * TOPK], U32),
            "top2": sb("top2", [P, TILES * TOPK]), "m_acc": sb("m_acc", [P, NEXP], BF16),
        }
        delta_and_gate(nc, t, keep)
        experts_and_combine(nc, t, keep)


def kernel(**inputs):
    import numpy as np
    import concourse.bacc as bacc
    from concourse.bass_utils import run_bass_kernel_spmd

    def arr(name):
        return np.asarray(inputs[name])

    def turned(name):
        return np.ascontiguousarray(arr(name).T)
    x = np.ascontiguousarray(arr("L0_attn_hidden_states").reshape(TOKENS, D))
    fir_long = np.zeros((D, FPAD), x.dtype)
    fir_long[:, P - 1:P - 1 + FIR] = arr("L0_attn_fir_long_w").reshape(D, FIR)[:, ::-1]
    arrays = {
        "x": x, "xT": np.ascontiguousarray(x.T),
        "WqT": turned("L0_attn_Wq"), "WkT": turned("L0_attn_Wk"), "WvT": turned("L0_attn_Wv"),
        "WbT": turned("L0_attn_Wb"), "WoT": turned("L0_attn_Wo"),
        "qconv": arr("L0_attn_qconv_w"), "kconv": arr("L0_attn_kconv_w"), "vconv": arr("L0_attn_vconv_w"),
        "fir_short": np.ascontiguousarray(arr("L0_attn_fir_short_w").reshape(D, SHORT)), "fir_long": fir_long,
        "w1T": turned("L0_attn_gate_w1"), "w2T": turned("L0_attn_gate_w2"),
        "b1": np.ascontiguousarray(arr("L0_attn_gate_b1").reshape(HID_CH, P).T),
        "bias": np.ascontiguousarray(arr("L0_attn_base_bias").reshape(-1)),
        "floor": np.ascontiguousarray(arr("L0_attn_floor_raw").reshape(-1)),
        "log_temp": arr("L0_attn_log_temp"), "onorm": arr("L0_attn_onorm_w"),
        "rw": arr("L0_ffn_router_w"), "rb": arr("L0_ffn_router_b"),
        "we_gate": arr("L0_ffn_we_gate"), "we_up": arr("L0_ffn_we_up"), "we_down": arr("L0_ffn_we_down"),
    }
    nc = bacc.Bacc("TRN2", target_bir_lowering=False, num_devices=1)
    t = {name: nc.dram_tensor(name, a.shape, mybir.dt.from_np(a.dtype), kind="ExternalInput").ap()
         for name, a in arrays.items()}
    t["out"] = nc.dram_tensor("out", (TOKENS, D), F32, kind="ExternalOutput").ap()
    post_norm_layer(nc, t)
    r = run_bass_kernel_spmd(nc, [arrays], core_ids=[0])
    return r.results[0]["out"].reshape(BATCH, SEQ, D)
```
